# Optimizing a Trainium2 kernel written in Bass

```python
import numpy as np
import jax
import jax.numpy as jnp

def _softmax(x, axis=-1):
    return jax.nn.softmax(x, axis=axis)

def _gelu(x):
    return jax.nn.gelu(x, approximate=True)

def _silu(x):
    return jax.nn.silu(x)

def _sigmoid(x):
    return jax.nn.sigmoid(x)

def _layernorm(x, axis=-1, eps=1e-05):
    m = jnp.mean(x, axis=axis, keepdims=True)
    v = jnp.var(x, axis=axis, keepdims=True)
    return (x - m) / jnp.sqrt(v + eps)

def _scatter_add(tgt, idx, src, axis=0):
    return tgt.at[idx].add(src)

def _segment_sum(src, seg, n):
    return jax.ops.segment_sum(src, seg, n)
kernel_name = 'mk_gnn_ffn_d1_gnn_r8_d09e81'

def setup_inputs(seed: int=0):
    np.random.seed(seed)
    _w = jnp.asarray

    def _rec_inputs():
        import jax
        import jax.numpy as jnp
        _gk = jax.random.key(seed)
        x = -0.0005963 + 1.001 * jax.random.normal(jax.random.fold_in(_gk, 1), (384, 1024), jnp.float32)
        src = jax.random.randint(jax.random.fold_in(_gk, 2), (6144,), 0, 384, jnp.int32)
        dst = jnp.minimum((384 * jax.random.uniform(jax.random.fold_in(_gk, 3), (6144,)) ** 2.0).astype(jnp.int32), 3071)
        _o = jnp.argsort(dst, stable=True)
        src = src[_o]
        dst = dst[_o]
        edge_type_5 = jax.random.randint(jax.random.fold_in(_gk, 12), (6144,), 0, 5, jnp.int32)
        return (x, src, dst, edge_type_5)
    x, src, dst, edge_type_5 = _rec_inputs()

    def _L0_gnn_setup():
        import jax, jax.numpy as jnp
        import numpy as np
        N = 384
        E = 12288
        IN_F = 1024
        OUT_F = 1024
        H = 16
        D = OUT_F // H
        NUM_ETYPES = 4

        def _build_mask(edge_index, edge_type, edge_type_weights, dtype):
            src, dst = (edge_index[0], edge_index[1])
            w = jax.nn.softplus(edge_type_weights)
            mask = jnp.full((N, N), -jnp.inf, dtype=dtype)
            mask = mask.at[src, dst].set(w[edge_type - 1])
            diag = jnp.diagonal(mask)
            idx = jnp.arange(N)
            mask = mask.at[idx, idx].set(jnp.where(jnp.isneginf(diag), w[3], diag))
            return mask
        key = jax.random.key(seed)
        ks = jax.random.split(key, 20)
        p = lambda k, shape: jax.random.normal(k, shape, dtype=jnp.float32) * 0.02
        return {'x': jax.random.normal(ks[0], (N, IN_F), dtype=jnp.float32), 'edge_index': jax.random.randint(ks[1], (2, E), 0, N), 'edge_type': jax.random.randint(ks[2], (E,), 1, NUM_ETYPES + 1), 'edge_type_weights': jnp.ones((NUM_ETYPES,), jnp.float32) + 0.1 * jax.random.normal(ks[3], (NUM_ETYPES,), dtype=jnp.float32), 'wq': p(ks[4], (OUT_F, IN_F)), 'bq': p(ks[5], (OUT_F,)), 'wk': p(ks[6], (OUT_F, IN_F)), 'bk': p(ks[7], (OUT_F,)), 'wv': p(ks[8], (OUT_F, IN_F)), 'bv': p(ks[9], (OUT_F,)), 'wiq': p(ks[10], (OUT_F, OUT_F)), 'biq': p(ks[11], (OUT_F,)), 'wik': p(ks[12], (OUT_F, OUT_F)), 'bik': p(ks[13], (OUT_F,)), 'wiv': p(ks[14], (OUT_F, OUT_F)), 'biv': p(ks[15], (OUT_F,)), 'wo': p(ks[16], (OUT_F, OUT_F)), 'bo': p(ks[17], (OUT_F,))}
    _L0_gnn_all = _L0_gnn_setup()
    _L0_gnn_in = {k: v for k, v in _L0_gnn_all.items() if k in ('edge_type_weights', 'wq', 'bq', 'wk', 'bk', 'wv', 'bv', 'wiq', 'biq', 'wik', 'bik', 'wiv', 'biv', 'wo', 'bo')}
    del _L0_gnn_all

    def _L0_ffn_setup():
        import jax, jax.numpy as jnp
        import numpy as np
        D, H, E, K = (1024, 512, 8, 2)
        B, T = (2, 256)

        def _layernorm(x, g, b, eps=1e-05):
            mu = jnp.mean(x, axis=-1, keepdims=True)
            var = jnp.mean(jnp.square(x - mu), axis=-1, keepdims=True)
            return (x - mu) * jax.lax.rsqrt(var + eps) * g + b

        def _expert(x, g, b, W1, b1, W2, b2, Wo, bo):
            x = _layernorm(x, g, b)
            x1 = x @ W1 + b1
            x2 = jnp.clip(x @ W2 + b2, -20.0, 20.0)
            hidden = jnp.clip(x1 * (x2 * jax.nn.sigmoid(x2)), -10000.0, 10000.0)
            return jnp.clip(hidden @ Wo + bo, -10000.0, 10000.0)
        key = jax.random.key(seed)
        ks = jax.random.split(key, 6)
        s = 0.02
        return {'x': jax.random.normal(ks[0], (B, T, D), jnp.float32), 'ln_g': jnp.ones((D,), jnp.float32), 'ln_b': jnp.zeros((D,), jnp.float32), 'router_w': jax.random.normal(ks[1], (D, E), jnp.float32) * s, 'eg': jnp.ones((E, D), jnp.float32), 'eb': jnp.zeros((E, D), jnp.float32), 'W1': jax.random.normal(ks[2], (E, D, H), jnp.float32) * s, 'b1': jnp.zeros((E, H), jnp.float32), 'W2': jax.random.normal(ks[3], (E, D, H), jnp.float32) * s, 'b2': jnp.zeros((E, H), jnp.float32), 'Wo': jax.random.normal(ks[4], (E, H, D), jnp.float32) * s, 'bo': jnp.zeros((E, D), jnp.float32)}
    _L0_ffn_all = _L0_ffn_setup()
    _L0_ffn_in = {k: v for k, v in _L0_ffn_all.items() if k in ('ln_g', 'ln_b', 'router_w', 'eg', 'eb', 'W1', 'b1', 'W2', 'b2', 'Wo', 'bo')}
    del _L0_ffn_all
    return {'x': x, 'src': src, 'dst': dst, 'edge_type_5': edge_type_5, 'L0_gnn_edge_type_weights': _L0_gnn_in['edge_type_weights'], 'L0_gnn_wq': _L0_gnn_in['wq'], 'L0_gnn_bq': _L0_gnn_in['bq'], 'L0_gnn_wk': _L0_gnn_in['wk'], 'L0_gnn_bk': _L0_gnn_in['bk'], 'L0_gnn_wv': _L0_gnn_in['wv'], 'L0_gnn_bv': _L0_gnn_in['bv'], 'L0_gnn_wiq': _L0_gnn_in['wiq'], 'L0_gnn_biq': _L0_gnn_in['biq'], 'L0_gnn_wik': _L0_gnn_in['wik'], 'L0_gnn_bik': _L0_gnn_in['bik'], 'L0_gnn_wiv': _L0_gnn_in['wiv'], 'L0_gnn_biv': _L0_gnn_in['biv'], 'L0_gnn_wo': _L0_gnn_in['wo'], 'L0_gnn_bo': _L0_gnn_in['bo'], 'L0_ffn_ln_g': _L0_ffn_in['ln_g'], 'L0_ffn_ln_b': _L0_ffn_in['ln_b'], 'L0_ffn_router_w': _L0_ffn_in['router_w'], 'L0_ffn_eg': _L0_ffn_in['eg'], 'L0_ffn_eb': _L0_ffn_in['eb'], 'L0_ffn_W1': _L0_ffn_in['W1'], 'L0_ffn_b1': _L0_ffn_in['b1'], 'L0_ffn_W2': _L0_ffn_in['W2'], 'L0_ffn_b2': _L0_ffn_in['b2'], 'L0_ffn_Wo': _L0_ffn_in['Wo'], 'L0_ffn_bo': _L0_ffn_in['bo']}

def reference(x, src, dst, edge_type_5, L0_gnn_edge_type_weights, L0_gnn_wq, L0_gnn_bq, L0_gnn_wk, L0_gnn_bk, L0_gnn_wv, L0_gnn_bv, L0_gnn_wiq, L0_gnn_biq, L0_gnn_wik, L0_gnn_bik, L0_gnn_wiv, L0_gnn_biv, L0_gnn_wo, L0_gnn_bo, L0_ffn_ln_g, L0_ffn_ln_b, L0_ffn_router_w, L0_ffn_eg, L0_ffn_eb, L0_ffn_W1, L0_ffn_b1, L0_ffn_W2, L0_ffn_b2, L0_ffn_Wo, L0_ffn_bo):
    import jax
    import jax.numpy as jnp

    def _L0_gnn_ref(x, edge_index, edge_type, edge_type_weights, wq, bq, wk, bk, wv, bv, wiq, biq, wik, bik, wiv, biv, wo, bo):
        import jax, jax.numpy as jnp
        import numpy as np
        N = 384
        E = 12288
        IN_F = 1024
        OUT_F = 1024
        H = 16
        D = OUT_F // H
        NUM_ETYPES = 4

        def _build_mask(edge_index, edge_type, edge_type_weights, dtype):
            src, dst = (edge_index[0], edge_index[1])
            w = jax.nn.softplus(edge_type_weights)
            mask = jnp.full((N, N), -jnp.inf, dtype=dtype)
            mask = mask.at[src, dst].set(w[edge_type - 1])
            diag = jnp.diagonal(mask)
            idx = jnp.arange(N)
            mask = mask.at[idx, idx].set(jnp.where(jnp.isneginf(diag), w[3], diag))
            return mask
        q = x @ wq.T + bq
        k = x @ wk.T + bk
        v = x @ wv.T + bv
        q2 = (q @ wiq.T + biq).reshape(N, H, D).transpose(1, 0, 2)
        k2 = (k @ wik.T + bik).reshape(N, H, D).transpose(1, 0, 2)
        v2 = (v @ wiv.T + biv).reshape(N, H, D).transpose(1, 0, 2)
        mask = _build_mask(edge_index, edge_type, edge_type_weights, x.dtype)
        scale = 1.0 / np.sqrt(D).astype(np.float32)
        scores = jnp.einsum('hnd,hmd->hnm', q2, k2) * scale + mask[None]
        attn = jax.nn.softmax(scores, axis=-1)
        out = jnp.einsum('hnm,hmd->hnd', attn, v2)
        out = out.transpose(1, 0, 2).reshape(N, OUT_F)
        return out @ wo.T + bo

    def _L0_ffn_ref(x, ln_g, ln_b, router_w, eg, eb, W1, b1, W2, b2, Wo, bo):
        import jax, jax.numpy as jnp
        import numpy as np
        D, H, E, K = (1024, 512, 8, 2)
        B, T = (2, 256)

        def _layernorm(x, g, b, eps=1e-05):
            mu = jnp.mean(x, axis=-1, keepdims=True)
            var = jnp.mean(jnp.square(x - mu), axis=-1, keepdims=True)
            return (x - mu) * jax.lax.rsqrt(var + eps) * g + b

        def _expert(x, g, b, W1, b1, W2, b2, Wo, bo):
            x = _layernorm(x, g, b)
            x1 = x @ W1 + b1
            x2 = jnp.clip(x @ W2 + b2, -20.0, 20.0)
            hidden = jnp.clip(x1 * (x2 * jax.nn.sigmoid(x2)), -10000.0, 10000.0)
            return jnp.clip(hidden @ Wo + bo, -10000.0, 10000.0)
        Bb, Tt, Dd = x.shape
        xf = _layernorm(x.reshape(-1, Dd), ln_g, ln_b)
        N = xf.shape[0]
        logits = xf @ router_w
        scores, idx = jax.lax.top_k(logits, K)
        gate = jax.nn.softmax(scores, axis=-1)
        gates_e = jnp.zeros((N, E), xf.dtype).at[jnp.arange(N)[:, None], idx].add(gate)

        def body(acc, p):
            gcol, g, b, w1, bb1, w2, bb2, wo, bbo = p
            return (acc + gcol[:, None] * _expert(xf, g, b, w1, bb1, w2, bb2, wo, bbo), None)
        out, _ = jax.lax.scan(body, jnp.zeros_like(xf), (gates_e.T, eg, eb, W1, b1, W2, b2, Wo, bo))
        return out.reshape(Bb, Tt, Dd)
    edge_index = jnp.stack([src, dst])
    x = x + _L0_gnn_ref(_layernorm(x, axis=-1), edge_index, edge_type_5, L0_gnn_edge_type_weights, L0_gnn_wq, L0_gnn_bq, L0_gnn_wk, L0_gnn_bk, L0_gnn_wv, L0_gnn_bv, L0_gnn_wiq, L0_gnn_biq, L0_gnn_wik, L0_gnn_bik, L0_gnn_wiv, L0_gnn_biv, L0_gnn_wo, L0_gnn_bo)
    x = x + _L0_ffn_ref(_layernorm(x, axis=-1)[None], L0_ffn_ln_g, L0_ffn_ln_b, L0_ffn_router_w, L0_ffn_eg, L0_ffn_eb, L0_ffn_W1, L0_ffn_b1, L0_ffn_W2, L0_ffn_b2, L0_ffn_Wo, L0_ffn_bo)[0]
    return x

_drawn_inputs = setup_inputs


def setup_inputs(seed=0):
    import zlib

    import numpy as np

    out = dict(_drawn_inputs(seed))
    spreads = {'L0_ffn_ln_g': (1.0, 0.2),
     'L0_ffn_ln_b': (0.0, 0.1),
     'L0_ffn_eg': (1.0, 0.6),
     'L0_ffn_eb': (0.0, 0.702),
     'L0_ffn_b1': (0.0, 0.646),
     'L0_ffn_b2': (0.0, 0.625),
     'L0_ffn_bo': (0.0, 0.1)}
    factors = {'L0_gnn_edge_type_weights': 6.319,
     'L0_gnn_wq': 4.013,
     'L0_gnn_bq': 8.0,
     'L0_gnn_wk': 4.129,
     'L0_gnn_bk': 8.0,
     'L0_gnn_bv': 6.33,
     'L0_gnn_wiq': 4.087,
     'L0_gnn_biq': 8.0,
     'L0_gnn_wik': 4.203,
     'L0_gnn_bik': 8.0,
     'L0_gnn_biv': 3.586}
    for name, (base, spread) in spreads.items():
        noise = np.random.default_rng([zlib.crc32(name.encode()), seed]).standard_normal(out[name].shape)
        drawn = base * np.exp(spread * noise) if base else spread * noise
        out[name] = jnp.asarray(drawn.astype(out[name].dtype))
    for name, factor in factors.items():
        out[name] = (out[name] * factor).astype(out[name].dtype)
    return out
```

```python
from contextlib import ExitStack, contextmanager

import numpy as np

import concourse.bass as bass
from concourse import mybir
from concourse.alu_op_type import AluOpType as ALU

F32 = mybir.dt.float32
F32R = mybir.dt.float32r
F16 = mybir.dt.float16
BF16 = mybir.dt.bfloat16
I32 = mybir.dt.int32
U32 = mybir.dt.uint32
ACT = mybir.ActivationFunctionType
AX = mybir.AxisListType.X

P = 128
N = 384
NT = N // P
D = 1024
KT = D // P
HEADS = 16
HD = D // HEADS
EDGES = 6144
EG = EDGES // P
NE = 8
HF = 512
HT = HF // P
EPS = 1e-5
NEG = -1e30
BIG = 3.0e38
CK = 4
CW = 512
CE = CK * CW
GNN_CHUNKS = 7 * 4
EXP_CHUNKS = 6
CAP = P
RAW = 3
PIECE = 12
OH = 4


def expert_order():
    order = []
    for e in range(NE + 1):
        if e < NE:
            order += [(e, 0), (e, 1), (e, 2), (e, 3)]
        if e > 0:
            order += [(e - 1, 4), (e - 1, 5)]
    return order


EXPERT_ORDER = expert_order()
CHUNKS = GNN_CHUNKS + len(EXPERT_ORDER)
SLOT = [c % 3 for c in range(GNN_CHUNKS)] + [(3, 4, 5, 1, 2, 0)[j % 6] for j in range(len(EXPERT_ORDER))]


def before(c):
    return max((p + 1 for p in range(c) if SLOT[p] == SLOT[c]), default=0)


def gnn_ffn(nc, x, src, dst, ety, srcb, dstb, ew, wg, bcols, bo, lng, lnb, rw, egc, ebc, wf, b1, b2, be, out):
    ctx = ExitStack()
    with ctx:
        def sem(name):
            return ctx.enter_context(nc.semaphore(name))

        def psum(name, shape, dt=F32):
            return ctx.enter_context(nc.psum_tensor(name, shape, dt))

        def sb(stack, name, shape, dt):
            return stack.enter_context(nc.sbuf_tensor(name, shape, dt))

        raw = sb(ctx, "raw", [P, RAW, CE], F32)
        hi = [sb(ctx, f"hi{s}", [P, CE], F32R) for s in range(3)]
        lo = [sb(ctx, f"lo{s}", [P, CE], F32R) for s in range(3)]
        ident = sb(ctx, "ident", [P, P], F32)
        small = sb(ctx, "small", [P, 192], F32)

        gnn = ExitStack()
        with gnn:
            xt_hi = sb(gnn, "xt_hi", [P, KT, N], F32R)
            xt_lo = sb(gnn, "xt_lo", [P, KT, N], F32R)
            t_hi = sb(gnn, "t_hi", [P, KT, N], F32R)
            t_lo = sb(gnn, "t_lo", [P, KT, N], F32R)
            v_hi = sb(gnn, "v_hi", [P, NT, D], F32R)
            v_lo = sb(gnn, "v_lo", [P, NT, D], F32R)
            mask8 = sb(gnn, "mask8", [P, NT, N], F32)
            with ExitStack() as early:
                xin = sb(early, "xin", [P, NT, D], F32)
                src_i = sb(early, "src_i", [P, 2, PIECE * P], I32)
                dst_i = sb(early, "dst_i", [P, 2, PIECE * P], I32)
                keyb = sb(early, "keyb", [P, PIECE * P], F32)
                eqt = sb(early, "eqt", [P, 2, P], F32)
            with ExitStack() as early2:
                s_oh = sb(early2, "s_oh", [P, OH, N], BF16)
                d_oh = sb(early2, "d_oh", [P, OH, N], BF16)
                code = sb(early2, "code", [P, NT, N], I32)
                term = sb(early2, "term", [P, 4, NT, N], F32)
            k_hi = sb(gnn, "k_hi", [P, KT, N], F32R)
            k_lo = sb(gnn, "k_lo", [P, KT, N], F32R)
            pr = sb(gnn, "pr", [P, 2, NT, N], F32)
            at_hi = sb(gnn, "at_hi", [P, 2, NT, N], F32R)
            at_lo = sb(gnn, "at_lo", [P, 2, NT, N], F32R)
            cols = sb(gnn, "cols", [P, 3, EG], I32)
            colf = sb(gnn, "colf", [P, 5, EG], F32)
            bits = sb(gnn, "bits", [P, 2, EG], I32)
            gbias = sb(gnn, "gbias", [P, 6, KT], F32)
            iota16 = sb(gnn, "iota16", [P, N], F16)
            later = sb(gnn, "later", [P, P], F32)
            dgb = sb(gnn, "dgb", [P, P], BF16)
            idb = sb(gnn, "idb", [P, P], BF16)
            eiota = sb(gnn, "eiota", [P, EG], F32)
            ewb = sb(gnn, "ewb", [P, 4, 4], F32)
        q_hi, q_lo = xt_hi, xt_lo

        with ExitStack() as ffn:
            xres = sb(ffn, "xres", [P, NT, D], F32)
            lngb = sb(ffn, "lngb", [P, D], F32)
            lnbb = sb(ffn, "lnbb", [P, D], F32)
            bob = sb(ffn, "bob", [P, D], F32)
            with ExitStack() as last:
                yg = sb(last, "yg", [P, 2 * NT, D], F32)
            xg = sb(ffn, "xg", [P, 2, D], F32)
            xg_hi = sb(ffn, "xg_hi", [P, 2, KT, P], F32R)
            xg_lo = sb(ffn, "xg_lo", [P, 2, KT, P], F32R)
            hi += [sb(ffn, f"hi{s}", [P, CE], F32R) for s in (3, 4, 5)]
            lo += [sb(ffn, f"lo{s}", [P, CE], F32R) for s in (3, 4, 5)]
            with ExitStack() as rowbuild:
                brow_f = sb(rowbuild, "brow_f", [48, 2 * D], F32)
            with ExitStack() as experts:
                y = sb(experts, "y", [P, 2, D], F32)
            xf = sb(ffn, "xf", [P, NT, D], F32)
            brow = sb(ffn, "brow", [48, 2 * D], F32R)
            with ExitStack() as router:
                xft = sb(router, "xft", [P, KT, P], F32)
            x2c = sb(ffn, "x2c", [P, CW], F32)
            sg = sb(ffn, "sg", [P, CW], F32)
            hh = sb(ffn, "hh", [P, CW], F32)
            with ExitStack() as router2:
                slot_oh = sb(router2, "slot_oh", [P, NE, NT, P], F16)
            ht_hi = sb(ffn, "ht_hi", [P, 2, HT, P], F32R)
            ht_lo = sb(ffn, "ht_lo", [P, 2, HT, P], F32R)
            rws = sb(ffn, "rws", [P, KT, NE], F32)
            egb = sb(ffn, "egb", [P, 2, NE, KT], F32)
            sels = sb(ffn, "sels", [48, NE], F32)
            selx = sb(ffn, "selx", [48, 2, P], F32R)
            r8 = sb(ffn, "r8", [P, 12, NT, NE], F32)
            r3 = sb(ffn, "r3", [P, 10, NT], F32)
            sel16 = sb(ffn, "sel16", [P, NT, NE], F16)
            ones16 = sb(ffn, "ones16", [P, P], F16)
            later16 = sb(ffn, "later16", [P, P], F16)
            slots16 = sb(ffn, "slots16", [P, P], F16)
            tok16 = sb(ffn, "tok16", [P, NT], F16)
            slot_tok = sb(ffn, "slot_tok", [P, NE], U32)
            most = sb(ffn, "most", [P, 1], I32)
            over_cols = sb(ffn, "over_cols", [P, 2, KT], F32)
            rows_u = sb(ffn, "rows_u", [P, 2, NT], U32)
            fstat = sb(ffn, "fstat", [P, NT, 2, 6], F32)
            xstat = sb(ffn, "xstat", [P, NT, 2, 6], F32)
            fmv = sb(ffn, "fmv", [P, NT, 4], F32)
            fr = sb(ffn, "fr", [P, NT, 8], F32)
        zbuf = nc.dram_tensor("z_rows", (N, D), F32, kind="Internal").ap()
        ybuf = nc.dram_tensor("y_rows", (NE * CAP, D), F32, kind="Internal").ap()

        ps = psum("ps", [P, 8, CW])
        B = [ps[:, i, :] for i in range(8)]

        raw_ready = [sem(f"raw_ready{s}") for s in range(RAW)]
        hi_done, lo_done, chunk_used = sem("hi_done"), sem("lo_done"), sem("chunk_used")
        x_in = [sem(f"x_in{t}") for t in range(NT)]
        edges_in, bias_in, keys_in = sem("edges_in"), sem("bias_in"), [sem("keys_in0"), sem("keys_in1")]
        consts_ready = sem("consts_ready")
        stats_ready, rstd_ready, pool_chain = sem("stats_ready"), sem("rstd_ready"), sem("pool_chain")
        normed, x_turned, x_hi, x_lo = sem("normed"), sem("x_turned"), sem("x_hi"), sem("x_lo")
        dve_chain, act_chain = sem("dve_chain"), sem("act_chain")
        mask_summed, bank_hi, group_evacuated = sem("mask_summed"), sem("bank_hi"), sem("group_evacuated")
        piece_done = sem("piece_done")
        onehots, onehots_used = sem("onehots"), sem("onehots_used")
        types_ready, mask_ready = sem("types_ready"), sem("mask_ready")
        score_ready, score_max, exp_done, inv_ready, normalised = (
            sem("score_ready"), sem("score_max"), sem("exp_done"), sem("inv_ready"), sem("normalised"))
        p_turned, at_hi_done, at_lo_done = sem("p_turned"), sem("at_hi_done"), sem("at_lo_done")
        o_ready, o_hi_done, o_lo_done = sem("o_ready"), sem("o_hi_done"), sem("o_lo_done")
        proj_ready, resid_done, resid_in = sem("proj_ready"), sem("resid_done"), sem("resid_in")
        stored = sem("stored")
        ffn_in, rows_in, ffn_consts, rows_ready = sem("ffn_in"), sem("rows_in"), sem("ffn_consts"), sem("rows_ready")
        mv_ready, xf_ready, xf_mv_ready, fr_ready, z_ready = sem("mv_ready"), sem("xf_ready"), sem("xf_mv_ready"), sem("fr_ready"), sem("z_ready")
        xf_turned, xft_ready, logits_ready, z_stored = sem("xf_turned"), sem("xft_ready"), sem("logits_ready"), sem("z_stored")
        gap_ready, gates_ready, sel_ready, pos_ready = sem("gap_ready"), sem("gates_ready"), sem("sel_ready"), sem("pos_ready")
        slot_oh_ready, tok_summed, tok_ready, rows_u_ready = sem("slot_oh_ready"), sem("tok_summed"), sem("tok_ready"), sem("rows_u_ready")
        gathered, sel_set = [sem("gathered0"), sem("gathered1")], sem("sel_set")
        xg_turned, xg_scaled, xg_hi_done, xg_lo_done = sem("xg_turned"), sem("xg_scaled"), sem("xg_hi_done"), sem("xg_lo_done")
        x2_clipped, sig_done, h_ready, h_turned, ht_hi_done, ht_lo_done = (
            sem("x2_clipped"), sem("sig_done"), sem("h_ready"), sem("h_turned"), sem("ht_hi_done"), sem("ht_lo_done"))
        x1_used, y_ready, y_stored = sem("x1_used"), sem("y_ready"), [sem("y_stored0"), sem("y_stored1")]
        y_rows_in = [sem(f"y_rows_in{j}") for j in range(2 * NT)]
        out_ready = sem("out_ready")
        most_ready, over_raw, over_cols_in = sem("most_ready"), [sem(f"over_raw{s}") for s in range(RAW)], sem("over_cols_in")
        over_w_hi, over_w_lo, over_expert, over_z_in = sem("over_w_hi"), sem("over_w_lo"), sem("over_expert"), sem("over_z_in")
        over_sel, over_turned, over_hi, over_lo = sem("over_sel"), sem("over_turned"), sem("over_hi"), sem("over_lo")
        over_up, over_clipped, over_sig, over_h = sem("over_up"), sem("over_clipped"), sem("over_sig"), sem("over_h")
        over_scaled, over_done, over_h_turned, over_h_hi, over_h_lo, over_down, over_added = (
            sem("over_scaled"), sem("over_done"), sem("over_h_turned"), sem("over_h_hi"), sem("over_h_lo"), sem("over_down"), sem("over_added"))
        over_dve = sem("over_dve")

        def f0(e):
            return GNN_CHUNKS + 6 * e - 2

        def up_chunks(e):
            return f0(e) + (2 if e == 0 else 0)

        stat = small[:, 0:36].rearrange("p (t k) -> p t k", t=NT)
        mv = small[:, 36:42].rearrange("p (t k) -> p t k", t=NT)
        rs = small[:, 42:48]
        halfneg = small[:, 48:49]
        negmax = small[:, 52:58].rearrange("p (b i) -> p b i", b=2)
        rsum = small[:, 58:64].rearrange("p (b i) -> p b i", b=2)
        rinv = small[:, 64:70].rearrange("p (b i) -> p b i", b=2)

        SCALE8 = 1.0 / 8.0

        HALVES = [(m, h) for m in range(6) for h in range(2)]
        NAMES = ["v1", "v2", "k1", "k2", "q1", "q2"]
        MASK_GROUP = 4
        OF_HALF = [i if i < MASK_GROUP else i + 1 for i in range(12)]

        def banks(group):
            return B[0:4] if group % 2 == 0 else B[4:8]

        def f32(ap):
            return ap.bitcast(F32)

        @contextmanager
        def crowded(engine):
            engine.wait_ge(most_ready, 1)
            tokens = engine.value_load(most[0:1, 0:1])
            with engine.If(tokens > CAP):
                with engine.Fori(0, NE) as e:
                    yield e

        block = ctx.enter_context(nc.Block())

        @block.sync
        def _(sp):
            xv = x.rearrange("(t p) d -> p t d", p=P)
            for t in range(NT):
                sp.dma_start(xin[:, t, :], xv[:, t, :]).then_inc(x_in[t], 16)

            def load(c):
                if c >= RAW:
                    sp.wait_ge(lo_done, c - RAW + 1)
                srcw = wg[c] if c < GNN_CHUNKS else wf[EXPERT_ORDER[c - GNN_CHUNKS][0], EXPERT_ORDER[c - GNN_CHUNKS][1]]
                sp.dma_start(raw[:, c % RAW, :], srcw).then_inc(raw_ready[c % RAW], 16)

            for c in range(30):
                load(c)
            sp.wait_ge(o_ready, HEADS)
            sp.wait_ge(rows_in, 1)
            for r in (0, 32):
                for a, cut in ((b1, slice(0, CW)), (b2, slice(CW, 2 * CW)), (be, slice(D, 2 * D))):
                    sp.dma_start(brow_f[r:r + NE, cut], a).then_inc(ffn_in, 16)
            for t in range(NT):
                sp.dma_start(xres[:, t, :], xv[:, t, :]).then_inc(resid_in, 16)
            for a, b in ((bob, bo), (lngb, lng), (lnbb, lnb)):
                sp.dma_start(a[:, :], b.partition_broadcast(P)).then_inc(resid_in, 16)
            for a, b in ((rws[:, :, :], rw), (egb[:, 0, :, :], egc), (egb[:, 1, :, :], ebc)):
                sp.dma_start(a, b).then_inc(resid_in, 16)
            for c in range(30, 33):
                load(c)
            for t in range(NT):
                sp.wait_ge(z_ready, t + 1)
                sp.dma_start(zbuf[t * P:(t + 1) * P, :], xf[:, t, :]).then_inc(z_stored, 16)
                load(33 + t)

            def y_store(e, par):
                sp.wait_ge(y_ready, e + 1)
                sp.dma_start(ybuf[e * CAP:(e + 1) * CAP, :], y[:, par, :]).then_inc(y_stored[par], 16)

            for c in range(36, CHUNKS):
                if c >= f0(2) + 4 and (c - f0(2) - 4) % 6 == 0:
                    e = (c - f0(2) - 4) // 6
                    y_store(e, e % 2)
                load(c)
            done = (CHUNKS - 1 - f0(2) - 4) // 6 + 1
            for e in range(done, NE):
                y_store(e, e % 2)
            with crowded(sp) as e:
                sp.wait_ge(over_expert, e + 1)
                for j in range(EXP_CHUNKS):
                    if j >= RAW:
                        sp.wait_ge(over_w_lo, e * EXP_CHUNKS + (j - RAW + 1))
                    sp.dma_start(raw[:, j % RAW, :], wf[bass.ds(e, 1), j].rearrange("o p c -> (o p) c")).then_inc(over_raw[j % RAW], 16)
                for j, a in enumerate((egc, ebc)):
                    sp.dma_start(over_cols[:, j, :], a[:, bass.ds(e, 1), :].rearrange("p o k -> p (o k)")).then_inc(over_cols_in, 16)
                for t in range(1, NT):
                    if t > 1:
                        sp.wait_ge(over_turned, e * (NT - 1) + (t - 1))
                    sp.dma_start(xg[:, 1, :], zbuf[t * P:(t + 1) * P, :]).then_inc(over_z_in, 16)
            for t in range(NT):
                sp.wait_ge(out_ready, t + 1)
                sp.dma_start(out[t * P:(t + 1) * P, :], xres[:, t, :]).then_inc(stored, 16)
            sp.wait_ge(stored, 16 * NT)

        @block.gpsimd
        def _(pool):
            chain = [0]

            def link(ins):
                chain[0] += 1
                ins.then_inc(pool_chain, 1)
                pool.wait_ge(pool_chain, chain[0])

            pool.memset(halfneg, -0.5).then_inc(consts_ready, 1)
            link(pool.memset(ident[:, :], 0.0))
            pool.affine_select(out=ident[:, :], in_=ident[:, :], compare_op=ALU.not_equal, fill=1.0, base=0,
                               pattern=[[-1, P]], channel_multiplier=1).then_inc(consts_ready, 1)
            link(pool.memset(later[:, :], 1.0))
            pool.affine_select(out=later[:, :], in_=later[:, :], compare_op=ALU.is_gt, fill=0.0, base=0,
                               pattern=[[1, P]], channel_multiplier=-1).then_inc(consts_ready, 1)
            pool.iota(iota16[:, :], pattern=[[1, N]], base=0, channel_multiplier=0,
                      allow_small_or_imprecise_dtypes=True).then_inc(consts_ready, 1)
            pool.iota(eiota[:, :], pattern=[[4, EG]], base=31, channel_multiplier=0,
                      allow_small_or_imprecise_dtypes=True).then_inc(consts_ready, 1)
            for t in range(NT):
                pool.wait_ge(stats_ready, t + 1)
                link(pool.tensor_scalar(rs[:, t:t + 1], mv[:, t, 1:2], EPS, None, ALU.add))
                pool.tensor_tensor(rs[:, 3 + t:4 + t], rs[:, t:t + 1], halfneg, ALU.pow).then_inc(rstd_ready, 1)
            for h in range(HEADS):
                pool.wait_ge(inv_ready, h + 1)
                for i in range(NT):
                    pool.tensor_scalar(pr[:, h % 2, i, :], pr[:, h % 2, i, :], rinv[:, h % 2, i:i + 1], None,
                                       ALU.mult).then_inc(normalised, 1)

            pool.wait_ge(o_ready, HEADS)
            pool.memset(brow_f[:, :], 0.0).then_inc(rows_in, 1)
            link(pool.memset(sels[:, :], 0.0))
            for base in (0, -32):
                link(pool.affine_select(out=sels[:, :], in_=sels[:, :], compare_op=ALU.not_equal, fill=1.0, base=base,
                                        pattern=[[-1, NE]], channel_multiplier=1))
            pool.memset(ones16[:, :], 1.0).then_inc(ffn_consts, 1)
            link(pool.memset(later16[:, :], 1.0))
            pool.affine_select(out=later16[:, :], in_=later16[:, :], compare_op=ALU.is_gt, fill=0.0, base=0,
                               pattern=[[1, P]], channel_multiplier=-1).then_inc(ffn_consts, 1)
            pool.iota(slots16[:, :], pattern=[[1, P]], base=0, channel_multiplier=0,
                      allow_small_or_imprecise_dtypes=True).then_inc(ffn_consts, 1)
            pool.iota(tok16[:, :], pattern=[[P, NT]], base=0, channel_multiplier=1,
                      allow_small_or_imprecise_dtypes=True).then_inc(ffn_consts, 1)
            pool.iota(r8[:, 10, :, :], pattern=[[0, NT], [-1, NE]], base=NE, channel_multiplier=0,
                      allow_small_or_imprecise_dtypes=True).then_inc(ffn_consts, 1)
            pool.iota(r8[:, 11, :, :], pattern=[[0, NT], [CAP, NE]], base=0, channel_multiplier=0,
                      allow_small_or_imprecise_dtypes=True).then_inc(ffn_consts, 1)
            for t in range(NT):
                v, a, r1, b, r2 = fmv[:, t, 1:2], fr[:, t, 0:1], fr[:, t, 1:2], fr[:, t, 2:3], fr[:, t, 3:4]
                pool.wait_ge(mv_ready, t + 1)
                link(pool.tensor_scalar(a, v, EPS, None, ALU.add))
                link(pool.tensor_tensor(r1, a, halfneg, ALU.pow))
                link(pool.tensor_scalar(b, r1, r1, v, ALU.mult, ALU.mult))
                link(pool.tensor_scalar(b, b, EPS, None, ALU.add))
                link(pool.tensor_tensor(r2, b, halfneg, ALU.pow))
                pool.tensor_tensor(fr[:, t, 4:5], r1, r2, ALU.mult).then_inc(fr_ready, 1)
                pool.wait_ge(xf_mv_ready, t + 1)
                link(pool.tensor_scalar(fr[:, t, 5:6], fmv[:, t, 3:4], EPS, None, ALU.add))
                pool.tensor_tensor(fr[:, t, 6:7], fr[:, t, 5:6], halfneg, ALU.pow).then_inc(fr_ready, 1)

            def gather_tokens(e, par):
                pool.indirect_dma_start(out=xg[:, par, :], out_offset=None, in_=zbuf[:, :],
                                        in_offset=bass.IndirectOffsetOnAxis(ap=slot_tok[:, e:e + 1], axis=0)).then_inc(gathered[par], 16)

            def select(e, par):
                pool.tensor_copy(selx[:, par, :], sels[:, e:e + 1].to_broadcast([48, P])).then_inc(sel_set, 1)

            pool.wait_ge(z_stored, 16 * NT)
            pool.wait_ge(tok_ready, 1)
            gather_tokens(0, 0)
            gather_tokens(1, 1)
            select(0, 0)
            select(1, 1)
            pool.wait_ge(tok_ready, 2)
            for e in range(NE - 2):
                pool.wait_ge(xg_lo_done, e + 1)
                gather_tokens(e + 2, e % 2)
                pool.wait_ge(chunk_used, f0(e + 1) + 5)
                select(e + 2, e % 2)
            pool.wait_ge(rows_u_ready, 1)
            for par in range(2):
                pool.wait_ge(y_stored[par], 16 * NE // 2)
            pool.wait_ge(over_done, 1)
            for j in range(2 * NT):
                pool.indirect_dma_start(out=yg[:, j, :], out_offset=None, in_=ybuf[:, :],
                                        in_offset=bass.IndirectOffsetOnAxis(ap=rows_u[:, j % 2, j // 2:j // 2 + 1], axis=0)).then_inc(y_rows_in[j], 16)

        @block.scalar
        def _(act):
            for j, a in enumerate((src, dst, ety)):
                act.dma_start(cols[:, j, :], a).then_inc(edges_in, 16)
            act.dma_start(gbias[:, :, :], bcols).then_inc(bias_in, 16)
            act.dma_start(ewb[:, 0, :], ew.partition_broadcast(P)).then_inc(bias_in, 16)

            def keys(q):
                if q >= 2:
                    act.wait_ge(piece_done, q - 1)
                for a, b in ((src_i, srcb), (dst_i, dstb)):
                    act.dma_start(a[:, q % 2, :], b[q * PIECE * P:(q + 1) * PIECE * P].partition_broadcast(P)).then_inc(keys_in[q % 2], 16)

            def split_hi(c):
                act.wait_ge(raw_ready[c % RAW], 16 * (c // RAW + 1))
                if before(c):
                    act.wait_ge(chunk_used, before(c))
                act.activation(hi[SLOT[c]][:, :], raw[:, c % RAW, :], ACT.Copy).then_inc(hi_done, 1)

            chain = [0]

            def link(ins):
                chain[0] += 1
                ins.then_inc(act_chain, 1)
                act.wait_ge(act_chain, chain[0])

            act.wait_ge(bias_in, 32)
            link(act.activation(ewb[:, 1, :], ewb[:, 0, :], ACT.Abs))
            link(act.activation(ewb[:, 1, :], ewb[:, 1, :], ACT.Exp, scale=-1.0))
            act.activation(ewb[:, 1, :], ewb[:, 1, :], ACT.Ln, bias=1.0).then_inc(types_ready, 1)
            split_hi(0)
            split_hi(1)
            for t in range(NT):
                act.wait_ge(x_turned, t + 1)
                for half in range(2):
                    act.activation(xt_hi[:, 4 * half:4 * half + 4, t * P:(t + 1) * P],
                                   B[2 * t + half][:, :].rearrange("p (k n) -> p k n", k=4), ACT.Copy).then_inc(x_hi, 1)

            def evac(i):
                m, h = HALVES[i]
                group = OF_HALF[i]
                act.wait_ge(chunk_used, 2 * i + 2)
                if NAMES[m] == "v2":
                    for t in range(NT):
                        act.activation(v_hi[:, t, h * CW:(h + 1) * CW], banks(group)[t][:, :], ACT.Copy).then_inc(bank_hi, 1)
                    return
                to = {"v1": t_hi, "k1": t_hi, "q1": t_hi, "k2": k_hi, "q2": q_hi}[NAMES[m]]
                for b in range(4):
                    o = 4 * h + b
                    act.activation(to[:, o, :], banks(group)[b][:, 0:N], ACT.Identity,
                                   bias=gbias[:, m, o:o + 1]).then_inc(bank_hi, 1)

            for i in range(12):
                split_hi(2 * i + 2)
                split_hi(2 * i + 3)
                if i < 4:
                    keys(i)
                evac(i)
            for s in range(HEADS + 2):
                if s < HEADS:
                    for i in range(NT):
                        act.wait_ge(score_max, 3 * s + i + 1)
                        act.activation(pr[:, s % 2, i, :], pr[:, s % 2, i, :], ACT.Exp, scale=-1.0,
                                       bias=negmax[:, s % 2, i:i + 1], accum_out=rsum[:, s % 2, i:i + 1]).then_inc(exp_done, 1)
                if s == 3:
                    split_hi(26)
                if 1 <= s <= HEADS:
                    h = s - 1
                    if h >= 2:
                        act.wait_ge(o_ready, h - 1)
                    for j in range(NT):
                        act.wait_ge(p_turned, 3 * h + j + 1)
                        act.activation(at_hi[:, h % 2, j, :], B[3 + j][:, 0:N], ACT.Copy).then_inc(at_hi_done, 1)
                if s >= 2:
                    h = s - 2
                    rows = slice(HD * (h % 2), HD * (h % 2) + HD)
                    act.wait_ge(o_ready, h + 1)
                    act.activation(t_hi[rows, h // 2, :], B[6 + h % 2][rows, 0:N], ACT.Identity,
                                   bias=gbias[rows, 1, h // 2:h // 2 + 1]).then_inc(o_hi_done, 1)
            split_hi(27)
            split_hi(28)
            split_hi(29)
            for t in range(NT):
                act.wait_ge(xf_turned, t + 1)
                if t:
                    act.wait_ge(logits_ready, t)
                a = 6 if t % 2 == 0 else 0
                act.activation(xft[:, :, :].rearrange("p (a k) n -> p a (k n)", a=2), ps[:, a:a + 2, :], ACT.Copy).then_inc(xft_ready, 1)
                split_hi(30 + t)
            act.wait_ge(gap_ready, 1)
            act.activation(r3[:, 8, :], r3[:, 7, :], ACT.Sigmoid)
            act.activation(r3[:, 9, :], r3[:, 7, :], ACT.Sigmoid, scale=-1.0).then_inc(gates_ready, 1)

            def scale_tokens(e, par):
                act.wait_ge(xg_turned, e + 1)
                for k in range(KT):
                    ins = act.activation(xg[:, par, k * P:(k + 1) * P], B[5 + k // 4][:, (k % 4) * P:(k % 4 + 1) * P],
                                         ACT.Identity, scale=egb[:, 0, e, k:k + 1], bias=egb[:, 1, e, k:k + 1])
                ins.then_inc(xg_scaled, 1)
                act.wait_ge(xg_scaled, e + 1)
                act.activation(xg_hi[:, par, :, :].rearrange("p k n -> p (k n)"), xg[:, par, :], ACT.Copy).then_inc(xg_hi_done, 1)

            def sigmoid(e):
                act.wait_ge(x2_clipped, e + 1)
                act.activation(sg[:, :], x2c[:, :], ACT.Sigmoid).then_inc(sig_done, 1)

            def turned_hi(e, par):
                act.wait_ge(h_turned, e + 1)
                act.activation(ht_hi[:, par, :, :].rearrange("p k n -> p (k n)"), B[2], ACT.Copy).then_inc(ht_hi_done, 1)

            scale_tokens(0, 0)
            for e in range(NE):
                nxt = [k if 33 <= k < CHUNKS else None for k in range(f0(e) + 3, f0(e) + 9)]
                if nxt[0]:
                    split_hi(nxt[0])
                if e + 1 < NE:
                    scale_tokens(e + 1, (e + 1) % 2)
                if nxt[1]:
                    split_hi(nxt[1])
                sigmoid(e)
                for k in nxt[2:4]:
                    if k:
                        split_hi(k)
                turned_hi(e, e % 2)
                for k in nxt[4:6]:
                    if k:
                        split_hi(k)
            with crowded(act) as e:
                act.wait_ge(over_expert, e + 1)
                for j in range(EXP_CHUNKS):
                    act.wait_ge(over_raw[j % RAW], e * 32 + 16 * (j // RAW + 1))
                    act.activation(hi[j][:, :], raw[:, j % RAW, :], ACT.Copy).then_inc(over_w_hi, 1)
                act.wait_ge(over_cols_in, e * 32 + 32)
                for t in range(1, NT):
                    step = e * (NT - 1) + t
                    act.wait_ge(over_turned, step)
                    for k in range(KT):
                        ins = act.activation(xg[:, 0, k * P:(k + 1) * P], B[5 + k // 4][:, (k % 4) * P:(k % 4 + 1) * P],
                                             ACT.Identity, scale=over_cols[:, 0, k:k + 1], bias=over_cols[:, 1, k:k + 1])
                    ins.then_inc(over_scaled, 1)
                    act.wait_ge(over_scaled, step)
                    act.activation(xg_hi[:, 0, :, :].rearrange("p k n -> p (k n)"), xg[:, 0, :], ACT.Copy).then_inc(over_hi, 1)
                    act.wait_ge(over_clipped, step)
                    act.activation(sg[:, :], x2c[:, :], ACT.Sigmoid).then_inc(over_sig, 1)
                    act.wait_ge(over_h_turned, step)
                    act.activation(ht_hi[:, 0, :, :].rearrange("p k n -> p (k n)"), B[2], ACT.Copy).then_inc(over_h_hi, 1)

        @block.vector
        def _(dve):
            chain = [0]

            def link(ins):
                chain[0] += 1
                ins.then_inc(dve_chain, 1)
                dve.wait_ge(dve_chain, chain[0])

            def split_lo(c):
                dve.wait_ge(hi_done, c + 1)
                dve.tensor_tensor(lo[SLOT[c]][:, :], raw[:, c % RAW, :], f32(hi[SLOT[c]][:, :]), ALU.subtract).then_inc(lo_done, 1)

            for t in range(NT):
                dve.wait_ge(x_in[t], 16)
                for half in range(2):
                    link(dve.bn_stats(stat[:, t, 6 * half:6 * half + 6], xin[:, t, half * CW:(half + 1) * CW]))
                dve.bn_aggr(mv[:, t, :], stat[:, t, :]).then_inc(stats_ready, 1)
            for t in range(NT):
                dve.wait_ge(rstd_ready, t + 1)
                dve.tensor_scalar(xin[:, t, :], xin[:, t, :], mv[:, t, 0:1], rs[:, 3 + t:4 + t], ALU.subtract, ALU.mult).then_inc(normed, 1)
            split_lo(0)
            for t in range(NT):
                for half in range(2):
                    dve.wait_ge(x_hi, 2 * t + half + 1)
                    cut = (slice(None), slice(4 * half, 4 * half + 4), slice(t * P, (t + 1) * P))
                    dve.tensor_tensor(xt_lo[cut], B[2 * t + half][:, :].rearrange("p (k n) -> p k n", k=4),
                                      f32(xt_hi[cut]), ALU.subtract).then_inc(x_lo, 1)
            split_lo(1)

            def evac(i):
                m, h = HALVES[i]
                group = OF_HALF[i]
                n0 = sum(NT if NAMES[HALVES[j][0]] == "v2" else 4 for j in range(i))
                if NAMES[m] == "v2":
                    for t in range(NT):
                        dve.wait_ge(bank_hi, n0 + t + 1)
                        cut = (slice(None), t, slice(h * CW, (h + 1) * CW))
                        ins = dve.tensor_tensor(v_lo[cut], banks(group)[t][:, :], f32(v_hi[cut]), ALU.subtract)
                    ins.then_inc(group_evacuated, 1)
                    return
                th, tl = {"v1": (t_hi, t_lo), "k1": (t_hi, t_lo), "q1": (t_hi, t_lo), "k2": (k_hi, k_lo),
                          "q2": (q_hi, q_lo)}[NAMES[m]]
                for b in range(4):
                    o = 4 * h + b
                    dve.wait_ge(bank_hi, n0 + b + 1)
                    ins = dve.scalar_tensor_tensor(out=tl[:, o, :], in0=banks(group)[b][:, 0:N], scalar=gbias[:, m, o:o + 1],
                                                   in1=f32(th[:, o, :]), op0=ALU.add, op1=ALU.subtract)
                ins.then_inc(group_evacuated, 1)

            def edge_columns():
                dve.wait_ge(edges_in, 48)
                link(dve.tensor_copy(colf[:, 0:2, :], cols[:, 0:2, :]))
                link(dve.scalar_tensor_tensor(out=colf[:, 2, :], in0=colf[:, 0, :], scalar=float(N), in1=colf[:, 1, :],
                                              op0=ALU.mult, op1=ALU.add))
                link(dve.tensor_scalar(bits[:, 0, :], cols[:, 2, :], 3, None, ALU.add))
                link(dve.tensor_scalar(bits[:, 0, :], bits[:, 0, :], 3, None, ALU.bitwise_and))
                dve.wait_ge(consts_ready, 5)
                link(dve.tensor_tensor(bits[:, 0, :], bits[:, 0, :], eiota[:, :], ALU.add))
                link(dve.tensor_scalar(bits[:, 1, :], bits[:, 0, :], 23, None, ALU.logical_shift_left))

            def duplicates(q):
                dve.wait_ge(keys_in[q % 2], 32 * (q // 2 + 1))
                link(dve.scalar_tensor_tensor(out=keyb[:, :], in0=src_i[:, q % 2, :], scalar=float(N), in1=dst_i[:, q % 2, :],
                                              op0=ALU.mult, op1=ALU.add))
                for j in range(PIECE):
                    g = q * PIECE + j
                    ins = dve.scalar_tensor_tensor(out=eqt[:, j % 2, :], in0=keyb[:, j * P:(j + 1) * P],
                                                   scalar=colf[:, 2, g:g + 1], in1=later[:, :], op0=ALU.is_equal,
                                                   op1=ALU.mult, accum_out=colf[:, 3, g:g + 1])
                    link(ins)
                dve.tensor_scalar(colf[:, 4, q * PIECE:(q + 1) * PIECE], colf[:, 3, q * PIECE:(q + 1) * PIECE],
                                  0.0, None, ALU.is_equal).then_inc(piece_done, 1)

            def build_mask():
                dve.wait_ge(piece_done, EG // PIECE)
                link(dve.tensor_tensor(colf[:, 4, :], colf[:, 4, :], bits[:, 1, :].bitcast(F32), ALU.mult))
                link(dve.tensor_copy(idb[:, :], ident[:, :]))
                dve.tensor_scalar(dgb[:, :], ident[:, :], 2.0 ** -97, None, ALU.mult).then_inc(onehots, 1)
                for g in range(EG):
                    if g >= OH:
                        dve.wait_ge(onehots_used, g - OH + 1)
                    dve.tensor_scalar(s_oh[:, g % OH, :], iota16[:, :], colf[:, 0, g:g + 1], None, ALU.is_equal)
                    dve.tensor_scalar(d_oh[:, g % OH, :], iota16[:, :], colf[:, 1, g:g + 1], colf[:, 4, g:g + 1],
                                      ALU.is_equal, ALU.mult).then_inc(onehots, 1)

            def decode_mask():
                dve.wait_ge(types_ready, 1)
                link(dve.tensor_scalar(ewb[:, 3, :], ewb[:, 0, :], 0.0, None, ALU.max))
                link(dve.tensor_tensor(ewb[:, 3, :], ewb[:, 3, :], ewb[:, 1, :], ALU.add))
                link(dve.tensor_scalar(ewb[:, 2, :], ewb[:, 3, :], 8.0, None, ALU.mult))
                dve.wait_ge(mask_summed, 1)
                for t in range(NT):
                    bank = banks(MASK_GROUP)[t][:, 0:N]
                    dve.tensor_scalar(mask8[:, t, :], bank, 0.0, NEG, ALU.is_equal, ALU.mult)
                    ins = dve.tensor_scalar(code[:, t, :], bank.bitcast(I32), 23, 3, ALU.logical_shift_right, ALU.bitwise_and)
                ins.then_inc(group_evacuated, 1)
                dve.wait_ge(group_evacuated, MASK_GROUP + 1)
                for w in range(4):
                    ins = dve.tensor_scalar(term[:, w, :, :], code[:, :, :], float((w + 3) % 4), ewb[:, 2, w:w + 1],
                                            ALU.is_equal, ALU.mult)
                link(ins)
                link(dve.tensor_tensor(term[:, 0:2, :, :], term[:, 0:2, :, :], term[:, 2:4, :, :], ALU.add))
                link(dve.tensor_tensor(term[:, 0, :, :], term[:, 0, :, :], term[:, 1, :, :], ALU.add))
                dve.tensor_tensor(mask8[:, :, :], mask8[:, :, :], term[:, 0, :, :], ALU.add).then_inc(mask_ready, 1)

            for i in range(12):
                if i == MASK_GROUP:
                    build_mask()
                split_lo(2 * i + 2)
                split_lo(2 * i + 3)
                if i == 0:
                    edge_columns()
                if i < 4:
                    duplicates(i)
                if i == MASK_GROUP:
                    decode_mask()
                evac(i)
            dve.wait_ge(mask_ready, 1)
            for s in range(HEADS + 2):
                if s < HEADS:
                    if s >= 2:
                        dve.wait_ge(p_turned, 3 * (s - 1))
                    for i in range(NT):
                        dve.wait_ge(score_ready, 3 * s + i + 1)
                        dve.tensor_tensor_reduce(out=pr[:, s % 2, i, :], in0=B[i][:, 0:N], in1=mask8[:, i, :],
                                                 scale=-SCALE8, scalar=BIG, op0=ALU.add, op1=ALU.min,
                                                 accum_out=negmax[:, s % 2, i:i + 1]).then_inc(score_max, 1)
                if s == 3:
                    split_lo(26)
                if 1 <= s <= HEADS:
                    h = s - 1
                    for j in range(NT):
                        dve.wait_ge(at_hi_done, 3 * h + j + 1)
                        dve.tensor_tensor(at_lo[:, h % 2, j, :], B[3 + j][:, 0:N], f32(at_hi[:, h % 2, j, :]),
                                          ALU.subtract).then_inc(at_lo_done, 1)
                if s < HEADS:
                    dve.wait_ge(exp_done, 3 * s + 3)
                    if s >= 2:
                        dve.wait_ge(normalised, 3 * (s - 1))
                    dve.reciprocal(rinv[:, s % 2, :], rsum[:, s % 2, :]).then_inc(inv_ready, 1)
                if s >= 2:
                    h = s - 2
                    rows = slice(HD * (h % 2), HD * (h % 2) + HD)
                    dve.wait_ge(o_hi_done, h + 1)
                    dve.scalar_tensor_tensor(out=t_lo[rows, h // 2, :], in0=B[6 + h % 2][rows, 0:N],
                                             scalar=gbias[rows, 1, h // 2:h // 2 + 1], in1=f32(t_hi[rows, h // 2, :]),
                                             op0=ALU.add, op1=ALU.subtract).then_inc(o_lo_done, 1)
            split_lo(27)
            dve.wait_ge(ffn_in, 16 * 6)
            link(dve.tensor_copy(brow[:, :], brow_f[:, :]))
            dve.tensor_tensor(brow[32:48, :], brow_f[32:48, :], f32(brow[32:48, :]), ALU.subtract).then_inc(rows_ready, 1)
            dve.wait_ge(resid_in, 16 * 9)
            for t in range(NT):
                ins = dve.tensor_tensor(xres[:, t, :], xres[:, t, :], bob[:, :], ALU.add)
            link(ins)

            def residual(h, t):
                cut = slice(h * CW, (h + 1) * CW)
                link(dve.tensor_tensor(xres[:, t, cut], xres[:, t, cut], B[NT * h + t], ALU.add))
                link(dve.bn_stats(xstat[:, t, h, :], xres[:, t, cut]))

            for t in range(NT):
                if t < NT - 1:
                    dve.wait_ge(proj_ready, t + 1)
                else:
                    dve.wait_ge(chunk_used, 26)
                residual(0, t)
            split_lo(28)
            split_lo(29)
            dve.wait_ge(rows_ready, 1)
            for t in range(NT):
                dve.wait_ge(proj_ready, NT + t)
                residual(1, t)
                dve.bn_aggr(fmv[:, t, 0:2], xstat[:, t, :, :].rearrange("p a b -> p (a b)")).then_inc(mv_ready, 1)
                dve.wait_ge(fr_ready, 2 * t + 1)
                link(dve.tensor_scalar(xf[:, t, :], xres[:, t, :], fmv[:, t, 0:1], fr[:, t, 4:5], ALU.subtract, ALU.mult))
                link(dve.tensor_tensor(xf[:, t, :], xf[:, t, :], lngb[:, :], ALU.mult))
                dve.tensor_tensor(xf[:, t, :], xf[:, t, :], lnbb[:, :], ALU.add).then_inc(xf_ready, 1)
                dve.wait_ge(xf_ready, t + 1)
                for h in range(2):
                    ins = dve.bn_stats(fstat[:, t, h, :], xf[:, t, h * CW:(h + 1) * CW])
                link(ins)
                dve.bn_aggr(fmv[:, t, 2:4], fstat[:, t, :, :].rearrange("p a b -> p (a b)")).then_inc(xf_mv_ready, 1)
                dve.wait_ge(fr_ready, 2 * t + 2)
                dve.wait_ge(xf_turned, t + 1)
                dve.tensor_scalar(xf[:, t, :], xf[:, t, :], fmv[:, t, 2:3], fr[:, t, 6:7], ALU.subtract, ALU.mult).then_inc(z_ready, 1)
                if t < NT - 1:
                    split_lo(30 + t)

            lg, eq, a, oh1, l2, oh2, pos, tmp, posm, over_gate = (r8[:, j, :, :] for j in range(10))
            order, first_row = r8[:, 10, :, :], r8[:, 11, :, :]
            m1, m2, mx = r3[:, 0, :], r3[:, 1, :], r3[:, 2, :]

            def wide(v):
                return v.unsqueeze(2).to_broadcast([P, NT, NE])

            def largest(values, top, onehot):
                link(dve.tensor_reduce(top, values, AX, ALU.max))
                link(dve.tensor_tensor(eq, values, wide(top), ALU.is_equal))
                link(dve.tensor_tensor(a, eq, order, ALU.mult))
                link(dve.tensor_reduce(mx, a, AX, ALU.max))
                link(dve.tensor_tensor(onehot, a, wide(mx), ALU.is_equal))

            dve.wait_ge(ffn_consts, 6)
            dve.wait_ge(logits_ready, NT)
            link(dve.tensor_copy(lg, B[2][:, 0:NT * NE].rearrange("p (t e) -> p t e", t=NT)))
            largest(lg, m1, oh1)
            link(dve.scalar_tensor_tensor(out=l2, in0=oh1, scalar=NEG, in1=lg, op0=ALU.mult, op1=ALU.add))
            largest(l2, m2, oh2)
            dve.tensor_tensor(sel16[:, :, :], oh1, oh2, ALU.add).then_inc(sel_ready, 1)
            dve.tensor_tensor(r3[:, 7, :], m1, m2, ALU.subtract).then_inc(gap_ready, 1)
            dve.wait_ge(sel_ready, 1)
            link(dve.tensor_scalar(tmp, sel16[:, :, :], -1024.0, 1024.0, ALU.mult, ALU.add))
            dve.wait_ge(pos_ready, 1)
            link(dve.tensor_copy(pos, B[0][:, 0:NT * NE].rearrange("p (t e) -> p t e", t=NT)))
            link(dve.tensor_tensor(posm, pos, tmp, ALU.add))
            for e in range(NE):
                for t in range(NT):
                    ins = dve.tensor_scalar(slot_oh[:, e, t, :], slots16[:, :], posm[:, t, e:e + 1], None, ALU.is_equal)
                ins.then_inc(slot_oh_ready, 1)
                if e == 1:
                    dve.wait_ge(tok_summed, 2)
                    dve.tensor_copy(slot_tok[:, 0:2], B[1][:, 0:2]).then_inc(tok_ready, 1)
            for j, oh in enumerate((oh1, oh2)):
                link(dve.tensor_tensor(tmp, oh, pos, ALU.mult))
                link(dve.tensor_reduce(r3[:, 5 + j, :], tmp, AX, ALU.add))
                link(dve.tensor_tensor(tmp, oh, first_row, ALU.mult))
                link(dve.tensor_reduce(r3[:, 3 + j, :], tmp, AX, ALU.add))
                link(dve.scalar_tensor_tensor(out=r3[:, 3 + j, :], in0=r3[:, 5 + j, :], scalar=float(CAP - 1),
                                              in1=r3[:, 3 + j, :], op0=ALU.min, op1=ALU.add))
            dve.tensor_copy(rows_u[:, :, :], r3[:, 3:5, :]).then_inc(rows_u_ready, 1)
            dve.wait_ge(gates_ready, 1)
            dve.wait_ge(rows_u_ready, 1)
            for j, oh in enumerate((oh1, oh2)):
                link(dve.scalar_tensor_tensor(out=r3[:, 3 + j, :], in0=r3[:, 5 + j, :], scalar=float(CAP),
                                              in1=r3[:, 8 + j, :], op0=ALU.is_ge, op1=ALU.mult))
                link(dve.scalar_tensor_tensor(out=r3[:, 8 + j, :], in0=r3[:, 5 + j, :], scalar=float(CAP),
                                              in1=r3[:, 8 + j, :], op0=ALU.is_lt, op1=ALU.mult))
                link(dve.tensor_tensor(over_gate if j == 0 else tmp, oh, wide(r3[:, 3 + j, :]), ALU.mult))
            link(dve.tensor_tensor(over_gate, over_gate, tmp, ALU.add))
            link(dve.tensor_reduce(r3[:, 2, 0:1], B[0][:, NT * NE:(NT + 1) * NE], AX, ALU.max))
            dve.tensor_copy(most[:, :], r3[:, 2, 0:1]).then_inc(most_ready, 1)
            dve.wait_ge(tok_summed, NE)
            dve.tensor_copy(slot_tok[:, 2:NE], B[7][:, 2:NE]).then_inc(tok_ready, 1)
            split_lo(32)

            def tokens_lo(e, par):
                dve.wait_ge(xg_hi_done, e + 1)
                dve.tensor_tensor(xg_lo[:, par, :, :].rearrange("p k n -> p (k n)"), xg[:, par, :],
                                  f32(xg_hi[:, par, :, :]).rearrange("p k n -> p (k n)"), ALU.subtract).then_inc(xg_lo_done, 1)

            def store_y(e, par):
                dve.wait_ge(chunk_used, f0(e + 1) + 6 if e < NE - 1 else CHUNKS)
                if e >= 2:
                    dve.wait_ge(y_stored[par], 16 * (e // 2))
                dve.tensor_scalar(y[:, par, :].rearrange("p (a n) -> p a n", a=2), ps[:, 3:5, :], 10000.0, -10000.0,
                                  ALU.min, ALU.max).then_inc(y_ready, 1)

            tokens_lo(0, 0)
            for e in range(NE):
                nxt = [k if 33 <= k < CHUNKS else None for k in range(f0(e) + 3, f0(e) + 9)]
                if nxt[0]:
                    split_lo(nxt[0])
                dve.wait_ge(chunk_used, up_chunks(e) + 2)
                if e:
                    dve.wait_ge(h_ready, e)
                dve.tensor_scalar(x2c[:, :], B[1], 20.0, -20.0, ALU.min, ALU.max).then_inc(x2_clipped, 1)
                if nxt[1]:
                    split_lo(nxt[1])
                if e + 1 < NE:
                    tokens_lo(e + 1, (e + 1) % 2)
                dve.wait_ge(sig_done, e + 1)
                link(dve.tensor_tensor(sg[:, :], x2c[:, :], sg[:, :], ALU.mult))
                if nxt[2]:
                    split_lo(nxt[2])
                dve.wait_ge(chunk_used, up_chunks(e) + 4)
                if e:
                    dve.wait_ge(h_turned, e)
                link(dve.tensor_tensor(hh[:, :], B[0], sg[:, :], ALU.mult))
                dve.tensor_scalar(hh[:, :], hh[:, :], 10000.0, -10000.0, ALU.min, ALU.max).then_inc(h_ready, 1)
                if nxt[3]:
                    split_lo(nxt[3])
                if e:
                    store_y(e - 1, (e - 1) % 2)
                if nxt[4]:
                    split_lo(nxt[4])
                dve.wait_ge(ht_hi_done, e + 1)
                par = e % 2
                dve.tensor_tensor(ht_lo[:, par, :, :].rearrange("p k n -> p (k n)"), B[2],
                                  f32(ht_hi[:, par, :, :]).rearrange("p k n -> p (k n)"), ALU.subtract).then_inc(ht_lo_done, 1)
                if nxt[5]:
                    split_lo(nxt[5])
            store_y(NE - 1, (NE - 1) % 2)
            with crowded(dve) as e:
                dve.wait_ge(y_stored[0], 16 * NE // 2)
                dve.tensor_copy(fr[:, :, 7:8], over_gate[:, :, bass.ds(e, 1)])
                dve.tensor_copy(selx[:, 0, :], sels[:, bass.ds(e, 1)].to_broadcast([48, P])).then_inc(over_sel, 1)
                dve.wait_ge(over_sel, e + 1)
                for j in range(EXP_CHUNKS):
                    dve.wait_ge(over_w_hi, e * EXP_CHUNKS + (j + 1))
                    dve.tensor_tensor(lo[j][:, :], raw[:, j % RAW, :], f32(hi[j][:, :]), ALU.subtract).then_inc(over_w_lo, 1)
                for t in range(1, NT):
                    step = e * (NT - 1) + t
                    dve.wait_ge(over_hi, step)
                    dve.tensor_tensor(xg_lo[:, 0, :, :].rearrange("p k n -> p (k n)"), xg[:, 0, :],
                                      f32(xg_hi[:, 0, :, :]).rearrange("p k n -> p (k n)"), ALU.subtract).then_inc(over_lo, 1)
                    dve.wait_ge(over_up, step)
                    dve.tensor_scalar(x2c[:, :], B[1], 20.0, -20.0, ALU.min, ALU.max).then_inc(over_clipped, 1)
                    dve.wait_ge(over_sig, step)
                    dve.tensor_tensor(sg[:, :], x2c[:, :], sg[:, :], ALU.mult).then_inc(over_dve, 1)
                    dve.wait_ge(over_dve, e * (3 * (NT - 1)) + (3 * t - 2))
                    dve.tensor_tensor(hh[:, :], B[0], sg[:, :], ALU.mult).then_inc(over_dve, 1)
                    dve.wait_ge(over_dve, e * (3 * (NT - 1)) + (3 * t - 1))
                    dve.tensor_scalar(hh[:, :], hh[:, :], 10000.0, -10000.0, ALU.min, ALU.max).then_inc(over_h, 1)
                    dve.wait_ge(over_h_hi, step)
                    dve.tensor_tensor(ht_lo[:, 0, :, :].rearrange("p k n -> p (k n)"), B[2],
                                      f32(ht_hi[:, 0, :, :]).rearrange("p k n -> p (k n)"), ALU.subtract).then_inc(over_h_lo, 1)
                    dve.wait_ge(over_down, step)
                    dve.tensor_scalar(y[:, 0, :].rearrange("p (a n) -> p a n", a=2), ps[:, 3:5, :], 10000.0, -10000.0,
                                      ALU.min, ALU.max).then_inc(over_dve, 1)
                    dve.wait_ge(over_dve, e * (3 * (NT - 1)) + 3 * t)
                    dve.scalar_tensor_tensor(out=xres[:, t, :], in0=y[:, 0, :], scalar=fr[:, t, 7:8],
                                             in1=xres[:, t, :], op0=ALU.mult, op1=ALU.add).then_inc(over_added, 1)
                    dve.wait_ge(over_added, step)
            dve.wait_ge(gates_ready, 1)
            for t in range(NT):
                for j in range(2):
                    dve.wait_ge(y_rows_in[2 * t + j], 16)
                    ins = dve.scalar_tensor_tensor(out=xres[:, t, :], in0=yg[:, 2 * t + j, :], scalar=r3[:, 8 + j, t:t + 1],
                                                   in1=xres[:, t, :], op0=ALU.mult, op1=ALU.add)
                    if j == 0:
                        link(ins)
                ins.then_inc(out_ready, 1)

        @block.tensor
        def _(pe):
            def three(o, a, b, first, last):
                for n, (s, m) in enumerate(((0, 0), (0, 1), (1, 0))):
                    ins = pe.matmul(o, a[s], b[m], start=first and n == 0, stop=last and n == 2)
                return ins

            pe.wait_ge(consts_ready, 2)
            for t in range(NT):
                pe.wait_ge(normed, t + 1)
                for k in range(KT):
                    ins = pe.transpose(B[2 * t + k // 4][:, (k % 4) * P:(k % 4 + 1) * P], xin[:, t, k * P:(k + 1) * P], ident[:, :])
                ins.then_inc(x_turned, 1)

            def weight(c, k, cut=slice(0, CW)):
                w = slice(k * CW + cut.start, k * CW + cut.stop)
                return hi[SLOT[c]][:, w], lo[SLOT[c]][:, w]

            def half(i):
                m, h = HALVES[i]
                group = OF_HALF[i]
                if group >= 2:
                    pe.wait_ge(group_evacuated, group - 1)
                for part in range(2):
                    c = 2 * i + part
                    pe.wait_ge(lo_done, c + 1)
                    if NAMES[m][1] == "2":
                        pe.wait_ge(group_evacuated, OF_HALF[2 * (m - 1) + part] + 1)
                    act_hi, act_lo = (t_hi, t_lo) if NAMES[m][1] == "2" else (xt_hi, xt_lo)
                    for kk in range(CK):
                        k = CK * part + kk
                        if NAMES[m] == "v2":
                            for t in range(NT):
                                tok = slice(t * P, (t + 1) * P)
                                ins = three(banks(group)[t][:, :], (act_hi[:, k, tok], act_lo[:, k, tok]), weight(c, kk),
                                            k == 0, k == KT - 1)
                        else:
                            for b in range(4):
                                ins = three(banks(group)[b][:, 0:N], weight(c, kk, slice(b * P, (b + 1) * P)),
                                            (act_hi[:, k, :], act_lo[:, k, :]), k == 0, k == KT - 1)
                    ins.then_inc(chunk_used, 1)

            def mask():
                if MASK_GROUP >= 2:
                    pe.wait_ge(group_evacuated, MASK_GROUP - 1)
                bk = banks(MASK_GROUP)
                for g in range(EG):
                    pe.wait_ge(onehots, g + 2)
                    for t in range(NT):
                        ins = pe.matmul(bk[t][:, 0:N], s_oh[:, g % OH, t * P:(t + 1) * P], d_oh[:, g % OH, :],
                                        start=g == 0, stop=False)
                    ins.then_inc(onehots_used, 1)
                for t in range(NT):
                    ins = pe.matmul(bk[t][:, t * P:(t + 1) * P], idb[:, :], dgb[:, :], start=False, stop=True)
                ins.then_inc(mask_summed, 1)

            def scores(h):
                rows = slice(HD * (h % 2), HD * (h % 2) + HD)
                for i in range(NT):
                    if h > 0:
                        pe.wait_ge(score_max, 3 * (h - 1) + i + 1)
                    tok = slice(i * P, (i + 1) * P)
                    three(B[i][:, 0:N], (q_hi[rows, h // 2, tok], q_lo[rows, h // 2, tok]),
                          (k_hi[rows, h // 2, :], k_lo[rows, h // 2, :]), True, True).then_inc(score_ready, 1)

            def turn(h):
                pe.wait_ge(normalised, 3 * h + 3)
                for j in range(NT):
                    if h > 0:
                        pe.wait_ge(at_lo_done, 3 * (h - 1) + j + 1)
                    for i in range(NT):
                        ins = pe.transpose(B[3 + j][:, i * P:(i + 1) * P], pr[:, h % 2, i, j * P:(j + 1) * P], ident[:, :])
                    ins.then_inc(p_turned, 1)

            def attend(h):
                if h >= 2:
                    pe.wait_ge(o_lo_done, h - 1)
                pair = slice((h // 2) * P, (h // 2 + 1) * P)
                for j in range(NT):
                    pe.wait_ge(at_lo_done, 3 * h + j + 1)
                    ins = three(B[6 + h % 2][:, 0:N], (v_hi[:, j, pair], v_lo[:, j, pair]),
                                (at_hi[:, h % 2, j, :], at_lo[:, h % 2, j, :]), j == 0, j == NT - 1)
                ins.then_inc(o_ready, 1)

            for i in range(12):
                if i == MASK_GROUP:
                    mask()
                if i == 0:
                    pe.wait_ge(x_lo, 2 * NT)
                half(i)
            pe.wait_ge(group_evacuated, 13)
            for s in range(HEADS + 2):
                if s < HEADS:
                    scores(s)
                if 1 <= s <= HEADS:
                    turn(s - 1)
                if s >= 2:
                    attend(s - 2)
            for part in range(2):
                c = 24 + part
                pe.wait_ge(lo_done, c + 1)
                for kk in range(CK):
                    k = CK * part + kk
                    pe.wait_ge(o_lo_done, 2 * k + 2)
                    for t in range(NT):
                        tok = slice(t * P, (t + 1) * P)
                        ins = three(B[t][:, :], (t_hi[:, k, tok], t_lo[:, k, tok]), weight(c, kk), k == 0, k == KT - 1)
                        if k == KT - 1 and t < NT - 1:
                            ins.then_inc(proj_ready, 1)
                if part == 0:
                    ins.then_inc(chunk_used, 1)
            ins.then_inc(chunk_used, 1)
            def router(t):
                a = 6 if t % 2 == 0 else 0
                pe.wait_ge(xf_ready, t + 1)
                if t == 2:
                    pe.wait_ge(xft_ready, 1)
                for k in range(KT):
                    ins = pe.transpose(B[a + k // 4][:, (k % 4) * P:(k % 4 + 1) * P], xf[:, t, k * P:(k + 1) * P], ident[:, :])
                    if t == NT - 1 and k == 0:
                        ins.then_inc(chunk_used, 1)
                ins.then_inc(xf_turned, 1)
                pe.wait_ge(xft_ready, t + 1)
                for k in range(KT):
                    ins = pe.matmul(B[2][:, t * NE:(t + 1) * NE], xft[:, k, :], rws[:, k, :], start=k == 0, stop=k == KT - 1)
                ins.then_inc(logits_ready, 1)

            pe.wait_ge(lo_done, GNN_CHUNKS)
            for t in range(NT):
                tok = slice(t * P, (t + 1) * P)
                for k in range(KT):
                    ins = three(B[3 + t][:, :], (t_hi[:, k, tok], t_lo[:, k, tok]), weight(26 + k // CK, k % CK), k == 0, k == KT - 1)
                    if t == NT - 1 and k == CK - 1:
                        ins.then_inc(chunk_used, 1)
                ins.then_inc(proj_ready, 1)
                if t:
                    router(t - 1)
            router(NT - 1)
            pe.wait_ge(sel_ready, 1)
            pe.wait_ge(ffn_consts, 6)
            for t in range(NT):
                for j in range(t + 1):
                    ins = pe.matmul(B[0][:, t * NE:(t + 1) * NE], ones16[:, :] if j < t else later16[:, :], sel16[:, j, :],
                                    start=j == 0, stop=j == t)
            for j in range(NT):
                ins = pe.matmul(B[0][:, NT * NE:(NT + 1) * NE], ones16[:, :], sel16[:, j, :], start=j == 0, stop=j == NT - 1)
            ins.then_inc(pos_ready, 1)
            for e in range(NE):
                pe.wait_ge(slot_oh_ready, e + 1)
                bank = B[1] if e < 2 else B[7]
                for t in range(NT):
                    ins = pe.matmul(bank[:, e:e + 1], slot_oh[:, e, t, :], tok16[:, t:t + 1], start=t == 0, stop=t == NT - 1)
                ins.then_inc(tok_summed, 1)

            def turn_tokens(e, par):
                pe.wait_ge(gathered[par], 16 * (e // 2 + 1))
                if e:
                    pe.wait_ge(xg_scaled, e)
                for k in range(KT):
                    ins = pe.transpose(B[5 + k // 4][:, (k % 4) * P:(k % 4 + 1) * P], xg[:, par, k * P:(k + 1) * P], ident[:, :])
                ins.then_inc(xg_turned, 1)

            def up(bank, e, par, c, cols):
                pe.matmul(bank, selx[0:40, par, :], brow[0:40, cols], start=True, stop=False)
                for part in range(2):
                    pe.wait_ge(lo_done, c + part + 1)
                    for kk in range(CK):
                        k = CK * part + kk
                        ins = three(bank, (xg_hi[:, par, k, :], xg_lo[:, par, k, :]), weight(c + part, kk), False, k == KT - 1)
                    ins.then_inc(chunk_used, 1)

            def down(e, par, c):
                pe.wait_ge(ht_lo_done, e + 1)
                if e:
                    pe.wait_ge(y_ready, e)
                for part in range(2):
                    cols = slice(D + part * CW, D + (part + 1) * CW)
                    pe.matmul(B[3 + part], selx[0:40, par, :], brow[0:40, cols], start=True, stop=False)
                for part in range(2):
                    pe.wait_ge(lo_done, c + part + 1)
                    for k in range(HT):
                        ins = three(B[3 + part], (ht_hi[:, par, k, :], ht_lo[:, par, k, :]), weight(c + part, k), False, k == HT - 1)
                    ins.then_inc(chunk_used, 1)

            def turn_hidden(e):
                pe.wait_ge(h_ready, e + 1)
                if e:
                    pe.wait_ge(ht_lo_done, e)
                for k in range(HT):
                    ins = pe.transpose(B[2][:, k * P:(k + 1) * P], hh[:, k * P:(k + 1) * P], ident[:, :])
                ins.then_inc(h_turned, 1)

            turn_tokens(0, 0)
            pe.wait_ge(rows_ready, 1)
            for e in range(NE):
                par = e % 2
                c = up_chunks(e)
                pe.wait_ge(xg_lo_done, e + 1)
                pe.wait_ge(sel_set, e + 1)
                if e:
                    pe.wait_ge(x2_clipped, e)
                up(B[1], e, par, c, slice(CW, 2 * CW))
                if e + 1 < NE:
                    turn_tokens(e + 1, 1 - par)
                if e:
                    pe.wait_ge(h_ready, e)
                up(B[0], e, par, c + 2, slice(0, CW))
                if e:
                    down(e - 1, 1 - par, c + 4)
                turn_hidden(e)
            down(NE - 1, 1, CHUNKS - 2)

            def over_sum(bank, act_hi, act_lo, tiles, chunk0, bias_cols):
                pe.matmul(bank, selx[0:40, 0, :], brow[0:40, bias_cols], start=True, stop=False)
                for k in range(tiles):
                    s, w = chunk0 + k // CK, slice(k % CK * CW, (k % CK + 1) * CW)
                    ins = three(bank, (act_hi[:, 0, k, :], act_lo[:, 0, k, :]), (hi[s][:, w], lo[s][:, w]), False, k == tiles - 1)
                return ins

            pe.wait_ge(y_ready, NE)
            pe.sem_inc(over_expert, 1)
            with crowded(pe) as e:
                pe.wait_ge(over_sel, e + 1)
                pe.wait_ge(over_w_lo, e * EXP_CHUNKS + EXP_CHUNKS)
                for t in range(1, NT):
                    step = e * (NT - 1) + t
                    if t > 1:
                        pe.wait_ge(over_added, e * (NT - 1) + (t - 1))
                    pe.wait_ge(over_z_in, (e * (NT - 1) + t) * 16)
                    for k in range(KT):
                        ins = pe.transpose(B[5 + k // 4][:, (k % 4) * P:(k % 4 + 1) * P], xg[:, 1, k * P:(k + 1) * P], ident[:, :])
                    ins.then_inc(over_turned, 1)
                    pe.wait_ge(over_lo, step)
                    over_sum(B[1], xg_hi, xg_lo, KT, 0, slice(CW, 2 * CW))
                    over_sum(B[0], xg_hi, xg_lo, KT, 2, slice(0, CW)).then_inc(over_up, 1)
                    pe.wait_ge(over_h, step)
                    for k in range(HT):
                        ins = pe.transpose(B[2][:, k * P:(k + 1) * P], hh[:, k * P:(k + 1) * P], ident[:, :])
                    ins.then_inc(over_h_turned, 1)
                    pe.wait_ge(over_h_lo, step)
                    over_sum(B[3], ht_hi, ht_lo, HT, 4, slice(D, D + CW))
                    over_sum(B[4], ht_hi, ht_lo, HT, 5, slice(D + CW, 2 * D)).then_inc(over_down, 1)
                pe.wait_ge(over_added, e * (NT - 1) + (NT - 1))
                pe.sem_inc(over_expert, 1)
            pe.sem_inc(over_done, 1)


_INS = ["x", "src", "dst", "ety", "srcb", "dstb", "ew", "wg", "bcols", "bo", "lng", "lnb", "rw", "egc", "ebc", "wf", "b1", "b2", "be"]


def layouts(i):
    c = np.ascontiguousarray
    f = {k: np.asarray(v) for k, v in i.items()}
    g = "L0_gnn_"

    def chunks(w):
        n = w.shape[1] // CW
        return w.reshape(-1, CK, P, n, CW).transpose(3, 0, 2, 1, 4).reshape(n, -1, P, CE)

    wg = np.concatenate([chunks(f[g + n].T).reshape(4, P, CE) for n in ("wv", "wiv", "wk", "wik", "wq", "wiq", "wo")])
    u = "L0_ffn_"
    wf = np.stack([np.concatenate([chunks(f[u + "W2"][e]).reshape(2, P, CE), chunks(f[u + "W1"][e]).reshape(2, P, CE),
                                   chunks(f[u + "Wo"][e]).reshape(2, P, CE)]) for e in range(NE)])

    def edge(a):
        return c(a.reshape(EG, P).T)

    return {
        "x": c(f["x"]), "src": edge(f["src"]), "dst": edge(f["dst"]), "ety": edge(f["edge_type_5"]),
        "srcb": c(f["src"]), "dstb": c(f["dst"]), "ew": c(f[g + "edge_type_weights"]), "wg": c(wg),
        "bcols": c(np.stack([f[g + n].reshape(KT, P).T for n in ("bv", "biv", "bk", "bik", "bq", "biq")], 1)),
        "bo": c(f[g + "bo"]), "lng": c(f[u + "ln_g"]), "lnb": c(f[u + "ln_b"]),
        "rw": c(f[u + "router_w"].reshape(KT, P, NE).transpose(1, 0, 2)),
        "egc": c(f[u + "eg"].reshape(NE, KT, P).transpose(2, 0, 1)), "ebc": c(f[u + "eb"].reshape(NE, KT, P).transpose(2, 0, 1)),
        "wf": c(wf), "b1": c(f[u + "b1"]), "b2": c(f[u + "b2"]), "be": c(f[u + "bo"]),
    }


def kernel(**inputs):
    import concourse.bacc as bacc
    from concourse.bass_utils import run_bass_kernel_spmd

    nc = bacc.Bacc("TRN2", target_bir_lowering=False, num_devices=1)
    arrays = layouts(inputs)
    args = [nc.dram_tensor(f"in_{n}", arrays[n].shape, mybir.dt.from_np(arrays[n].dtype), kind="ExternalInput").ap() for n in _INS]
    out = nc.dram_tensor("out_0", (N, D), F32, kind="ExternalOutput").ap()
    gnn_ffn(nc, *args, out)
    r = run_bass_kernel_spmd(nc, [{f"in_{n}": arrays[n] for n in _INS}], core_ids=[0])
    return r.results[0]["out_0"]
```

```python
from contextlib import ExitStack, contextmanager

import numpy as np

import concourse.bass as bass
from concourse import mybir
from concourse.alu_op_type import AluOpType as ALU

F32 = mybir.dt.float32
F32R = mybir.dt.float32r
F16 = mybir.dt.float16
BF16 = mybir.dt.bfloat16
I32 = mybir.dt.int32
U32 = mybir.dt.uint32
ACT = mybir.ActivationFunctionType
AX = mybir.AxisListType.X

P = 128
N = 384
NT = N // P
D = 1024
KT = D // P
HEADS = 16
HD = D // HEADS
EDGES = 6144
EG = EDGES // P
NE = 8
HF = 512
HT = HF // P
EPS = 1e-5
NEG = -1e30
BIG = 3.0e38
CK = 4
CW = 512
CE = CK * CW
GNN_CHUNKS = 7 * 4
EXP_CHUNKS = 6
CAP = P
RAW = 3
WIN = 2
PIECE = 12


def expert_order():
    order = []
    for e in range(NE + 1):
        if e < NE:
            order += [(e, 0), (e, 1), (e, 2), (e, 3)]
        if e > 0:
            order += [(e - 1, 4), (e - 1, 5)]
    return order


EXPERT_ORDER = expert_order()
CHUNKS = GNN_CHUNKS + len(EXPERT_ORDER)
SLOT = [c % 3 for c in range(GNN_CHUNKS - 1)] + [5] + [(3, 4, 0, 1, 2, 5)[j % 6] for j in range(len(EXPERT_ORDER))]


def before(c):
    return max((p + 1 for p in range(c) if SLOT[p] == SLOT[c]), default=0)


def gnn_ffn(nc, x, src, dst, ety, srcb, dstb, ew, wg, bcols, bo, lng, lnb, rw, egc, ebc, wf, b1, b2, be, out):
    ctx = ExitStack()
    with ctx:
        def sem(name):
            return ctx.enter_context(nc.semaphore(name))

        def psum(name, shape, dt=F32):
            return ctx.enter_context(nc.psum_tensor(name, shape, dt))

        def sb(stack, name, shape, dt):
            return stack.enter_context(nc.sbuf_tensor(name, shape, dt))

        raw = sb(ctx, "raw", [P, RAW, CE], F32)
        hi = [sb(ctx, f"hi{s}", [P, CE], F32R) for s in range(3)]
        lo = [sb(ctx, f"lo{s}", [P, CE], F32R) for s in range(3)]
        ident = sb(ctx, "ident", [P, P], F32)
        small = sb(ctx, "small", [P, 70], F32)
        gbias = sb(ctx, "gbias", [P, 6, KT], F32)

        gnn = ExitStack()
        with gnn:
            xt_hi = sb(gnn, "xt_hi", [P, KT, N], F32R)
            xt_lo = sb(gnn, "xt_lo", [P, KT, N], F32R)
            t_hi = sb(gnn, "t_hi", [P, KT, N], F32R)
            t_lo = sb(gnn, "t_lo", [P, KT, N], F32R)
            v_hi = sb(gnn, "v_hi", [P, NT, D], F32R)
            v_lo = sb(gnn, "v_lo", [P, NT, D], F32R)
            mask8 = sb(gnn, "mask8", [P, NT, N], F32)
            with ExitStack() as early:
                xin = sb(early, "xin", [P, NT, D], F32)
                src_i = sb(early, "src_i", [P, 2, PIECE * P], I32)
                dst_i = sb(early, "dst_i", [P, 2, PIECE * P], I32)
                keyb = sb(early, "keyb", [P, PIECE * P], F32)
                eqt = sb(early, "eqt", [P, 2, WIN * P], F32)
            k_hi = sb(gnn, "k_hi", [P, KT, N], F32R)
            k_lo = sb(gnn, "k_lo", [P, KT, N], F32R)
            pr = sb(gnn, "pr", [P, 2, NT, N], F32)
            at_hi = sb(gnn, "at_hi", [P, 2, NT, N], F32R)
            at_lo = sb(gnn, "at_lo", [P, 2, NT, N], F32R)
            cols = sb(gnn, "cols", [P, 3, EG], I32)
            colf = sb(gnn, "colf", [P, 6, EG], F32)
            wterm = sb(gnn, "wterm", [P, 4, EG], F32)
            bits = sb(gnn, "bits", [P, 2, EG], I32)
            dump = sb(gnn, "dump", [P, EG], F32)
            later = sb(gnn, "later", [P, WIN * P], F32)
            ewb = sb(gnn, "ewb", [P, 4, 4], F32)
        q_hi, q_lo = xt_hi, xt_lo

        with ExitStack() as ffn:
            xres = sb(ffn, "xres", [P, NT, D], F32)
            lngb = sb(ffn, "lngb", [P, D], F32)
            lnbb = sb(ffn, "lnbb", [P, D], F32)
            bob = sb(ffn, "bob", [P, D], F32)
            with ExitStack() as last:
                yg = sb(last, "yg", [P, 2 * NT, D], F32)
            xg = sb(ffn, "xg", [P, 2, D], F32)
            xg_hi = sb(ffn, "xg_hi", [P, 2, KT, P], F32R)
            xg_lo = sb(ffn, "xg_lo", [P, 2, KT, P], F32R)
            for s in (3, 4, 5):
                hi.append(sb(ffn, f"hi{s}", [P, CE], F32R))
                lo.append(sb(ffn, f"lo{s}", [P, CE], F32R))
            with ExitStack() as rowbuild:
                brow_f = sb(rowbuild, "brow_f", [48, 2 * D], F32)
            with ExitStack() as experts:
                y = sb(experts, "y", [P, 2, D], F32)
            xf = sb(ffn, "xf", [P, NT, D], F32)
            brow = sb(ffn, "brow", [48, 2 * D], F32R)
            with ExitStack() as router:
                xft = sb(router, "xft", [P, KT, P], F32)
            x2c = sb(ffn, "x2c", [P, CW], F32)
            sg = sb(ffn, "sg", [P, CW], F32)
            hh = sb(ffn, "hh", [P, CW], F32)
            with ExitStack() as router2:
                slot_oh = sb(router2, "slot_oh", [P, NE, NT, P], F16)
            ht_hi = sb(ffn, "ht_hi", [P, 2, HT, P], F32R)
            ht_lo = sb(ffn, "ht_lo", [P, 2, HT, P], F32R)
            rws = sb(ffn, "rws", [P, KT, NE], F32)
            egb = sb(ffn, "egb", [P, 2, NE, KT], F32)
            sels = sb(ffn, "sels", [48, NE], F32)
            selx = sb(ffn, "selx", [48, 2, P], F32R)
            r8 = sb(ffn, "r8", [P, 12, NT, NE], F32)
            r3 = sb(ffn, "r3", [P, 10, NT], F32)
            sel16 = sb(ffn, "sel16", [P, NT, NE], F16)
            ones16 = sb(ffn, "ones16", [P, P], F16)
            later16 = sb(ffn, "later16", [P, P], F16)
            slots16 = sb(ffn, "slots16", [P, P], F16)
            tok16 = sb(ffn, "tok16", [P, NT], F16)
            slot_tok = sb(ffn, "slot_tok", [P, NE], U32)
            most = sb(ffn, "most", [P, 1], I32)
            over_cols = sb(ffn, "over_cols", [P, 2, KT], F32)
            rows_u = sb(ffn, "rows_u", [P, 2, NT], U32)
            fstat = sb(ffn, "fstat", [P, NT, 2, 6], F32)
            xstat = sb(ffn, "xstat", [P, NT, 2, 6], F32)
            fmv = sb(ffn, "fmv", [P, NT, 4], F32)
            fr = sb(ffn, "fr", [P, NT, 8], F32)
        zbuf = nc.dram_tensor("z_rows", (N, D), F32, kind="Internal").ap()
        ybuf = nc.dram_tensor("y_rows", (NE * CAP, D), F32, kind="Internal").ap()

        mbuf = nc.dram_tensor("mask_rows", (N * N + WIN * P, 1), F32, kind="Internal").ap()
        mask_rows = mbuf[0:N * N, :].rearrange("(t p j) o -> p t (j o)", t=NT, p=P)

        ps = psum("ps", [P, 8, CW])
        B = [ps[:, i, :] for i in range(8)]

        raw_ready = [sem(f"raw_ready{s}") for s in range(RAW)]
        hi_done, lo_done, chunk_used = sem("hi_done"), sem("lo_done"), sem("chunk_used")
        x_in = [sem(f"x_in{t}") for t in range(NT)]
        edges_in, bias_in, keys_in = sem("edges_in"), sem("bias_in"), [sem("keys_in0"), sem("keys_in1")]
        consts_ready = sem("consts_ready")
        stats_ready, rstd_ready, pool_chain = sem("stats_ready"), sem("rstd_ready"), sem("pool_chain")
        normed, x_turned, x_hi, x_lo = sem("normed"), sem("x_turned"), sem("x_hi"), sem("x_lo")
        dve_chain, act_chain = sem("dve_chain"), sem("act_chain")
        bank_hi, group_evacuated = sem("bank_hi"), sem("group_evacuated")
        types_ready, base_filled, base_ready, base_stored = sem("types_ready"), sem("base_filled"), sem("base_ready"), sem("base_stored")
        places_ready, scattered, mask_in = sem("places_ready"), sem("scattered"), sem("mask_in")
        score_ready, score_max, exp_done, normalised = (
            sem("score_ready"), sem("score_max"), sem("exp_done"), sem("normalised"))
        first_inverse, first_normalised = sem("first_inverse"), sem("first_normalised")
        p_turned, at_hi_done, at_lo_done = sem("p_turned"), sem("at_hi_done"), sem("at_lo_done")
        o_ready, o_hi_done, o_lo_done = sem("o_ready"), sem("o_hi_done"), sem("o_lo_done")
        proj_ready, resid_in = sem("proj_ready"), sem("resid_in")
        stored = sem("stored")
        ffn_in, rows_in, ffn_consts, rows_ready = sem("ffn_in"), sem("rows_in"), sem("ffn_consts"), sem("rows_ready")
        resid_ready, var_ready, xf_ready, fr_ready, z_ready = sem("resid_ready"), sem("var_ready"), sem("xf_ready"), sem("fr_ready"), sem("z_ready")
        xf_turned, xft_ready, logits_ready, z_stored = sem("xf_turned"), sem("xft_ready"), sem("logits_ready"), sem("z_stored")
        gap_ready, gates_ready, sel_ready, pos_ready = sem("gap_ready"), sem("gates_ready"), sem("sel_ready"), sem("pos_ready")
        slot_oh_ready, tok_summed, tok_ready, rows_u_ready = sem("slot_oh_ready"), sem("tok_summed"), sem("tok_ready"), sem("rows_u_ready")
        gathered, sel_set = [sem("gathered0"), sem("gathered1")], sem("sel_set")
        xg_turned, xg_scaled, xg_hi_done, xg_lo_done = sem("xg_turned"), sem("xg_scaled"), sem("xg_hi_done"), sem("xg_lo_done")
        x2_clipped, sig_done, h_ready, h_turned, ht_hi_done, ht_lo_done = (
            sem("x2_clipped"), sem("sig_done"), sem("h_ready"), sem("h_turned"), sem("ht_hi_done"), sem("ht_lo_done"))
        x1_used, y_ready, y_stored = sem("x1_used"), sem("y_ready"), [sem("y_stored0"), sem("y_stored1")]
        y_rows_in = [sem(f"y_rows_in{j}") for j in range(2 * NT)]
        out_ready = sem("out_ready")
        most_ready, over_raw, over_cols_in = sem("most_ready"), [sem(f"over_raw{s}") for s in range(RAW)], sem("over_cols_in")
        over_w_hi, over_w_lo, over_expert, over_z_in = sem("over_w_hi"), sem("over_w_lo"), sem("over_expert"), sem("over_z_in")
        over_sel, over_turned, over_hi, over_lo = sem("over_sel"), sem("over_turned"), sem("over_hi"), sem("over_lo")
        over_up, over_clipped, over_sig, over_h = sem("over_up"), sem("over_clipped"), sem("over_sig"), sem("over_h")
        over_scaled, over_done, over_h_turned, over_h_hi, over_h_lo, over_down, over_added = (
            sem("over_scaled"), sem("over_done"), sem("over_h_turned"), sem("over_h_hi"), sem("over_h_lo"), sem("over_down"), sem("over_added"))
        over_dve = sem("over_dve")

        def f0(e):
            return GNN_CHUNKS + 6 * e - 2

        def up_chunks(e):
            return f0(e) + (2 if e == 0 else 0)

        stat = small[:, 0:36].rearrange("p (t k) -> p t k", t=NT)
        mv = small[:, 36:42].rearrange("p (t k) -> p t k", t=NT)
        rs = small[:, 42:48]
        halfneg = small[:, 48:49]
        negmax = small[:, 52:58].rearrange("p (b i) -> p b i", b=2)
        rsum = small[:, 58:64].rearrange("p (b i) -> p b i", b=2)

        rinv = small[:, 64:70].rearrange("p (b i) -> p b i", b=2)

        SCALE8 = 1.0 / 8.0

        HALVES = [(m, h) for m in range(6) for h in range(2)]
        NAMES = ["v1", "v2", "k1", "k2", "q1", "q2"]

        def banks(group):
            return B[0:4] if group % 2 == 0 else B[4:8]

        def f32(ap):
            return ap.bitcast(F32)

        @contextmanager
        def crowded(engine):
            engine.wait_ge(most_ready, 1)
            tokens = engine.value_load(most[0:1, 0:1])
            with engine.If(tokens > CAP):
                with engine.Fori(0, NE) as e:
                    yield e

        block = ctx.enter_context(nc.Block())

        @block.sync
        def _(sp):
            xv = x.rearrange("(t p) d -> p t d", p=P)
            for t in range(NT):
                sp.dma_start(xin[:, t, :], xv[:, t, :]).then_inc(x_in[t], 16)

            def load(c):
                if c >= RAW:
                    sp.wait_ge(lo_done, c - RAW + 1)
                srcw = wg[c] if c < GNN_CHUNKS else wf[EXPERT_ORDER[c - GNN_CHUNKS][0], EXPERT_ORDER[c - GNN_CHUNKS][1]]
                sp.dma_start(raw[:, c % RAW, :], srcw).then_inc(raw_ready[c % RAW], 16)

            for c in range(30):
                load(c)
                if c == 3:
                    sp.wait_ge(base_ready, 1)
                    sp.dma_start(mask_rows, mask8[:, :, :]).then_inc(base_stored, 16)
            sp.wait_ge(score_ready, NT * HEADS)
            for t in range(NT):
                sp.dma_start(xres[:, t, :], xv[:, t, :]).then_inc(resid_in, 16)
            for a, b in ((bob, bo), (lngb, lng), (lnbb, lnb)):
                sp.dma_start(a[:, :], b.partition_broadcast(P)).then_inc(resid_in, 16)
            sp.wait_ge(o_ready, HEADS)
            sp.wait_ge(rows_in, 1)
            for r in (0, 32):
                for a, cut in ((b1, slice(0, CW)), (b2, slice(CW, 2 * CW)), (be, slice(D, 2 * D))):
                    sp.dma_start(brow_f[r:r + NE, cut], a).then_inc(ffn_in, 16)
            for a, b in ((rws[:, :, :], rw), (egb[:, 0, :, :], egc), (egb[:, 1, :, :], ebc)):
                sp.dma_start(a, b).then_inc(ffn_in, 16)
            for c in range(30, 33):
                load(c)
            for t in range(NT):
                sp.wait_ge(z_ready, t + 1)
                sp.dma_start(zbuf[t * P:(t + 1) * P, :], xf[:, t, :]).then_inc(z_stored, 16)
                load(33 + t)

            def y_store(e, par):
                sp.wait_ge(y_ready, e + 1)
                sp.dma_start(ybuf[e * CAP:(e + 1) * CAP, :], y[:, par, :]).then_inc(y_stored[par], 16)

            for c in range(36, CHUNKS):
                if c >= f0(2) + 4 and (c - f0(2) - 4) % 6 == 0:
                    e = (c - f0(2) - 4) // 6
                    y_store(e, e % 2)
                load(c)
            done = (CHUNKS - 1 - f0(2) - 4) // 6 + 1
            for e in range(done, NE):
                y_store(e, e % 2)
            with crowded(sp) as e:
                sp.wait_ge(over_expert, e + 1)
                for j in range(EXP_CHUNKS):
                    if j >= RAW:
                        sp.wait_ge(over_w_lo, e * EXP_CHUNKS + (j - RAW + 1))
                    sp.dma_start(raw[:, j % RAW, :], wf[bass.ds(e, 1), j].rearrange("o p c -> (o p) c")).then_inc(over_raw[j % RAW], 16)
                for j, a in enumerate((egc, ebc)):
                    sp.dma_start(over_cols[:, j, :], a[:, bass.ds(e, 1), :].rearrange("p o k -> p (o k)")).then_inc(over_cols_in, 16)
                for t in range(1, NT):
                    if t > 1:
                        sp.wait_ge(over_turned, e * (NT - 1) + (t - 1))
                    sp.dma_start(xg[:, 1, :], zbuf[t * P:(t + 1) * P, :]).then_inc(over_z_in, 16)
            for t in range(NT):
                sp.wait_ge(out_ready, t + 1)
                sp.dma_start(out[t * P:(t + 1) * P, :], xres[:, t, :]).then_inc(stored, 16)
            sp.wait_ge(stored, 16 * NT)

        @block.gpsimd
        def _(pool):
            chain = [0]

            def link(ins):
                chain[0] += 1
                ins.then_inc(pool_chain, 1)
                pool.wait_ge(pool_chain, chain[0])

            pool.memset(halfneg, -0.5).then_inc(consts_ready, 1)
            link(pool.memset(ident[:, :], 0.0))
            pool.affine_select(out=ident[:, :], in_=ident[:, :], compare_op=ALU.not_equal, fill=1.0, base=0,
                               pattern=[[-1, P]], channel_multiplier=1).then_inc(consts_ready, 1)
            link(pool.memset(later[:, :], 1.0))
            pool.affine_select(out=later[:, :], in_=later[:, :], compare_op=ALU.is_gt, fill=0.0, base=0,
                               pattern=[[1, WIN * P]], channel_multiplier=-1).then_inc(consts_ready, 1)
            pool.iota(dump[:, :].rearrange("p (g w) -> p g w", w=WIN), pattern=[[0, EG // WIN], [P, WIN]], base=N * N, channel_multiplier=1,
                      allow_small_or_imprecise_dtypes=True).then_inc(consts_ready, 1)
            for t in range(NT):
                pool.wait_ge(stats_ready, t + 1)
                link(pool.tensor_scalar(rs[:, t:t + 1], mv[:, t, 1:2], EPS, None, ALU.add))
                pool.tensor_tensor(rs[:, 3 + t:4 + t], rs[:, t:t + 1], halfneg, ALU.pow).then_inc(rstd_ready, 1)
            link(pool.memset(mask8[:, :, :], NEG))
            for t in range(NT):
                pool.affine_select(out=mask8[:, t, t * P:(t + 1) * P], in_=mask8[:, t, t * P:(t + 1) * P], compare_op=ALU.not_equal,
                                   fill=0.0, base=0, pattern=[[-1, P]], channel_multiplier=1).then_inc(base_filled, 1)
            pool.wait_ge(base_stored, 16)
            for g in range(EG):
                pool.wait_ge(places_ready, g // PIECE + 1)
                if g and g % WIN == 0:
                    pool.wait_ge(scattered, 16 * g)
                pool.indirect_dma_start(out=mbuf[:, :], out_offset=bass.IndirectOffsetOnAxis(ap=bits[:, 1, g:g + 1], axis=0),
                                        in_=colf[:, 5, g:g + 1], in_offset=None).then_inc(scattered, 16)
            pool.wait_ge(scattered, 16 * EG)
            pool.dma_start(mask8[:, :, :], mask_rows).then_inc(mask_in, 16)

            for h in range(HEADS):
                pool.wait_ge(first_inverse, h + 1)
                pool.tensor_scalar(pr[:, h % 2, 0, :], pr[:, h % 2, 0, :], rinv[:, h % 2, 0:1], None,
                                   ALU.mult).then_inc(first_normalised, 1)

            pool.wait_ge(o_ready, HEADS)
            pool.memset(brow_f[:, :], 0.0).then_inc(rows_in, 1)
            link(pool.memset(sels[:, :], 0.0))
            for base in (0, -32):
                link(pool.affine_select(out=sels[:, :], in_=sels[:, :], compare_op=ALU.not_equal, fill=1.0, base=base,
                                        pattern=[[-1, NE]], channel_multiplier=1))
            pool.memset(ones16[:, :], 1.0).then_inc(ffn_consts, 1)
            link(pool.memset(later16[:, :], 1.0))
            pool.affine_select(out=later16[:, :], in_=later16[:, :], compare_op=ALU.is_gt, fill=0.0, base=0,
                               pattern=[[1, P]], channel_multiplier=-1).then_inc(ffn_consts, 1)
            pool.iota(slots16[:, :], pattern=[[1, P]], base=0, channel_multiplier=0,
                      allow_small_or_imprecise_dtypes=True).then_inc(ffn_consts, 1)
            pool.iota(tok16[:, :], pattern=[[P, NT]], base=0, channel_multiplier=1,
                      allow_small_or_imprecise_dtypes=True).then_inc(ffn_consts, 1)
            pool.iota(r8[:, 10, :, :], pattern=[[0, NT], [-1, NE]], base=NE, channel_multiplier=0,
                      allow_small_or_imprecise_dtypes=True).then_inc(ffn_consts, 1)
            pool.iota(r8[:, 11, :, :], pattern=[[0, NT], [CAP, NE]], base=0, channel_multiplier=0,
                      allow_small_or_imprecise_dtypes=True).then_inc(ffn_consts, 1)
            pool.wait_ge(resid_in, 16 * 6)
            for t in range(NT):
                pool.tensor_tensor(xres[:, t, :], xres[:, t, :], bob[:, :], ALU.add).then_inc(resid_ready, 1)
            for t in range(NT):
                for n in range(2):
                    pool.wait_ge(var_ready, 2 * t + n + 1)
                    pool.tensor_tensor(fr[:, t, 4 + 2 * n:5 + 2 * n], fr[:, t, n:n + 1], halfneg, ALU.pow).then_inc(fr_ready, 1)

            def gather_tokens(e, par):
                pool.indirect_dma_start(out=xg[:, par, :], out_offset=None, in_=zbuf[:, :],
                                        in_offset=bass.IndirectOffsetOnAxis(ap=slot_tok[:, e:e + 1], axis=0)).then_inc(gathered[par], 16)

            def select(e, par):
                pool.tensor_copy(selx[:, par, :], sels[:, e:e + 1].to_broadcast([48, P])).then_inc(sel_set, 1)

            pool.wait_ge(z_stored, 16 * NT)
            pool.wait_ge(tok_ready, 1)
            gather_tokens(0, 0)
            gather_tokens(1, 1)
            select(0, 0)
            select(1, 1)
            pool.wait_ge(tok_ready, 2)
            for e in range(NE - 2):
                pool.wait_ge(xg_lo_done, e + 1)
                gather_tokens(e + 2, e % 2)
                pool.wait_ge(chunk_used, f0(e + 1) + 5)
                select(e + 2, e % 2)
            pool.wait_ge(rows_u_ready, 1)
            for par in range(2):
                pool.wait_ge(y_stored[par], 16 * NE // 2)
            pool.wait_ge(over_done, 1)
            for j in range(2 * NT):
                pool.indirect_dma_start(out=yg[:, j, :], out_offset=None, in_=ybuf[:, :],
                                        in_offset=bass.IndirectOffsetOnAxis(ap=rows_u[:, j % 2, j // 2:j // 2 + 1], axis=0)).then_inc(y_rows_in[j], 16)

        @block.scalar
        def _(act):
            for j, a in enumerate((src, dst, ety)):
                act.dma_start(cols[:, j, :], a).then_inc(edges_in, 16)
            act.dma_start(gbias[:, :, :], bcols).then_inc(bias_in, 16)
            act.dma_start(ewb[:, 0, :], ew.partition_broadcast(P)).then_inc(bias_in, 16)

            def keys(q):
                if q >= 2:
                    act.wait_ge(places_ready, q - 1)
                for a, b in ((src_i, srcb), (dst_i, dstb)):
                    act.dma_start(a[:, q % 2, :], b[q * PIECE * P:(q + 1) * PIECE * P].partition_broadcast(P)).then_inc(keys_in[q % 2], 16)

            def split_hi(c):
                act.wait_ge(raw_ready[c % RAW], 16 * (c // RAW + 1))
                if before(c):
                    act.wait_ge(chunk_used, before(c))
                act.activation(hi[SLOT[c]][:, :], raw[:, c % RAW, :], ACT.Copy).then_inc(hi_done, 1)

            chain = [0]

            def link(ins):
                chain[0] += 1
                ins.then_inc(act_chain, 1)
                act.wait_ge(act_chain, chain[0])

            split_hi(0)
            for t in range(NT):
                act.wait_ge(x_turned, t + 1)
                for half in range(2):
                    act.activation(xt_hi[:, 4 * half:4 * half + 4, t * P:(t + 1) * P],
                                   B[2 * t + half][:, :].rearrange("p (k n) -> p k n", k=4), ACT.Copy).then_inc(x_hi, 1)
            split_hi(1)

            def evac(i):
                m, h = HALVES[i]
                group = i
                act.wait_ge(chunk_used, 2 * i + 2)
                if NAMES[m] == "v2":
                    for t in range(NT):
                        act.activation(v_hi[:, t, h * CW:(h + 1) * CW], banks(group)[t][:, :], ACT.Copy).then_inc(bank_hi, 1)
                    return
                to = {"v1": t_hi, "k1": t_hi, "q1": t_hi, "k2": k_hi, "q2": q_hi}[NAMES[m]]
                for b in range(4):
                    o = 4 * h + b
                    act.activation(to[:, o, :], banks(group)[b][:, 0:N], ACT.Identity,
                                   bias=gbias[:, m, o:o + 1]).then_inc(bank_hi, 1)

            for i in range(12):
                split_hi(2 * i + 2)
                split_hi(2 * i + 3)
                if i == 0:
                    act.wait_ge(bias_in, 32)
                    link(act.activation(ewb[:, 1, :], ewb[:, 0, :], ACT.Abs))
                    link(act.activation(ewb[:, 1, :], ewb[:, 1, :], ACT.Exp, scale=-1.0))
                    act.activation(ewb[:, 1, :], ewb[:, 1, :], ACT.Ln, bias=1.0).then_inc(types_ready, 1)
                if i < 4:
                    keys(i)
                evac(i)
            def exps(h):
                for i in range(NT):
                    act.wait_ge(score_max, NT * h + i + 1)
                    act.activation(pr[:, h % 2, i, :], pr[:, h % 2, i, :], ACT.Exp, scale=-1.0,
                                   bias=negmax[:, h % 2, i:i + 1], accum_out=rsum[:, h % 2, i:i + 1]).then_inc(exp_done, 1)

            exps(0)
            for h in range(HEADS + 2):
                if h >= 2:
                    o, rows = h - 2, slice(HD * (h % 2), HD * (h % 2) + HD)
                    act.wait_ge(o_ready, o + 1)
                    act.activation(t_hi[rows, o // 2, :], B[6 + h % 2][rows, 0:N], ACT.Identity,
                                   bias=gbias[rows, 1, o // 2:o // 2 + 1]).then_inc(o_hi_done, 1)
                if h == 3:
                    split_hi(26)
                if h < HEADS:
                    for j in range(NT):
                        act.wait_ge(p_turned, NT * h + j + 1)
                        act.activation(at_hi[:, h % 2, j, :], B[3 + j][:, 0:N], ACT.Copy).then_inc(at_hi_done, 1)
                if h + 1 < HEADS:
                    exps(h + 1)
            split_hi(27)
            split_hi(28)
            split_hi(29)
            for t in range(NT):
                if t:
                    act.wait_ge(logits_ready, t)
                for a in range(2):
                    act.wait_ge(xf_turned, 2 * t + a + 1)
                    act.activation(xft[:, 4 * a:4 * a + 4, :].rearrange("p k n -> p (k n)"), B[6 + a], ACT.Copy).then_inc(xft_ready, 1)
                if t == 0:
                    split_hi(30)
                    split_hi(31)
                elif t == 1:
                    split_hi(32)
            act.wait_ge(gap_ready, 1)
            act.activation(r3[:, 8, :], r3[:, 7, :], ACT.Sigmoid)
            act.activation(r3[:, 9, :], r3[:, 7, :], ACT.Sigmoid, scale=-1.0).then_inc(gates_ready, 1)

            def scale_tokens(e, par):
                act.wait_ge(xg_turned, e + 1)
                for k in range(KT):
                    ins = act.activation(xg[:, par, k * P:(k + 1) * P], B[5 + k // 4][:, (k % 4) * P:(k % 4 + 1) * P],
                                         ACT.Identity, scale=egb[:, 0, e, k:k + 1], bias=egb[:, 1, e, k:k + 1])
                ins.then_inc(xg_scaled, 1)
                act.wait_ge(xg_scaled, e + 1)
                act.activation(xg_hi[:, par, :, :].rearrange("p k n -> p (k n)"), xg[:, par, :], ACT.Copy).then_inc(xg_hi_done, 1)

            def sigmoid(e):
                act.wait_ge(x2_clipped, e + 1)
                act.activation(sg[:, :], x2c[:, :], ACT.Sigmoid).then_inc(sig_done, 1)

            def turned_hi(e, par):
                act.wait_ge(h_turned, e + 1)
                act.activation(ht_hi[:, par, :, :].rearrange("p k n -> p (k n)"), B[2], ACT.Copy).then_inc(ht_hi_done, 1)

            scale_tokens(0, 0)
            for e in range(NE):
                nxt = [k if 33 <= k < CHUNKS else None for k in range(f0(e) + 3, f0(e) + 9)]
                if nxt[0]:
                    split_hi(nxt[0])
                if e + 1 < NE:
                    scale_tokens(e + 1, (e + 1) % 2)
                if nxt[1]:
                    split_hi(nxt[1])
                sigmoid(e)
                for k in nxt[2:4]:
                    if k:
                        split_hi(k)
                turned_hi(e, e % 2)
                for k in nxt[4:6]:
                    if k:
                        split_hi(k)
            with crowded(act) as e:
                act.wait_ge(over_expert, e + 1)
                for j in range(EXP_CHUNKS):
                    act.wait_ge(over_raw[j % RAW], e * 32 + 16 * (j // RAW + 1))
                    act.activation(hi[j][:, :], raw[:, j % RAW, :], ACT.Copy).then_inc(over_w_hi, 1)
                act.wait_ge(over_cols_in, e * 32 + 32)
                for t in range(1, NT):
                    step = e * (NT - 1) + t
                    act.wait_ge(over_turned, step)
                    for k in range(KT):
                        ins = act.activation(xg[:, 0, k * P:(k + 1) * P], B[5 + k // 4][:, (k % 4) * P:(k % 4 + 1) * P],
                                             ACT.Identity, scale=over_cols[:, 0, k:k + 1], bias=over_cols[:, 1, k:k + 1])
                    ins.then_inc(over_scaled, 1)
                    act.wait_ge(over_scaled, step)
                    act.activation(xg_hi[:, 0, :, :].rearrange("p k n -> p (k n)"), xg[:, 0, :], ACT.Copy).then_inc(over_hi, 1)
                    act.wait_ge(over_clipped, step)
                    act.activation(sg[:, :], x2c[:, :], ACT.Sigmoid).then_inc(over_sig, 1)
                    act.wait_ge(over_h_turned, step)
                    act.activation(ht_hi[:, 0, :, :].rearrange("p k n -> p (k n)"), B[2], ACT.Copy).then_inc(over_h_hi, 1)

        @block.vector
        def _(dve):
            chain = [0]

            def link(ins):
                chain[0] += 1
                ins.then_inc(dve_chain, 1)
                dve.wait_ge(dve_chain, chain[0])

            def split_lo(c):
                dve.wait_ge(hi_done, c + 1)
                dve.tensor_tensor(lo[SLOT[c]][:, :], raw[:, c % RAW, :], f32(hi[SLOT[c]][:, :]), ALU.subtract).then_inc(lo_done, 1)

            for t in range(NT):
                dve.wait_ge(x_in[t], 16)
                for half in range(2):
                    link(dve.bn_stats(stat[:, t, 6 * half:6 * half + 6], xin[:, t, half * CW:(half + 1) * CW]))
                dve.bn_aggr(mv[:, t, :], stat[:, t, :]).then_inc(stats_ready, 1)
            for t in range(NT):
                dve.wait_ge(rstd_ready, t + 1)
                dve.tensor_scalar(xin[:, t, :], xin[:, t, :], mv[:, t, 0:1], rs[:, 3 + t:4 + t], ALU.subtract, ALU.mult).then_inc(normed, 1)
            split_lo(0)
            for t in range(NT):
                for half in range(2):
                    dve.wait_ge(x_hi, 2 * t + half + 1)
                    cut = (slice(None), slice(4 * half, 4 * half + 4), slice(t * P, (t + 1) * P))
                    dve.tensor_tensor(xt_lo[cut], B[2 * t + half][:, :].rearrange("p (k n) -> p k n", k=4),
                                      f32(xt_hi[cut]), ALU.subtract).then_inc(x_lo, 1)
            split_lo(1)

            def evac(i):
                m, h = HALVES[i]
                group = i
                n0 = sum(NT if NAMES[HALVES[j][0]] == "v2" else 4 for j in range(i))
                if NAMES[m] == "v2":
                    for t in range(NT):
                        dve.wait_ge(bank_hi, n0 + t + 1)
                        cut = (slice(None), t, slice(h * CW, (h + 1) * CW))
                        ins = dve.tensor_tensor(v_lo[cut], banks(group)[t][:, :], f32(v_hi[cut]), ALU.subtract)
                    ins.then_inc(group_evacuated, 1)
                    return
                th, tl = {"v1": (t_hi, t_lo), "k1": (t_hi, t_lo), "q1": (t_hi, t_lo), "k2": (k_hi, k_lo),
                          "q2": (q_hi, q_lo)}[NAMES[m]]
                for b in range(4):
                    o = 4 * h + b
                    dve.wait_ge(bank_hi, n0 + b + 1)
                    ins = dve.scalar_tensor_tensor(out=tl[:, o, :], in0=banks(group)[b][:, 0:N], scalar=gbias[:, m, o:o + 1],
                                                   in1=f32(th[:, o, :]), op0=ALU.add, op1=ALU.subtract)
                ins.then_inc(group_evacuated, 1)

            def edge_columns():
                dve.wait_ge(edges_in, 48)
                link(dve.tensor_copy(colf[:, 0:2, :], cols[:, 0:2, :]))
                link(dve.scalar_tensor_tensor(out=colf[:, 2, :], in0=colf[:, 0, :], scalar=float(N), in1=colf[:, 1, :],
                                              op0=ALU.mult, op1=ALU.add))
                dve.wait_ge(consts_ready, 4)
                link(dve.tensor_tensor(colf[:, 4, :], dump[:, :], colf[:, 2, :], ALU.subtract))
                dve.wait_ge(types_ready, 1)
                link(dve.tensor_scalar(ewb[:, 3, :], ewb[:, 0, :], 0.0, None, ALU.max))
                link(dve.tensor_tensor(ewb[:, 3, :], ewb[:, 3, :], ewb[:, 1, :], ALU.add))
                link(dve.tensor_scalar(ewb[:, 2, :], ewb[:, 3, :], 8.0, None, ALU.mult))
                link(dve.tensor_scalar(bits[:, 0, :], cols[:, 2, :], 3, None, ALU.add))
                link(dve.tensor_scalar(bits[:, 0, :], bits[:, 0, :], 3, None, ALU.bitwise_and))
                for w in range(4):
                    ins = dve.tensor_scalar(wterm[:, w, :], bits[:, 0, :], float(w), ewb[:, 2, w:w + 1], ALU.is_equal, ALU.mult)
                link(ins)
                link(dve.tensor_tensor(wterm[:, 0:2, :], wterm[:, 0:2, :], wterm[:, 2:4, :], ALU.add))
                link(dve.tensor_tensor(colf[:, 5, :], wterm[:, 0, :], wterm[:, 1, :], ALU.add))
                dve.wait_ge(base_filled, NT)
                for t in range(NT):
                    block = mask8[:, t, t * P:(t + 1) * P]
                    ins = dve.scalar_tensor_tensor(out=block, in0=ident[:, :], scalar=ewb[:, 2, 3:4], in1=block, op0=ALU.mult, op1=ALU.add)
                ins.then_inc(base_ready, 1)

            def duplicates(q):
                dve.wait_ge(keys_in[q % 2], 32 * (q // 2 + 1))
                if q:
                    dve.wait_ge(places_ready, q)
                link(dve.scalar_tensor_tensor(out=keyb[:, :], in0=src_i[:, q % 2, :], scalar=float(N), in1=dst_i[:, q % 2, :],
                                              op0=ALU.mult, op1=ALU.add))
                for j in range(PIECE):
                    g = q * PIECE + j
                    width = (WIN - g % WIN) * P
                    ins = dve.scalar_tensor_tensor(out=eqt[:, j % 2, 0:width], in0=keyb[:, j * P:j * P + width],
                                                   scalar=colf[:, 2, g:g + 1], in1=later[:, 0:width], op0=ALU.is_equal,
                                                   op1=ALU.mult, accum_out=colf[:, 3, g:g + 1])
                    link(ins)
                part = slice(q * PIECE, (q + 1) * PIECE)
                link(dve.scalar_tensor_tensor(out=colf[:, 3, part], in0=colf[:, 3, part], scalar=0.0, in1=colf[:, 4, part],
                                              op0=ALU.is_gt, op1=ALU.mult))
                dve.tensor_tensor(bits[:, 1, part], colf[:, 2, part], colf[:, 3, part], ALU.add).then_inc(places_ready, 1)

            for i in range(12):
                split_lo(2 * i + 2)
                split_lo(2 * i + 3)
                if i == 0:
                    edge_columns()
                if 1 <= i < 5:
                    duplicates(i - 1)
                evac(i)
            dve.wait_ge(mask_in, 16)
            def maxima(h):
                if h >= 2:
                    dve.wait_ge(p_turned, NT * (h - 1))
                for i in range(NT):
                    dve.wait_ge(score_ready, NT * h + i + 1)
                    dve.tensor_tensor_reduce(out=pr[:, h % 2, i, :], in0=B[i][:, 0:N], in1=mask8[:, i, :],
                                             scale=-SCALE8, scalar=BIG, op0=ALU.add, op1=ALU.min,
                                             accum_out=negmax[:, h % 2, i:i + 1]).then_inc(score_max, 1)

            def normalise(h):
                dve.wait_ge(exp_done, NT * (h + 1))
                link(dve.reciprocal(rinv[:, h % 2, 1:NT], rsum[:, h % 2, 1:NT]))
                for i in range(1, NT):
                    dve.tensor_scalar(pr[:, h % 2, i, :], pr[:, h % 2, i, :], rinv[:, h % 2, i:i + 1], None,
                                      ALU.mult).then_inc(normalised, 1)

            def inverse(h):
                dve.wait_ge(exp_done, NT * h + 1)
                dve.reciprocal(rinv[:, h % 2, 0:1], rsum[:, h % 2, 0:1]).then_inc(first_inverse, 1)

            maxima(0)
            inverse(0)
            normalise(0)
            for h in range(HEADS + 2):
                if h + 1 < HEADS:
                    maxima(h + 1)
                if h >= 2:
                    o, rows = h - 2, slice(HD * (h % 2), HD * (h % 2) + HD)
                    dve.wait_ge(o_hi_done, o + 1)
                    dve.scalar_tensor_tensor(out=t_lo[rows, o // 2, :], in0=B[6 + h % 2][rows, 0:N],
                                             scalar=gbias[rows, 1, o // 2:o // 2 + 1], in1=f32(t_hi[rows, o // 2, :]),
                                             op0=ALU.add, op1=ALU.subtract).then_inc(o_lo_done, 1)
                if h == 3:
                    split_lo(26)
                if h < HEADS:
                    for j in range(NT):
                        if j == NT - 1 and h + 1 < HEADS:
                            inverse(h + 1)
                        dve.wait_ge(at_hi_done, NT * h + j + 1)
                        dve.tensor_tensor(at_lo[:, h % 2, j, :], B[3 + j][:, 0:N], f32(at_hi[:, h % 2, j, :]),
                                          ALU.subtract).then_inc(at_lo_done, 1)
                if h + 1 < HEADS:
                    normalise(h + 1)
            split_lo(27)
            split_lo(28)
            split_lo(29)
            dve.wait_ge(ffn_in, 16 * 9)
            link(dve.tensor_copy(brow[:, :], brow_f[:, :]))
            dve.tensor_tensor(brow[32:48, :], brow_f[32:48, :], f32(brow[32:48, :]), ALU.subtract).then_inc(rows_ready, 1)
            dve.wait_ge(rows_ready, 1)
            dve.wait_ge(resid_ready, NT)

            def both_stats(src, stat, to):
                for h in range(2):
                    ins = dve.bn_stats(stat[:, h, :], src[:, h * CW:(h + 1) * CW])
                link(ins)
                link(dve.bn_aggr(to, stat.rearrange("p a b -> p (a b)")))

            for t in range(NT):
                for h in range(2):
                    cut = slice(h * CW, (h + 1) * CW)
                    dve.wait_ge(proj_ready, 2 * t + h + 1)
                    link(dve.tensor_tensor(xres[:, t, cut], xres[:, t, cut], B[2 * t + h], ALU.add))
                    if h == 0:
                        dve.bn_stats(xstat[:, t, h, :], xres[:, t, cut])
                    else:
                        link(dve.bn_stats(xstat[:, t, h, :], xres[:, t, cut]))
                mean, v, a, b = fmv[:, t, 0:1], fmv[:, t, 1:2], fr[:, t, 2:3], fr[:, t, 0:1]
                link(dve.bn_aggr(fmv[:, t, 0:2], xstat[:, t, :, :].rearrange("p a b -> p (a b)")))
                link(dve.tensor_scalar(a, v, EPS, EPS, ALU.add, ALU.mult))
                dve.tensor_tensor(b, a, v, ALU.add).then_inc(var_ready, 1)
                link(dve.scalar_tensor_tensor(out=xf[:, t, :], in0=xres[:, t, :], scalar=mean, in1=lngb[:, :],
                                              op0=ALU.subtract, op1=ALU.mult))
                dve.wait_ge(fr_ready, 2 * t + 1)
                dve.scalar_tensor_tensor(out=xf[:, t, :], in0=xf[:, t, :], scalar=fr[:, t, 4:5], in1=lnbb[:, :],
                                         op0=ALU.mult, op1=ALU.add).then_inc(xf_ready, 1)
                dve.wait_ge(xf_ready, t + 1)
                both_stats(xf[:, t, :], fstat[:, t, :, :], fmv[:, t, 2:4])
                dve.tensor_scalar(fr[:, t, 1:2], fmv[:, t, 3:4], EPS, None, ALU.add).then_inc(var_ready, 1)
                if t > 0:
                    split_lo(29 + t)
                dve.wait_ge(fr_ready, 2 * t + 2)
                dve.wait_ge(xf_turned, 2 * t + 2)
                dve.tensor_scalar(xf[:, t, :], xf[:, t, :], fmv[:, t, 2:3], fr[:, t, 6:7], ALU.subtract, ALU.mult).then_inc(z_ready, 1)

            lg, eq, a, oh1, l2, oh2, pos, tmp, posm, over_gate = (r8[:, j, :, :] for j in range(10))
            order, first_row = r8[:, 10, :, :], r8[:, 11, :, :]
            m1, m2, mx = r3[:, 0, :], r3[:, 1, :], r3[:, 2, :]

            def wide(v):
                return v.unsqueeze(2).to_broadcast([P, NT, NE])

            def largest(values, top, onehot):
                link(dve.tensor_reduce(top, values, AX, ALU.max))
                link(dve.tensor_tensor(eq, values, wide(top), ALU.is_equal))
                link(dve.tensor_tensor(a, eq, order, ALU.mult))
                link(dve.tensor_reduce(mx, a, AX, ALU.max))
                link(dve.tensor_tensor(onehot, a, wide(mx), ALU.is_equal))

            dve.wait_ge(ffn_consts, 6)
            dve.wait_ge(logits_ready, NT)
            link(dve.tensor_copy(lg, B[0][:, 0:NT * NE].rearrange("p (t e) -> p t e", t=NT)))
            largest(lg, m1, oh1)
            link(dve.scalar_tensor_tensor(out=l2, in0=oh1, scalar=NEG, in1=lg, op0=ALU.mult, op1=ALU.add))
            largest(l2, m2, oh2)
            dve.tensor_tensor(sel16[:, :, :], oh1, oh2, ALU.add).then_inc(sel_ready, 1)
            dve.tensor_tensor(r3[:, 7, :], m1, m2, ALU.subtract).then_inc(gap_ready, 1)
            dve.wait_ge(sel_ready, 1)
            link(dve.tensor_scalar(tmp, sel16[:, :, :], -1024.0, 1024.0, ALU.mult, ALU.add))
            dve.wait_ge(pos_ready, 1)
            link(dve.tensor_copy(pos, B[3][:, 0:NT * NE].rearrange("p (t e) -> p t e", t=NT)))
            link(dve.tensor_tensor(posm, pos, tmp, ALU.add))
            for e in range(NE):
                for t in range(NT):
                    ins = dve.tensor_scalar(slot_oh[:, e, t, :], slots16[:, :], posm[:, t, e:e + 1], None, ALU.is_equal)
                ins.then_inc(slot_oh_ready, 1)
                if e == 1:
                    dve.wait_ge(tok_summed, 2)
                    dve.tensor_copy(slot_tok[:, 0:2], B[2][:, 0:2]).then_inc(tok_ready, 1)
            for j, oh in enumerate((oh1, oh2)):
                link(dve.tensor_tensor(tmp, oh, pos, ALU.mult))
                link(dve.tensor_reduce(r3[:, 5 + j, :], tmp, AX, ALU.add))
                link(dve.tensor_tensor(tmp, oh, first_row, ALU.mult))
                link(dve.tensor_reduce(r3[:, 3 + j, :], tmp, AX, ALU.add))
                link(dve.scalar_tensor_tensor(out=r3[:, 3 + j, :], in0=r3[:, 5 + j, :], scalar=float(CAP - 1),
                                              in1=r3[:, 3 + j, :], op0=ALU.min, op1=ALU.add))
            dve.tensor_copy(rows_u[:, :, :], r3[:, 3:5, :]).then_inc(rows_u_ready, 1)
            dve.wait_ge(gates_ready, 1)
            dve.wait_ge(rows_u_ready, 1)
            for j, oh in enumerate((oh1, oh2)):
                link(dve.scalar_tensor_tensor(out=r3[:, 3 + j, :], in0=r3[:, 5 + j, :], scalar=float(CAP),
                                              in1=r3[:, 8 + j, :], op0=ALU.is_ge, op1=ALU.mult))
                link(dve.scalar_tensor_tensor(out=r3[:, 8 + j, :], in0=r3[:, 5 + j, :], scalar=float(CAP),
                                              in1=r3[:, 8 + j, :], op0=ALU.is_lt, op1=ALU.mult))
                link(dve.tensor_tensor(over_gate if j == 0 else tmp, oh, wide(r3[:, 3 + j, :]), ALU.mult))
            link(dve.tensor_tensor(over_gate, over_gate, tmp, ALU.add))
            link(dve.tensor_reduce(r3[:, 2, 0:1], B[3][:, NT * NE:(NT + 1) * NE], AX, ALU.max))
            dve.tensor_copy(most[:, :], r3[:, 2, 0:1]).then_inc(most_ready, 1)
            dve.wait_ge(tok_summed, NE)
            dve.tensor_copy(slot_tok[:, 2:NE], B[7][:, 2:NE]).then_inc(tok_ready, 1)

            def tokens_lo(e, par):
                dve.wait_ge(xg_hi_done, e + 1)
                dve.tensor_tensor(xg_lo[:, par, :, :].rearrange("p k n -> p (k n)"), xg[:, par, :],
                                  f32(xg_hi[:, par, :, :]).rearrange("p k n -> p (k n)"), ALU.subtract).then_inc(xg_lo_done, 1)

            def store_y(e, par):
                dve.wait_ge(chunk_used, f0(e + 1) + 6 if e < NE - 1 else CHUNKS)
                if e >= 2:
                    dve.wait_ge(y_stored[par], 16 * (e // 2))
                dve.tensor_scalar(y[:, par, :].rearrange("p (a n) -> p a n", a=2), ps[:, 3:5, :], 10000.0, -10000.0,
                                  ALU.min, ALU.max).then_inc(y_ready, 1)

            split_lo(32)
            tokens_lo(0, 0)
            for e in range(NE):
                nxt = [k if 33 <= k < CHUNKS else None for k in range(f0(e) + 3, f0(e) + 9)]
                if nxt[0]:
                    split_lo(nxt[0])
                dve.wait_ge(chunk_used, up_chunks(e) + 2)
                if e:
                    dve.wait_ge(h_ready, e)
                dve.tensor_scalar(x2c[:, :], B[1], 20.0, -20.0, ALU.min, ALU.max).then_inc(x2_clipped, 1)
                if nxt[1]:
                    split_lo(nxt[1])
                if e + 1 < NE:
                    tokens_lo(e + 1, (e + 1) % 2)
                dve.wait_ge(sig_done, e + 1)
                link(dve.tensor_tensor(sg[:, :], x2c[:, :], sg[:, :], ALU.mult))
                if nxt[2]:
                    split_lo(nxt[2])
                dve.wait_ge(chunk_used, up_chunks(e) + 4)
                if e:
                    dve.wait_ge(h_turned, e)
                link(dve.tensor_tensor(hh[:, :], B[0], sg[:, :], ALU.mult))
                dve.tensor_scalar(hh[:, :], hh[:, :], 10000.0, -10000.0, ALU.min, ALU.max).then_inc(h_ready, 1)
                if nxt[3]:
                    split_lo(nxt[3])
                if e:
                    store_y(e - 1, (e - 1) % 2)
                if nxt[4]:
                    split_lo(nxt[4])
                dve.wait_ge(ht_hi_done, e + 1)
                par = e % 2
                dve.tensor_tensor(ht_lo[:, par, :, :].rearrange("p k n -> p (k n)"), B[2],
                                  f32(ht_hi[:, par, :, :]).rearrange("p k n -> p (k n)"), ALU.subtract).then_inc(ht_lo_done, 1)
                if nxt[5]:
                    split_lo(nxt[5])
            store_y(NE - 1, (NE - 1) % 2)
            with crowded(dve) as e:
                dve.wait_ge(y_stored[0], 16 * NE // 2)
                dve.tensor_copy(fr[:, :, 7:8], over_gate[:, :, bass.ds(e, 1)])
                dve.tensor_copy(selx[:, 0, :], sels[:, bass.ds(e, 1)].to_broadcast([48, P])).then_inc(over_sel, 1)
                dve.wait_ge(over_sel, e + 1)
                for j in range(EXP_CHUNKS):
                    dve.wait_ge(over_w_hi, e * EXP_CHUNKS + (j + 1))
                    dve.tensor_tensor(lo[j][:, :], raw[:, j % RAW, :], f32(hi[j][:, :]), ALU.subtract).then_inc(over_w_lo, 1)
                for t in range(1, NT):
                    step = e * (NT - 1) + t
                    dve.wait_ge(over_hi, step)
                    dve.tensor_tensor(xg_lo[:, 0, :, :].rearrange("p k n -> p (k n)"), xg[:, 0, :],
                                      f32(xg_hi[:, 0, :, :]).rearrange("p k n -> p (k n)"), ALU.subtract).then_inc(over_lo, 1)
                    dve.wait_ge(over_up, step)
                    dve.tensor_scalar(x2c[:, :], B[1], 20.0, -20.0, ALU.min, ALU.max).then_inc(over_clipped, 1)
                    dve.wait_ge(over_sig, step)
                    dve.tensor_tensor(sg[:, :], x2c[:, :], sg[:, :], ALU.mult).then_inc(over_dve, 1)
                    dve.wait_ge(over_dve, e * (3 * (NT - 1)) + (3 * t - 2))
                    dve.tensor_tensor(hh[:, :], B[0], sg[:, :], ALU.mult).then_inc(over_dve, 1)
                    dve.wait_ge(over_dve, e * (3 * (NT - 1)) + (3 * t - 1))
                    dve.tensor_scalar(hh[:, :], hh[:, :], 10000.0, -10000.0, ALU.min, ALU.max).then_inc(over_h, 1)
                    dve.wait_ge(over_h_hi, step)
                    dve.tensor_tensor(ht_lo[:, 0, :, :].rearrange("p k n -> p (k n)"), B[2],
                                      f32(ht_hi[:, 0, :, :]).rearrange("p k n -> p (k n)"), ALU.subtract).then_inc(over_h_lo, 1)
                    dve.wait_ge(over_down, step)
                    dve.tensor_scalar(y[:, 0, :].rearrange("p (a n) -> p a n", a=2), ps[:, 3:5, :], 10000.0, -10000.0,
                                      ALU.min, ALU.max).then_inc(over_dve, 1)
                    dve.wait_ge(over_dve, e * (3 * (NT - 1)) + 3 * t)
                    dve.scalar_tensor_tensor(out=xres[:, t, :], in0=y[:, 0, :], scalar=fr[:, t, 7:8],
                                             in1=xres[:, t, :], op0=ALU.mult, op1=ALU.add).then_inc(over_added, 1)
                    dve.wait_ge(over_added, step)
            dve.wait_ge(gates_ready, 1)
            for t in range(NT):
                for j in range(2):
                    dve.wait_ge(y_rows_in[2 * t + j], 16)
                    ins = dve.scalar_tensor_tensor(out=xres[:, t, :], in0=yg[:, 2 * t + j, :], scalar=r3[:, 8 + j, t:t + 1],
                                                   in1=xres[:, t, :], op0=ALU.mult, op1=ALU.add)
                    if j == 0:
                        link(ins)
                ins.then_inc(out_ready, 1)

        @block.tensor
        def _(pe):
            def three(o, a, b, first, last):
                for n, (s, m) in enumerate(((0, 0), (0, 1), (1, 0))):
                    ins = pe.matmul(o, a[s], b[m], start=first and n == 0, stop=last and n == 2)
                return ins

            pe.wait_ge(consts_ready, 2)
            for t in range(NT):
                pe.wait_ge(normed, t + 1)
                for k in range(KT):
                    ins = pe.transpose(B[2 * t + k // 4][:, (k % 4) * P:(k % 4 + 1) * P], xin[:, t, k * P:(k + 1) * P], ident[:, :])
                ins.then_inc(x_turned, 1)

            def weight(c, k, cut=slice(0, CW)):
                w = slice(k * CW + cut.start, k * CW + cut.stop)
                return hi[SLOT[c]][:, w], lo[SLOT[c]][:, w]

            def half(i):
                m, h = HALVES[i]
                group = i
                if group >= 2:
                    pe.wait_ge(group_evacuated, group - 1)
                for part in range(2):
                    c = 2 * i + part
                    pe.wait_ge(lo_done, c + 1)
                    if NAMES[m][1] == "2":
                        pe.wait_ge(group_evacuated, 2 * (m - 1) + part + 1)
                    act_hi, act_lo = (t_hi, t_lo) if NAMES[m][1] == "2" else (xt_hi, xt_lo)
                    for kk in range(CK):
                        k = CK * part + kk
                        if NAMES[m] == "v2":
                            for t in range(NT):
                                tok = slice(t * P, (t + 1) * P)
                                ins = three(banks(group)[t][:, :], (act_hi[:, k, tok], act_lo[:, k, tok]), weight(c, kk),
                                            k == 0, k == KT - 1)
                        else:
                            for b in range(4):
                                ins = three(banks(group)[b][:, 0:N], weight(c, kk, slice(b * P, (b + 1) * P)),
                                            (act_hi[:, k, :], act_lo[:, k, :]), k == 0, k == KT - 1)
                    ins.then_inc(chunk_used, 1)

            def scores(h):
                rows = slice(HD * (h % 2), HD * (h % 2) + HD)
                for i in range(NT):
                    if h > 0:
                        pe.wait_ge(score_max, 3 * (h - 1) + i + 1)
                    tok = slice(i * P, (i + 1) * P)
                    three(B[i][:, 0:N], (q_hi[rows, h // 2, tok], q_lo[rows, h // 2, tok]),
                          (k_hi[rows, h // 2, :], k_lo[rows, h // 2, :]), True, True).then_inc(score_ready, 1)

            def turn(h):
                pe.wait_ge(first_normalised, h + 1)
                pe.wait_ge(normalised, (NT - 1) * (h + 1))
                for j in range(NT):
                    if h > 0:
                        pe.wait_ge(at_lo_done, 3 * (h - 1) + j + 1)
                    for i in range(NT):
                        ins = pe.transpose(B[3 + j][:, i * P:(i + 1) * P], pr[:, h % 2, i, j * P:(j + 1) * P], ident[:, :])
                    ins.then_inc(p_turned, 1)

            def attend(h):
                if h >= 2:
                    pe.wait_ge(o_lo_done, h - 1)
                pair = slice((h // 2) * P, (h // 2 + 1) * P)
                for j in range(NT):
                    pe.wait_ge(at_lo_done, 3 * h + j + 1)
                    ins = three(B[6 + h % 2][:, 0:N], (v_hi[:, j, pair], v_lo[:, j, pair]),
                                (at_hi[:, h % 2, j, :], at_lo[:, h % 2, j, :]), j == 0, j == NT - 1)
                ins.then_inc(o_ready, 1)

            for i in range(12):
                if i == 0:
                    pe.wait_ge(x_lo, 2 * NT)
                half(i)
            pe.wait_ge(group_evacuated, 12)
            scores(0)
            scores(1)
            for h in range(HEADS + 1):
                if h < HEADS:
                    turn(h)
                if h >= 1:
                    attend(h - 1)
                if h + 2 < HEADS:
                    scores(h + 2)
            def router(t):
                pe.wait_ge(xf_ready, t + 1)
                for k in range(KT):
                    if t and k % 4 == 0:
                        pe.wait_ge(xft_ready, 2 * (t - 1) + k // 4 + 1)
                    ins = pe.transpose(B[6 + k // 4][:, (k % 4) * P:(k % 4 + 1) * P], xf[:, t, k * P:(k + 1) * P], ident[:, :])
                    if k % 4 == 3:
                        ins.then_inc(xf_turned, 1)
                    if t == NT - 1 and k == 0:
                        ins.then_inc(chunk_used, 1)
                for k in range(KT):
                    pe.wait_ge(xft_ready, 2 * t + k // 4 + 1)
                    ins = pe.matmul(B[0][:, t * NE:(t + 1) * NE], xft[:, k, :], rws[:, k, :], start=k == 0, stop=k == KT - 1)
                ins.then_inc(logits_ready, 1)

            for t in range(NT):
                tok = slice(t * P, (t + 1) * P)
                for h in range(2):
                    for k in range(KT):
                        if t == 0:
                            pe.wait_ge(lo_done, 24 + 2 * h + k // CK + 1)
                            if h == 0:
                                pe.wait_ge(o_lo_done, 2 * k + 2)
                        elif k == 6 and h == 1:
                            router(t - 1)
                        ins = three(B[2 * t + h], (t_hi[:, k, tok], t_lo[:, k, tok]), weight(24 + 2 * h + k // CK, k % CK),
                                    k == 0, k == KT - 1)
                        if t == NT - 1 and (h, k) in ((0, CK), (1, 0), (1, CK - 1)):
                            ins.then_inc(chunk_used, 1)
                    ins.then_inc(proj_ready, 1)
            router(NT - 1)
            pe.wait_ge(sel_ready, 1)
            pe.wait_ge(ffn_consts, 6)
            for t in range(NT):
                for j in range(t + 1):
                    ins = pe.matmul(B[3][:, t * NE:(t + 1) * NE], ones16[:, :] if j < t else later16[:, :], sel16[:, j, :],
                                    start=j == 0, stop=j == t)
            for j in range(NT):
                ins = pe.matmul(B[3][:, NT * NE:(NT + 1) * NE], ones16[:, :], sel16[:, j, :], start=j == 0, stop=j == NT - 1)
            ins.then_inc(pos_ready, 1)
            for e in range(NE):
                pe.wait_ge(slot_oh_ready, e + 1)
                bank = B[2] if e < 2 else B[7]
                for t in range(NT):
                    ins = pe.matmul(bank[:, e:e + 1], slot_oh[:, e, t, :], tok16[:, t:t + 1], start=t == 0, stop=t == NT - 1)
                ins.then_inc(tok_summed, 1)

            def turn_tokens(e, par):
                pe.wait_ge(gathered[par], 16 * (e // 2 + 1))
                if e:
                    pe.wait_ge(xg_scaled, e)
                for k in range(KT):
                    ins = pe.transpose(B[5 + k // 4][:, (k % 4) * P:(k % 4 + 1) * P], xg[:, par, k * P:(k + 1) * P], ident[:, :])
                ins.then_inc(xg_turned, 1)

            def up(bank, e, par, c, cols):
                pe.matmul(bank, selx[0:40, par, :], brow[0:40, cols], start=True, stop=False)
                for part in range(2):
                    pe.wait_ge(lo_done, c + part + 1)
                    for kk in range(CK):
                        k = CK * part + kk
                        ins = three(bank, (xg_hi[:, par, k, :], xg_lo[:, par, k, :]), weight(c + part, kk), False, k == KT - 1)
                    ins.then_inc(chunk_used, 1)

            def down(e, par, c):
                pe.wait_ge(ht_lo_done, e + 1)
                if e:
                    pe.wait_ge(y_ready, e)
                for part in range(2):
                    cols = slice(D + part * CW, D + (part + 1) * CW)
                    pe.matmul(B[3 + part], selx[0:40, par, :], brow[0:40, cols], start=True, stop=False)
                for part in range(2):
                    pe.wait_ge(lo_done, c + part + 1)
                    for k in range(HT):
                        ins = three(B[3 + part], (ht_hi[:, par, k, :], ht_lo[:, par, k, :]), weight(c + part, k), False, k == HT - 1)
                    ins.then_inc(chunk_used, 1)

            def turn_hidden(e):
                pe.wait_ge(h_ready, e + 1)
                if e:
                    pe.wait_ge(ht_lo_done, e)
                for k in range(HT):
                    ins = pe.transpose(B[2][:, k * P:(k + 1) * P], hh[:, k * P:(k + 1) * P], ident[:, :])
                ins.then_inc(h_turned, 1)

            turn_tokens(0, 0)
            pe.wait_ge(rows_ready, 1)
            for e in range(NE):
                par = e % 2
                c = up_chunks(e)
                pe.wait_ge(xg_lo_done, e + 1)
                pe.wait_ge(sel_set, e + 1)
                if e:
                    pe.wait_ge(x2_clipped, e)
                up(B[1], e, par, c, slice(CW, 2 * CW))
                if e + 1 < NE:
                    turn_tokens(e + 1, 1 - par)
                if e:
                    pe.wait_ge(h_ready, e)
                up(B[0], e, par, c + 2, slice(0, CW))
                if e:
                    down(e - 1, 1 - par, c + 4)
                turn_hidden(e)
            down(NE - 1, 1, CHUNKS - 2)

            def over_sum(bank, act_hi, act_lo, tiles, chunk0, bias_cols):
                pe.matmul(bank, selx[0:40, 0, :], brow[0:40, bias_cols], start=True, stop=False)
                for k in range(tiles):
                    s, w = chunk0 + k // CK, slice(k % CK * CW, (k % CK + 1) * CW)
                    ins = three(bank, (act_hi[:, 0, k, :], act_lo[:, 0, k, :]), (hi[s][:, w], lo[s][:, w]), False, k == tiles - 1)
                return ins

            pe.wait_ge(y_ready, NE)
            pe.sem_inc(over_expert, 1)
            with crowded(pe) as e:
                pe.wait_ge(over_sel, e + 1)
                pe.wait_ge(over_w_lo, e * EXP_CHUNKS + EXP_CHUNKS)
                for t in range(1, NT):
                    step = e * (NT - 1) + t
                    if t > 1:
                        pe.wait_ge(over_added, e * (NT - 1) + (t - 1))
                    pe.wait_ge(over_z_in, (e * (NT - 1) + t) * 16)
                    for k in range(KT):
                        ins = pe.transpose(B[5 + k // 4][:, (k % 4) * P:(k % 4 + 1) * P], xg[:, 1, k * P:(k + 1) * P], ident[:, :])
                    ins.then_inc(over_turned, 1)
                    pe.wait_ge(over_lo, step)
                    over_sum(B[1], xg_hi, xg_lo, KT, 0, slice(CW, 2 * CW))
                    over_sum(B[0], xg_hi, xg_lo, KT, 2, slice(0, CW)).then_inc(over_up, 1)
                    pe.wait_ge(over_h, step)
                    for k in range(HT):
                        ins = pe.transpose(B[2][:, k * P:(k + 1) * P], hh[:, k * P:(k + 1) * P], ident[:, :])
                    ins.then_inc(over_h_turned, 1)
                    pe.wait_ge(over_h_lo, step)
                    over_sum(B[3], ht_hi, ht_lo, HT, 4, slice(D, D + CW))
                    over_sum(B[4], ht_hi, ht_lo, HT, 5, slice(D + CW, 2 * D)).then_inc(over_down, 1)
                pe.wait_ge(over_added, e * (NT - 1) + (NT - 1))
                pe.sem_inc(over_expert, 1)
            pe.sem_inc(over_done, 1)


_INS = ["x", "src", "dst", "ety", "srcb", "dstb", "ew", "wg", "bcols", "bo", "lng", "lnb", "rw", "egc", "ebc", "wf", "b1", "b2", "be"]


def layouts(i):
    c = np.ascontiguousarray
    f = {k: np.asarray(v) for k, v in i.items()}
    g = "L0_gnn_"

    def chunks(w):
        n = w.shape[1] // CW
        return w.reshape(-1, CK, P, n, CW).transpose(3, 0, 2, 1, 4).reshape(n, -1, P, CE)

    wg = np.concatenate([chunks(f[g + n].T).reshape(4, P, CE) for n in ("wv", "wiv", "wk", "wik", "wq", "wiq", "wo")])
    u = "L0_ffn_"
    wf = np.stack([np.concatenate([chunks(f[u + "W2"][e]).reshape(2, P, CE), chunks(f[u + "W1"][e]).reshape(2, P, CE),
                                   chunks(f[u + "Wo"][e]).reshape(2, P, CE)]) for e in range(NE)])

    def edge(a):
        return c(a.reshape(EG, P).T)

    return {
        "x": c(f["x"]), "src": edge(f["src"]), "dst": edge(f["dst"]), "ety": edge(f["edge_type_5"]),
        "srcb": c(f["src"]), "dstb": c(f["dst"]), "ew": c(f[g + "edge_type_weights"]), "wg": c(wg),
        "bcols": c(np.stack([f[g + n].reshape(KT, P).T for n in ("bv", "biv", "bk", "bik", "bq", "biq")], 1)),
        "bo": c(f[g + "bo"]), "lng": c(f[u + "ln_g"]), "lnb": c(f[u + "ln_b"]),
        "rw": c(f[u + "router_w"].reshape(KT, P, NE).transpose(1, 0, 2)),
        "egc": c(f[u + "eg"].reshape(NE, KT, P).transpose(2, 0, 1)), "ebc": c(f[u + "eb"].reshape(NE, KT, P).transpose(2, 0, 1)),
        "wf": c(wf), "b1": c(f[u + "b1"]), "b2": c(f[u + "b2"]), "be": c(f[u + "bo"]),
    }


def kernel(**inputs):
    import concourse.bacc as bacc
    from concourse.bass_utils import run_bass_kernel_spmd

    nc = bacc.Bacc("TRN2", target_bir_lowering=False, num_devices=1)
    arrays = layouts(inputs)
    args = [nc.dram_tensor(f"in_{n}", arrays[n].shape, mybir.dt.from_np(arrays[n].dtype), kind="ExternalInput").ap() for n in _INS]
    out = nc.dram_tensor("out_0", (N, D), F32, kind="ExternalOutput").ap()
    gnn_ffn(nc, *args, out)
    r = run_bass_kernel_spmd(nc, [{f"in_{n}": arrays[n] for n in _INS}], core_ids=[0])
    return r.results[0]["out_0"]
```

```python
from contextlib import ExitStack, contextmanager

import numpy as np

import concourse.bass as bass
from concourse import mybir
from concourse.alu_op_type import AluOpType as ALU

F32 = mybir.dt.float32
F32R = mybir.dt.float32r
F16 = mybir.dt.float16
I32 = mybir.dt.int32
U32 = mybir.dt.uint32
ACT = mybir.ActivationFunctionType
AX = mybir.AxisListType.X

P = 128
N = 384
NT = N // P
D = 1024
KT = D // P
HEADS = 16
HD = D // HEADS
EDGES = 6144
EG = EDGES // P
NE = 8
HF = 512
HT = HF // P
EPS = 1e-5
NEG = -1e30
BIG = 3.0e38
CK = 4
CW = 512
CE = CK * CW
GNN_CHUNKS = 7 * 4
EXP_CHUNKS = 6
CAP = P
WARM_UP = 24
WIN = 2
PIECE = 12


def expert_order():
    order = []
    for e in range(NE + 1):
        if e < NE:
            order += [(e, 0), (e, 1), (e, 2), (e, 3)]
        if e > 0:
            order += [(e - 1, 4), (e - 1, 5)]
    return order


EXPERT_ORDER = expert_order()
LO_ON_POOL = (1, 4)
CHUNKS = GNN_CHUNKS + len(EXPERT_ORDER)
RAWS = 7
OUT_LAST = GNN_CHUNKS - 1
LNB_FREE = OUT_LAST + 8
XF_FREE = LNB_FREE + 1
UP_LAST = CHUNKS - 5
SLOT = [c % 3 for c in range(OUT_LAST)] + [4] + [(3, 0, 1, 2, 4)[j % 5] for j in range(len(EXPERT_ORDER))]
RAW = [c % 3 if c < OUT_LAST else (c - OUT_LAST) % 5 if c < LNB_FREE else (5, 6, 3, 4, 0, 1, 2)[(c - LNB_FREE) % RAWS] for c in range(CHUNKS)]
FIRST = GNN_CHUNKS + 5
LAST = (NE - 2, NE - 1)
POOL_LO = {c for c in range(FIRST, CHUNKS - 3) if (c - FIRST) % 6 in LO_ON_POOL} | {CHUNKS - 2}


def nth(c):
    return sum(1 for k in range(c + 1) if (k in POOL_LO) == (c in POOL_LO))


def before(c):
    return max((p + 1 for p in range(c) if SLOT[p] == SLOT[c]), default=0)


def raw_before(c):
    return max((p for p in range(c) if RAW[p] == RAW[c]), default=None)


def raw_loads(c):
    return sum(1 for p in range(c + 1) if RAW[p] == RAW[c])


def gnn_ffn(nc, x, src, dst, ety, srcb, dstb, ew, wg, bcols, bo, lng, lnb, rw, egc, ebc, wf, b1, b2, be, out):
    ctx = ExitStack()
    with ctx:
        def sem(name):
            return ctx.enter_context(nc.semaphore(name))

        def psum(name, shape, dt=F32):
            return ctx.enter_context(nc.psum_tensor(name, shape, dt))

        def sb(stack, name, shape, dt):
            return stack.enter_context(nc.sbuf_tensor(name, shape, dt))

        raw = sb(ctx, "raw", [P, 3, CE], F32)
        hi = [sb(ctx, f"hi{s}", [P, CE], F32R) for s in range(3)]
        lo = [sb(ctx, f"lo{s}", [P, CE], F32R) for s in range(3)]
        ident = sb(ctx, "ident", [P, P], F32)
        small = sb(ctx, "small", [P, 70], F32)
        gbias = sb(ctx, "gbias", [P, 6, KT], F32)

        gnn = ExitStack()
        with gnn:
            xt_hi = sb(gnn, "xt_hi", [P, KT, N], F32R)
            xt_lo = sb(gnn, "xt_lo", [P, KT, N], F32R)
            t_hi = sb(gnn, "t_hi", [P, KT, N], F32R)
            t_lo = sb(gnn, "t_lo", [P, KT, N], F32R)
            v_hi = sb(gnn, "v_hi", [P, NT, D], F32R)
            v_lo = sb(gnn, "v_lo", [P, NT, D], F32R)
            mask8 = sb(gnn, "mask8", [P, NT, N], F32)
            with ExitStack() as early:
                xin = sb(early, "xin", [P, NT, D], F32)
                src_i = sb(early, "src_i", [P, 2, PIECE * P], I32)
                dst_i = sb(early, "dst_i", [P, 2, PIECE * P], I32)
                keyb = sb(early, "keyb", [P, PIECE * P], F32)
                eqt = sb(early, "eqt", [P, 2, WIN * P], F32)
            k_hi = sb(gnn, "k_hi", [P, KT, N], F32R)
            k_lo = sb(gnn, "k_lo", [P, KT, N], F32R)
            pr = sb(gnn, "pr", [P, 2, NT, N], F32)
            at_hi = sb(gnn, "at_hi", [P, 2, NT, N], F32R)
            at_lo = sb(gnn, "at_lo", [P, 2, NT, N], F32R)
            cols = sb(gnn, "cols", [P, 3, EG], I32)
            colf = sb(gnn, "colf", [P, 6, EG], F32)
            wterm = sb(gnn, "wterm", [P, 4, EG], F32)
            bits = sb(gnn, "bits", [P, 2, EG], I32)
            dump = sb(gnn, "dump", [P, EG], F32)
            later = sb(gnn, "later", [P, WIN * P], F32)
            ewb = sb(gnn, "ewb", [P, 4, 4], F32)
        q_hi, q_lo = xt_hi, xt_lo

        with ExitStack() as ffn:
            xres = sb(ffn, "xres", [P, NT, D], F32)
            raw5 = sb(ffn, "raw5", [P, CE], F32)
            lngb, lnbb = raw5[:, 0:D], raw5[:, D:2 * D]
            x2c = sb(ffn, "x2c", [P, CW], F32)
            sg = sb(ffn, "sg", [P, CW], F32)
            with ExitStack() as last:
                yg = sb(last, "yg", [P, 2 * NT, D], F32)
            xg = sb(ffn, "xg", [P, 2, D], F32)
            xg_hi = sb(ffn, "xg_hi", [P, 2, KT, P], F32R)
            xg_lo = sb(ffn, "xg_lo", [P, 2, KT, P], F32R)
            hi.append(sb(ffn, "hi3", [P, CE], F32R))
            lo.append(sb(ffn, "lo3", [P, CE], F32R))
            with ExitStack() as over:
                over_wo_hi, over_wo_lo = sb(over, "over_wo_hi", [P, CE], F32R), sb(over, "over_wo_lo", [P, CE], F32R)
            raws = [raw[:, j, :] for j in range(3)] + [sb(ffn, f"raw{s}", [P, CE], F32)[:, :] for s in (3, 4)]
            hi += [sb(ffn, "hi4", [P, CE], F32R), over_wo_hi]
            lo += [sb(ffn, "lo4", [P, CE], F32R), over_wo_lo]
            with ExitStack() as rowbuild:
                brow_f = sb(rowbuild, "brow_f", [48, 2 * D], F32)
            with ExitStack() as experts:
                y = sb(experts, "y", [P, 2, D], F32)
            xfb = sb(ffn, "xfb", [P, NT + 1, D], F32)
            xf, bob = xfb[:, 0:NT, :], xfb[:, NT, :]
            brow = sb(ffn, "brow", [48, 2 * D], F32R)
            with ExitStack() as router:
                xft = sb(router, "xft", [P, KT, P], F32)
            raws += [raw5[:, :], xfb[:, NT - 1:NT + 1, :].rearrange("p a d -> p (a d)")]
            hh = sb(ffn, "hh", [P, CW], F32)
            with ExitStack() as router2:
                slot_oh = sb(router2, "slot_oh", [P, NE, NT, P], F16)
            ht_hi = sb(ffn, "ht_hi", [P, 2, HT, P], F32R)
            ht_lo = sb(ffn, "ht_lo", [P, 2, HT, P], F32R)
            rws = sb(ffn, "rws", [P, KT, NE], F32)
            egb = sb(ffn, "egb", [P, 2, NE, KT], F32)
            sels = sb(ffn, "sels", [48, NE], F32)
            selx = sb(ffn, "selx", [48, 3, P], F32R)
            r8 = sb(ffn, "r8", [P, 12, NT, NE], F32)
            r3 = sb(ffn, "r3", [P, 10, NT], F32)
            sel16 = sb(ffn, "sel16", [P, NT, NE], F16)
            ones16 = sb(ffn, "ones16", [P, P], F16)
            later16 = sb(ffn, "later16", [P, P], F16)
            slots16 = sb(ffn, "slots16", [P, P], F16)
            tok16 = sb(ffn, "tok16", [P, NT], F16)
            slot_tok = sb(ffn, "slot_tok", [P, NE], U32)
            most = sb(ffn, "most", [P, 1], I32)
            over_cols = sb(ffn, "over_cols", [P, 2, KT], F32)
            rows_u = sb(ffn, "rows_u", [P, 2, NT], U32)
            xstat = sb(ffn, "xstat", [P, NT, 2, 6], F32)
            fmv = sb(ffn, "fmv", [P, NT, 4], F32)
            fr = sb(ffn, "fr", [P, NT, 8], F32)
        zbuf = nc.dram_tensor("z_rows", (N, D), F32, kind="Internal").ap()
        ybuf = nc.dram_tensor("y_rows", (LAST[0] * CAP, D), F32, kind="Internal").ap()

        mbuf = nc.dram_tensor("mask_rows", (N * N + WIN * P, 1), F32, kind="Internal").ap()
        mask_rows = mbuf[0:N * N, :].rearrange("(t p j) o -> p t (j o)", t=NT, p=P)

        ps = psum("ps", [P, 8, CW])
        B = [ps[:, i, :] for i in range(8)]

        raw_ready = [sem(f"raw_ready{s}") for s in range(RAWS)]
        hi_done, lo_done, chunk_used = sem("hi_done"), sem("lo_done"), sem("chunk_used")
        pool_lo_done = sem("pool_lo_done")
        x_in = [sem(f"x_in{t}") for t in range(NT)]
        edges_in, bias_in, keys_in = sem("edges_in"), sem("bias_in"), [sem("keys_in0"), sem("keys_in1")]
        consts_ready = sem("consts_ready")
        stats_ready, rstd_ready, pool_chain = sem("stats_ready"), sem("rstd_ready"), sem("pool_chain")
        normed, x_turned, x_hi, x_lo = sem("normed"), sem("x_turned"), sem("x_hi"), sem("x_lo")
        dve_chain, act_chain = sem("dve_chain"), sem("act_chain")
        bank_hi, group_evacuated = sem("bank_hi"), sem("group_evacuated")
        types_ready, base_filled, base_ready, base_stored = sem("types_ready"), sem("base_filled"), sem("base_ready"), sem("base_stored")
        places_ready, scattered, mask_in = sem("places_ready"), sem("scattered"), sem("mask_in")
        score_ready, score_max, exp_done, normalised = (
            sem("score_ready"), sem("score_max"), sem("exp_done"), sem("normalised"))
        first_inverse, first_normalised = sem("first_inverse"), sem("first_normalised")
        p_turned, at_hi_done, at_lo_done = sem("p_turned"), sem("at_hi_done"), sem("at_lo_done")
        o_ready, o_hi_done, o_lo_done = sem("o_ready"), sem("o_hi_done"), sem("o_lo_done")
        proj_ready, resid_in = sem("proj_ready"), sem("resid_in")
        stored = sem("stored")
        ffn_in, rows_in, ffn_consts, rows_ready = sem("ffn_in"), sem("rows_in"), sem("ffn_consts"), sem("rows_ready")
        resid_ready, var_ready, xf_ready, fr_ready, z_ready = sem("resid_ready"), sem("var_ready"), sem("xf_ready"), sem("fr_ready"), sem("z_ready")
        xf_turned, xft_ready, logits_ready, z_stored = sem("xf_turned"), sem("xft_ready"), sem("logits_ready"), sem("z_stored")
        gap_ready, gates_ready, sel_ready, pos_ready = sem("gap_ready"), sem("gates_ready"), sem("sel_ready"), sem("pos_ready")
        slot_oh_ready, tok_summed, tok_ready, rows_u_ready = sem("slot_oh_ready"), sem("tok_summed"), sem("tok_ready"), sem("rows_u_ready")
        gathered, sel_set = [sem("gathered0"), sem("gathered1")], sem("sel_set")
        xg_turned, xg_scaled, xg_hi_done, xg_lo_done = sem("xg_turned"), sem("xg_scaled"), sem("xg_hi_done"), sem("xg_lo_done")
        x2_clipped, sig_done, h_ready, h_turned, ht_hi_done, ht_lo_done = (
            sem("x2_clipped"), sem("sig_done"), sem("h_ready"), sem("h_turned"), sem("ht_hi_done"), sem("ht_lo_done"))
        y_ready, y_stored = sem("y_ready"), [sem("y_stored0"), sem("y_stored1")]
        y_rows_in = [[sem(f"y_rows_in{j}_{t}") for t in range(NT)] for j in range(2)]
        last_oh, last_oh_turned, last_oh_ready = sem("last_oh"), sem("last_oh_turned"), sem("last_oh_ready")
        slot_gates, y_half, y_hi_done, y_lo_done = sem("slot_gates"), sem("y_half"), sem("y_hi_done"), sem("y_lo_done")
        rows_scaled, tile_added, last_summed, out_ready = sem("rows_scaled"), sem("tile_added"), sem("last_summed"), sem("out_ready")
        most_ready, over_raw, over_cols_in = sem("most_ready"), [sem(f"over_raw{s}") for s in range(3)], sem("over_cols_in")
        over_w_hi, over_w_lo, over_expert, over_z_in = sem("over_w_hi"), sem("over_w_lo"), sem("over_expert"), sem("over_z_in")
        over_sel, over_turned, over_hi, over_lo = sem("over_sel"), sem("over_turned"), sem("over_hi"), sem("over_lo")
        over_up, over_clipped, over_sig, over_h = sem("over_up"), sem("over_clipped"), sem("over_sig"), sem("over_h")
        over_scaled, over_h_turned, over_h_hi, over_h_lo, over_down, over_added = (
            sem("over_scaled"), sem("over_h_turned"), sem("over_h_hi"), sem("over_h_lo"), sem("over_down"), sem("over_added"))
        over_dve = sem("over_dve")

        def f0(e):
            return GNN_CHUNKS + 6 * e - 2

        def up_chunks(e):
            return f0(e) + (2 if e == 0 else 0)

        stat = small[:, 0:36].rearrange("p (t k) -> p t k", t=NT)
        mv = small[:, 36:42].rearrange("p (t k) -> p t k", t=NT)
        rs = small[:, 42:48]
        halfneg = small[:, 48:49]
        negmax = small[:, 52:58].rearrange("p (b i) -> p b i", b=2)
        rsum = small[:, 58:64].rearrange("p (b i) -> p b i", b=2)

        rinv = small[:, 64:70].rearrange("p (b i) -> p b i", b=2)

        SCALE8 = 1.0 / 8.0

        HALVES = [(m, h) for m in range(6) for h in range(2)]
        NAMES = ["v1", "v2", "k1", "k2", "q1", "q2"]

        GATHERS = [(0, 0), (0, 1), (1, 0), (1, 1), (2, 0), (2, 1)]
        YG_SLOT = [0, 2, 4, 1, 3, 5]

        last_rows = raws[RAW[UP_LAST]][:, 0:2 * NT * P].rearrange("p (e t s) -> p e t s", e=2, t=NT)
        last_slots = hi[SLOT[UP_LAST]][:, D:D + 2 * NT * P].rearrange("p (e t s) -> p e t s", e=2, t=NT)
        y_hi = [hi[SLOT[c]][:, 0:D] for c in (UP_LAST, UP_LAST + 1)]
        y_lo = [lo[SLOT[c]][:, 0:D] for c in (UP_LAST, UP_LAST + 1)]
        slot_gate = r3[:, 7, 0:2]
        lg, eq, ranked, oh1, gates, oh2, pos, tmp, posm, over_gate = (r8[:, j, :, :] for j in range(10))
        SUM_BANKS = [(0, 1), (5, 6), (2, 7)]

        def banks(group):
            return B[0:4] if group % 2 == 0 else B[4:8]

        X_HALVES = [(half, t) for half in range(2) for t in range(NT)]

        def x_bank(t, half):
            return B[4 * half + t]

        def f32(ap):
            return ap.bitcast(F32)

        def wait_lo(engine, c):
            engine.wait_ge(pool_lo_done if c in POOL_LO else lo_done, nth(c))

        @contextmanager
        def crowded(engine, at_end=None):
            engine.wait_ge(most_ready, 1)
            tokens = engine.value_load(most[0:1, 0:1])
            with engine.If(tokens > CAP):
                with engine.Fori(0, NE) as e:
                    yield e
                if at_end is not None:
                    engine.wait_ge(*at_end)

        block = ctx.enter_context(nc.Block())

        @block.sync
        def _(sp):
            xv = x.rearrange("(t p) d -> p t d", p=P)
            for t in range(NT):
                sp.dma_start(xin[:, t, :], xv[:, t, :]).then_inc(x_in[t], 16)

            def load(c):
                if raw_before(c) is not None:
                    wait_lo(sp, raw_before(c))
                srcw = wg[c] if c < GNN_CHUNKS else wf[EXPERT_ORDER[c - GNN_CHUNKS][0], EXPERT_ORDER[c - GNN_CHUNKS][1]]
                sp.dma_start(raws[RAW[c]], srcw).then_inc(raw_ready[RAW[c]], 16)

            for c in range(GNN_CHUNKS + 2):
                load(c)
                if c == 3:
                    sp.wait_ge(base_ready, 1)
                    sp.dma_start(mask_rows, mask8[:, :, :]).then_inc(base_stored, 16)
            sp.wait_ge(score_ready, NT * HEADS)
            for t in range(NT):
                sp.dma_start(xres[:, t, :], xv[:, t, :]).then_inc(resid_in, 16)
            for a, b in ((lngb, lng), (lnbb, lnb)):
                sp.dma_start(a, b.partition_broadcast(P)).then_inc(resid_in, 16)
            sp.wait_ge(o_ready, HEADS)
            sp.dma_start(bob, bo.partition_broadcast(P)).then_inc(resid_in, 16)
            sp.wait_ge(rows_in, 1)
            for r in (0, 32):
                for a, cut in ((b1, slice(0, CW)), (b2, slice(CW, 2 * CW)), (be, slice(D, 2 * D))):
                    sp.dma_start(brow_f[r:r + NE, cut], a).then_inc(ffn_in, 16)
            for a, b in ((rws[:, :, :], rw), (egb[:, 0, :, :], egc), (egb[:, 1, :, :], ebc)):
                sp.dma_start(a, b).then_inc(ffn_in, 16)
            for c in (GNN_CHUNKS + 2, GNN_CHUNKS + 3):
                load(c)
            for t in range(NT):
                sp.wait_ge(z_ready, t + 1)
                sp.dma_start(zbuf[t * P:(t + 1) * P, :], xf[:, t, :]).then_inc(z_stored, 16)
                load(GNN_CHUNKS + 4 + t)

            def y_store(e, par):
                sp.wait_ge(y_ready, e + 1)
                sp.dma_start(ybuf[e * CAP:(e + 1) * CAP, :], y[:, par, :]).then_inc(y_stored[par], 16)

            stores = 0
            for c in range(LNB_FREE, CHUNKS):
                if stores < LAST[0] and c == min(f0(stores + 2) + 8, CHUNKS - 1):
                    y_store(stores, stores % 2)
                    stores += 1
                if c == XF_FREE:
                    sp.wait_ge(sel_set, 1)
                load(c)
            with crowded(sp, at_end=(over_added, NE * (NT - 1))) as e:
                sp.wait_ge(over_expert, e + 1)
                sp.wait_ge(over_sel, e + 1)
                for j in range(EXP_CHUNKS):
                    if j >= 3:
                        sp.wait_ge(over_w_lo, e * EXP_CHUNKS + (j - 2))
                    sp.dma_start(raws[j % 3], wf[bass.ds(e, 1), j].rearrange("o p c -> (o p) c")).then_inc(over_raw[j % 3], 16)
                for j, a in enumerate((egc, ebc)):
                    sp.dma_start(over_cols[:, j, :], a[:, bass.ds(e, 1), :].rearrange("p o k -> p (o k)")).then_inc(over_cols_in, 16)
                for t in range(1, NT):
                    if t > 1:
                        sp.wait_ge(over_turned, e * (NT - 1) + (t - 1))
                    sp.dma_start(xg[:, 1, :], zbuf[t * P:(t + 1) * P, :]).then_inc(over_z_in, 16)
            for n in range(2 * NT):
                rows, cut = slice(n % NT * P, (n % NT + 1) * P), slice(n // NT * CW, (n // NT + 1) * CW)
                sp.wait_ge(out_ready, n + 1)
                sp.dma_start(out[rows, cut], xres[:, n % NT, cut]).then_inc(stored, 16)
            sp.wait_ge(stored, 16 * 2 * NT)

        @block.gpsimd
        def _(pool):
            chain = [0]

            def link(ins):
                chain[0] += 1
                ins.then_inc(pool_chain, 1)
                pool.wait_ge(pool_chain, chain[0])

            pool.memset(halfneg, -0.5).then_inc(consts_ready, 1)
            link(pool.memset(ident[:, :], 0.0))
            pool.affine_select(out=ident[:, :], in_=ident[:, :], compare_op=ALU.not_equal, fill=1.0, base=0,
                               pattern=[[-1, P]], channel_multiplier=1).then_inc(consts_ready, 1)
            link(pool.memset(later[:, :], 1.0))
            pool.affine_select(out=later[:, :], in_=later[:, :], compare_op=ALU.is_gt, fill=0.0, base=0,
                               pattern=[[1, WIN * P]], channel_multiplier=-1).then_inc(consts_ready, 1)
            pool.iota(dump[:, :].rearrange("p (g w) -> p g w", w=WIN), pattern=[[0, EG // WIN], [P, WIN]], base=N * N, channel_multiplier=1,
                      allow_small_or_imprecise_dtypes=True).then_inc(consts_ready, 1)
            for t in range(NT):
                pool.wait_ge(stats_ready, t + 1)
                link(pool.tensor_scalar(rs[:, t:t + 1], mv[:, t, 1:2], EPS, None, ALU.add))
                pool.tensor_tensor(rs[:, 3 + t:4 + t], rs[:, t:t + 1], halfneg, ALU.pow).then_inc(rstd_ready, 1)
            link(pool.memset(mask8[:, :, :], NEG))
            for t in range(NT):
                pool.affine_select(out=mask8[:, t, t * P:(t + 1) * P], in_=mask8[:, t, t * P:(t + 1) * P], compare_op=ALU.not_equal,
                                   fill=0.0, base=0, pattern=[[-1, P]], channel_multiplier=1).then_inc(base_filled, 1)
            pool.wait_ge(base_stored, 16)
            for g in range(EG):
                pool.wait_ge(places_ready, g // PIECE + 1)
                if g and g % WIN == 0:
                    pool.wait_ge(scattered, 16 * g)
                pool.indirect_dma_start(out=mbuf[:, :], out_offset=bass.IndirectOffsetOnAxis(ap=bits[:, 1, g:g + 1], axis=0),
                                        in_=colf[:, 5, g:g + 1], in_offset=None).then_inc(scattered, 16)
            pool.wait_ge(scattered, 16 * EG)
            pool.dma_start(mask8[:, :, :], mask_rows).then_inc(mask_in, 16)

            for h in range(HEADS):
                pool.wait_ge(first_inverse, h + 1)
                pool.tensor_scalar(pr[:, h % 2, 0, :], pr[:, h % 2, 0, :], rinv[:, h % 2, 0:1], None,
                                   ALU.mult).then_inc(first_normalised, 1)

            pool.wait_ge(o_ready, HEADS)
            pool.memset(brow_f[:, :], 0.0).then_inc(rows_in, 1)
            link(pool.memset(sels[:, :], 0.0))
            for base in (0, -32):
                link(pool.affine_select(out=sels[:, :], in_=sels[:, :], compare_op=ALU.not_equal, fill=1.0, base=base,
                                        pattern=[[-1, NE]], channel_multiplier=1))
            pool.memset(ones16[:, :], 1.0).then_inc(ffn_consts, 1)
            link(pool.memset(later16[:, :], 1.0))
            pool.affine_select(out=later16[:, :], in_=later16[:, :], compare_op=ALU.is_gt, fill=0.0, base=0,
                               pattern=[[1, P]], channel_multiplier=-1).then_inc(ffn_consts, 1)
            pool.iota(slots16[:, :], pattern=[[1, P]], base=0, channel_multiplier=0,
                      allow_small_or_imprecise_dtypes=True).then_inc(ffn_consts, 1)
            pool.iota(tok16[:, :], pattern=[[P, NT]], base=0, channel_multiplier=1,
                      allow_small_or_imprecise_dtypes=True).then_inc(ffn_consts, 1)
            pool.iota(r8[:, 10, :, :], pattern=[[0, NT], [-1, NE]], base=NE, channel_multiplier=0,
                      allow_small_or_imprecise_dtypes=True).then_inc(ffn_consts, 1)
            pool.iota(r8[:, 11, :, :], pattern=[[0, NT], [CAP, NE]], base=0, channel_multiplier=0,
                      allow_small_or_imprecise_dtypes=True).then_inc(ffn_consts, 1)
            pool.wait_ge(resid_in, 16 * 6)
            for t in range(NT):
                pool.tensor_tensor(xres[:, t, :], xres[:, t, :], bob, ALU.add).then_inc(resid_ready, 1)
            for t in range(NT):
                for n in range(2):
                    pool.wait_ge(var_ready, 2 * t + n + 1)
                    pool.tensor_tensor(fr[:, t, 4 + 2 * n:5 + 2 * n], fr[:, t, n:n + 1], halfneg, ALU.pow).then_inc(fr_ready, 1)

            def split_lo(c):
                pool.wait_ge(hi_done, c + 1)
                pool.tensor_tensor(lo[SLOT[c]][:, :], raws[RAW[c]], f32(hi[SLOT[c]][:, :]), ALU.subtract).then_inc(pool_lo_done, 1)

            def gather_rows(n):
                t, j = GATHERS[n]
                pool.indirect_dma_start(out=yg[:, YG_SLOT[n], :], out_offset=None, in_=ybuf[:, :],
                                        in_offset=bass.IndirectOffsetOnAxis(ap=rows_u[:, j, t:t + 1], axis=0)).then_inc(y_rows_in[j][t], 16)

            def gather_tokens(e, par):
                pool.indirect_dma_start(out=xg[:, par, :], out_offset=None, in_=zbuf[:, :],
                                        in_offset=bass.IndirectOffsetOnAxis(ap=slot_tok[:, e:e + 1], axis=0)).then_inc(gathered[par], 16)

            def select(e, slot):
                pool.tensor_copy(selx[:, slot, :], sels[:, e:e + 1].to_broadcast([48, P])).then_inc(sel_set, 1)

            pool.wait_ge(z_stored, 16 * NT)
            pool.wait_ge(tok_ready, 1)
            gather_tokens(0, 0)
            gather_tokens(1, 1)
            select(0, 0)
            select(1, 1)
            pool.wait_ge(tok_ready, 2)
            select(2, 2)
            for e in range(NE):
                if e < NE - 2:
                    pool.wait_ge(xg_lo_done, 2 * e + 2)
                    gather_tokens(e + 2, e % 2)
                if e == NE - 1:
                    pool.wait_ge(rows_u_ready, 1)
                    pool.wait_ge(y_stored[0], 16 * 3)
                    pool.wait_ge(y_stored[1], 16 * 3)
                    for n in range(3):
                        gather_rows(n)
                for c in range(f0(e) + 3, min(f0(e) + 9, CHUNKS)):
                    if c in POOL_LO:
                        split_lo(c)
                if e == NE - 1:
                    pool.wait_ge(chunk_used, up_chunks(e) + 4)
                    for n in range(3, 6):
                        gather_rows(n)
                    for n in (4, 5):
                        t, j = GATHERS[n]
                        pool.wait_ge(rows_scaled, n - 3)
                        ins = pool.tensor_tensor(xres[:, t, :], xres[:, t, :], yg[:, YG_SLOT[n], :], ALU.add)
                        if n == 4:
                            link(ins)
                    ins.then_inc(tile_added, 1)
                if 1 <= e < NE - 2:
                    pool.wait_ge(chunk_used, f0(e) + 5)
                    select(e + 2, (e + 2) % 3)

        @block.scalar
        def _(act):
            for j, a in enumerate((src, dst, ety)):
                act.dma_start(cols[:, j, :], a).then_inc(edges_in, 16)
            act.dma_start(gbias[:, :, :], bcols).then_inc(bias_in, 16)
            act.dma_start(ewb[:, 0, :], ew.partition_broadcast(P)).then_inc(bias_in, 16)

            def keys(q):
                if q >= 2:
                    act.wait_ge(places_ready, q - 1)
                for a, b in ((src_i, srcb), (dst_i, dstb)):
                    act.dma_start(a[:, q % 2, :], b[q * PIECE * P:(q + 1) * PIECE * P].partition_broadcast(P)).then_inc(keys_in[q % 2], 16)

            def split_hi(c):
                act.wait_ge(raw_ready[RAW[c]], 16 * raw_loads(c))
                if before(c):
                    act.wait_ge(chunk_used, before(c))
                act.activation(hi[SLOT[c]][:, :], raws[RAW[c]], ACT.Copy).then_inc(hi_done, 1)

            chain = [0]

            def link(ins):
                chain[0] += 1
                ins.then_inc(act_chain, 1)
                act.wait_ge(act_chain, chain[0])

            split_hi(0)
            for half, t in X_HALVES:
                act.wait_ge(x_turned, 2 * t + half + 1)
                act.activation(xt_hi[:, CK * half:CK * (half + 1), t * P:(t + 1) * P],
                               x_bank(t, half).rearrange("p (k n) -> p k n", k=CK), ACT.Copy).then_inc(x_hi, 1)
            split_hi(1)

            def evac(i):
                m, h = HALVES[i]
                group = i
                act.wait_ge(chunk_used, 2 * i + 2)
                if NAMES[m] == "v2":
                    for t in range(NT):
                        act.activation(v_hi[:, t, h * CW:(h + 1) * CW], banks(group)[t][:, :], ACT.Copy).then_inc(bank_hi, 1)
                    return
                to = {"v1": t_hi, "k1": t_hi, "q1": t_hi, "k2": k_hi, "q2": q_hi}[NAMES[m]]
                for b in range(4):
                    o = 4 * h + b
                    act.activation(to[:, o, :], banks(group)[b][:, 0:N], ACT.Identity,
                                   bias=gbias[:, m, o:o + 1]).then_inc(bank_hi, 1)

            for i in range(12):
                split_hi(2 * i + 2)
                split_hi(2 * i + 3)
                if i == 0:
                    act.wait_ge(bias_in, 32)
                    link(act.activation(ewb[:, 1, :], ewb[:, 0, :], ACT.Abs))
                    link(act.activation(ewb[:, 1, :], ewb[:, 1, :], ACT.Exp, scale=-1.0))
                    act.activation(ewb[:, 1, :], ewb[:, 1, :], ACT.Ln, bias=1.0).then_inc(types_ready, 1)
                if i < 4:
                    keys(i)
                evac(i)
            def exps(h):
                for i in range(NT):
                    act.wait_ge(score_max, NT * h + i + 1)
                    act.activation(pr[:, h % 2, i, :], pr[:, h % 2, i, :], ACT.Exp, scale=-1.0,
                                   bias=negmax[:, h % 2, i:i + 1], accum_out=rsum[:, h % 2, i:i + 1]).then_inc(exp_done, 1)

            exps(0)
            for h in range(HEADS + 2):
                if h >= 2:
                    o, rows = h - 2, slice(HD * (h % 2), HD * (h % 2) + HD)
                    act.wait_ge(o_ready, o + 1)
                    act.activation(t_hi[rows, o // 2, :], B[6 + h % 2][rows, 0:N], ACT.Identity,
                                   bias=gbias[rows, 1, o // 2:o // 2 + 1]).then_inc(o_hi_done, 1)
                if h == 3:
                    split_hi(OUT_LAST - 1)
                if h < HEADS:
                    for j in range(NT):
                        act.wait_ge(p_turned, NT * h + j + 1)
                        act.activation(at_hi[:, h % 2, j, :], B[3 + j][:, 0:N], ACT.Copy).then_inc(at_hi_done, 1)
                if h + 1 < HEADS:
                    exps(h + 1)
            split_hi(OUT_LAST)
            split_hi(GNN_CHUNKS)
            for t in range(NT):
                if t:
                    act.wait_ge(logits_ready, t)
                for a in range(2):
                    act.wait_ge(xf_turned, 2 * t + a + 1)
                    act.activation(xft[:, 4 * a:4 * a + 4, :].rearrange("p k n -> p (k n)"), B[6 + a], ACT.Copy).then_inc(xft_ready, 1)
                for c in ((29, 30), (31,), (32,))[t]:
                    split_hi(c)
            act.wait_ge(gap_ready, 1)
            act.activation(r3[:, 8, :], r3[:, 7, :], ACT.Sigmoid)
            act.activation(r3[:, 9, :], r3[:, 7, :], ACT.Sigmoid, scale=-1.0).then_inc(gates_ready, 1)

            def scale_tokens(e, par):
                for a in range(2):
                    act.wait_ge(xg_turned, 2 * e + a + 1)
                    for k in range(4 * a, 4 * a + 4):
                        ins = act.activation(xg[:, par, k * P:(k + 1) * P], B[5 + a][:, (k % 4) * P:(k % 4 + 1) * P],
                                             ACT.Identity, scale=egb[:, 0, e, k:k + 1], bias=egb[:, 1, e, k:k + 1])
                    ins.then_inc(xg_scaled, 1)
                    act.wait_ge(xg_scaled, 2 * e + a + 1)
                    act.activation(xg_hi[:, par, 4 * a:4 * a + 4, :].rearrange("p k n -> p (k n)"), xg[:, par, a * CW:(a + 1) * CW],
                                   ACT.Copy).then_inc(xg_hi_done, 1)

            def sigmoid(e):
                act.wait_ge(x2_clipped, e + 1)
                act.activation(sg[:, :], x2c[:, :], ACT.Sigmoid).then_inc(sig_done, 1)

            def turned_hi(e, par):
                act.wait_ge(h_turned, e + 1)
                act.activation(ht_hi[:, par, :, :].rearrange("p k n -> p (k n)"), B[2], ACT.Copy).then_inc(ht_hi_done, 1)

            scale_tokens(0, 0)
            for e in range(NE):
                nxt = [k if FIRST <= k < CHUNKS else None for k in range(f0(e) + 3, f0(e) + 9)]
                if e:
                    turned_hi(e - 1, (e - 1) % 2)
                for k in nxt[0:3]:
                    if k:
                        split_hi(k)
                sigmoid(e)
                if e + 1 < NE:
                    scale_tokens(e + 1, (e + 1) % 2)
                for k in nxt[3:6]:
                    if k:
                        split_hi(k)
            turned_hi(NE - 1, (NE - 1) % 2)
            act.wait_ge(last_oh_turned, 1)
            act.wait_ge(chunk_used, UP_LAST + 1)
            for j in range(2):
                act.activation(last_slots[:, j, :, :].rearrange("p t s -> p (t s)"), B[5 + j][:, 0:NT * P], ACT.Copy).then_inc(last_oh_ready, 1)
            act.wait_ge(slot_gates, 1)
            act.wait_ge(y_ready, NE - 1)
            act.activation(y_hi[0], y[:, 0, :], ACT.Copy, scale=slot_gate[:, 0:1]).then_inc(y_hi_done, 1)
            act.wait_ge(most_ready, 1)
            for n in (4, 5):
                t, j = GATHERS[n]
                act.wait_ge(y_rows_in[j][t], 16)
                act.activation(yg[:, YG_SLOT[n], :], yg[:, YG_SLOT[n], :], ACT.Copy, scale=r3[:, 8 + j, t:t + 1]).then_inc(rows_scaled, 1)
            for half in range(2):
                act.wait_ge(y_half, half + 1)
                act.wait_ge(chunk_used, UP_LAST + 2)
                act.activation(y_hi[1][:, half * CW:(half + 1) * CW], y[:, 1, half * CW:(half + 1) * CW], ACT.Copy,
                               scale=slot_gate[:, 1:2]).then_inc(y_hi_done, 1)
            with crowded(act) as e:
                act.wait_ge(over_expert, e + 1)
                for j in range(EXP_CHUNKS):
                    act.wait_ge(over_raw[j % 3], e * 32 + 16 * (j // 3 + 1))
                    act.activation(hi[j][:, :], raws[j % 3], ACT.Copy).then_inc(over_w_hi, 1)
                act.wait_ge(over_cols_in, e * 32 + 32)
                for t in range(1, NT):
                    step = e * (NT - 1) + t
                    act.wait_ge(over_turned, step)
                    for k in range(KT):
                        ins = act.activation(xg[:, 0, k * P:(k + 1) * P], B[5 + k // 4][:, (k % 4) * P:(k % 4 + 1) * P],
                                             ACT.Identity, scale=over_cols[:, 0, k:k + 1], bias=over_cols[:, 1, k:k + 1])
                    ins.then_inc(over_scaled, 1)
                    act.wait_ge(over_scaled, step)
                    act.activation(xg_hi[:, 0, :, :].rearrange("p k n -> p (k n)"), xg[:, 0, :], ACT.Copy).then_inc(over_hi, 1)
                    act.wait_ge(over_clipped, step)
                    act.activation(sg[:, :], x2c[:, :], ACT.Sigmoid).then_inc(over_sig, 1)
                    act.wait_ge(over_h_turned, step)
                    act.activation(ht_hi[:, 0, :, :].rearrange("p k n -> p (k n)"), B[2], ACT.Copy).then_inc(over_h_hi, 1)

        @block.vector
        def _(dve):
            chain = [0]

            def link(ins):
                chain[0] += 1
                ins.then_inc(dve_chain, 1)
                dve.wait_ge(dve_chain, chain[0])

            def split_lo(c):
                dve.wait_ge(hi_done, c + 1)
                dve.tensor_tensor(lo[SLOT[c]][:, :], raws[RAW[c]], f32(hi[SLOT[c]][:, :]), ALU.subtract).then_inc(lo_done, 1)

            def x_stats(t):
                dve.wait_ge(x_in[t], 16)
                for half in range(2):
                    link(dve.bn_stats(stat[:, t, 6 * half:6 * half + 6], xin[:, t, half * CW:(half + 1) * CW]))
                dve.bn_aggr(mv[:, t, :], stat[:, t, :]).then_inc(stats_ready, 1)

            def x_norm(t):
                dve.wait_ge(rstd_ready, t + 1)
                dve.tensor_scalar(xin[:, t, :], xin[:, t, :], mv[:, t, 0:1], rs[:, 3 + t:4 + t], ALU.subtract, ALU.mult).then_inc(normed, 1)

            def x_rest(n):
                half, t = X_HALVES[n]
                dve.wait_ge(x_hi, n + 1)
                cut = (slice(None), slice(CK * half, CK * (half + 1)), slice(t * P, (t + 1) * P))
                dve.tensor_tensor(xt_lo[cut], x_bank(t, half).rearrange("p (k n) -> p k n", k=CK),
                                  f32(xt_hi[cut]), ALU.subtract).then_inc(x_lo, 1)

            x_stats(0)
            x_stats(1)
            x_norm(0)
            x_stats(2)
            x_norm(1)
            x_norm(2)
            split_lo(0)
            for n in range(2 * NT):
                x_rest(n)
            split_lo(1)

            def evac(i):
                m, h = HALVES[i]
                group = i
                n0 = sum(NT if NAMES[HALVES[j][0]] == "v2" else 4 for j in range(i))
                if NAMES[m] == "v2":
                    for t in range(NT):
                        dve.wait_ge(bank_hi, n0 + t + 1)
                        cut = (slice(None), t, slice(h * CW, (h + 1) * CW))
                        ins = dve.tensor_tensor(v_lo[cut], banks(group)[t][:, :], f32(v_hi[cut]), ALU.subtract)
                    ins.then_inc(group_evacuated, 1)
                    return
                th, tl = {"v1": (t_hi, t_lo), "k1": (t_hi, t_lo), "q1": (t_hi, t_lo), "k2": (k_hi, k_lo),
                          "q2": (q_hi, q_lo)}[NAMES[m]]
                for b in range(4):
                    o = 4 * h + b
                    dve.wait_ge(bank_hi, n0 + b + 1)
                    ins = dve.scalar_tensor_tensor(out=tl[:, o, :], in0=banks(group)[b][:, 0:N], scalar=gbias[:, m, o:o + 1],
                                                   in1=f32(th[:, o, :]), op0=ALU.add, op1=ALU.subtract)
                ins.then_inc(group_evacuated, 1)

            def edge_columns():
                dve.wait_ge(edges_in, 48)
                link(dve.tensor_copy(colf[:, 0:2, :], cols[:, 0:2, :]))
                link(dve.scalar_tensor_tensor(out=colf[:, 2, :], in0=colf[:, 0, :], scalar=float(N), in1=colf[:, 1, :],
                                              op0=ALU.mult, op1=ALU.add))
                dve.wait_ge(consts_ready, 4)
                link(dve.tensor_tensor(colf[:, 4, :], dump[:, :], colf[:, 2, :], ALU.subtract))
                dve.wait_ge(types_ready, 1)
                link(dve.tensor_scalar(ewb[:, 3, :], ewb[:, 0, :], 0.0, None, ALU.max))
                link(dve.tensor_tensor(ewb[:, 3, :], ewb[:, 3, :], ewb[:, 1, :], ALU.add))
                link(dve.tensor_scalar(ewb[:, 2, :], ewb[:, 3, :], 8.0, None, ALU.mult))
                link(dve.tensor_scalar(bits[:, 0, :], cols[:, 2, :], 3, None, ALU.add))
                link(dve.tensor_scalar(bits[:, 0, :], bits[:, 0, :], 3, None, ALU.bitwise_and))
                for w in range(4):
                    ins = dve.tensor_scalar(wterm[:, w, :], bits[:, 0, :], float(w), ewb[:, 2, w:w + 1], ALU.is_equal, ALU.mult)
                link(ins)
                link(dve.tensor_tensor(wterm[:, 0:2, :], wterm[:, 0:2, :], wterm[:, 2:4, :], ALU.add))
                link(dve.tensor_tensor(colf[:, 5, :], wterm[:, 0, :], wterm[:, 1, :], ALU.add))
                dve.wait_ge(base_filled, NT)
                for t in range(NT):
                    block = mask8[:, t, t * P:(t + 1) * P]
                    ins = dve.scalar_tensor_tensor(out=block, in0=ident[:, :], scalar=ewb[:, 2, 3:4], in1=block, op0=ALU.mult, op1=ALU.add)
                ins.then_inc(base_ready, 1)

            def duplicates(q):
                dve.wait_ge(keys_in[q % 2], 32 * (q // 2 + 1))
                if q:
                    dve.wait_ge(places_ready, q)
                link(dve.scalar_tensor_tensor(out=keyb[:, :], in0=src_i[:, q % 2, :], scalar=float(N), in1=dst_i[:, q % 2, :],
                                              op0=ALU.mult, op1=ALU.add))
                for j in range(PIECE):
                    g = q * PIECE + j
                    width = (WIN - g % WIN) * P
                    ins = dve.scalar_tensor_tensor(out=eqt[:, j % 2, 0:width], in0=keyb[:, j * P:j * P + width],
                                                   scalar=colf[:, 2, g:g + 1], in1=later[:, 0:width], op0=ALU.is_equal,
                                                   op1=ALU.mult, accum_out=colf[:, 3, g:g + 1])
                    link(ins)
                part = slice(q * PIECE, (q + 1) * PIECE)
                link(dve.scalar_tensor_tensor(out=colf[:, 3, part], in0=colf[:, 3, part], scalar=0.0, in1=colf[:, 4, part],
                                              op0=ALU.is_gt, op1=ALU.mult))
                dve.tensor_tensor(bits[:, 1, part], colf[:, 2, part], colf[:, 3, part], ALU.add).then_inc(places_ready, 1)

            for i in range(12):
                split_lo(2 * i + 2)
                split_lo(2 * i + 3)
                if i == 0:
                    edge_columns()
                if 1 <= i < 5:
                    duplicates(i - 1)
                evac(i)
            dve.wait_ge(mask_in, 16)
            def maxima(h):
                if h >= 2:
                    dve.wait_ge(p_turned, NT * (h - 1))
                for i in range(NT):
                    dve.wait_ge(score_ready, NT * h + i + 1)
                    dve.tensor_tensor_reduce(out=pr[:, h % 2, i, :], in0=B[i][:, 0:N], in1=mask8[:, i, :],
                                             scale=-SCALE8, scalar=BIG, op0=ALU.add, op1=ALU.min,
                                             accum_out=negmax[:, h % 2, i:i + 1]).then_inc(score_max, 1)

            def normalise(h):
                dve.wait_ge(exp_done, NT * (h + 1))
                link(dve.reciprocal(rinv[:, h % 2, 1:NT], rsum[:, h % 2, 1:NT]))
                for i in range(1, NT):
                    dve.tensor_scalar(pr[:, h % 2, i, :], pr[:, h % 2, i, :], rinv[:, h % 2, i:i + 1], None,
                                      ALU.mult).then_inc(normalised, 1)

            def inverse(h):
                dve.wait_ge(exp_done, NT * h + 1)
                dve.reciprocal(rinv[:, h % 2, 0:1], rsum[:, h % 2, 0:1]).then_inc(first_inverse, 1)

            maxima(0)
            inverse(0)
            normalise(0)
            for h in range(HEADS + 2):
                if h + 1 < HEADS:
                    maxima(h + 1)
                if h >= 2:
                    o, rows = h - 2, slice(HD * (h % 2), HD * (h % 2) + HD)
                    dve.wait_ge(o_hi_done, o + 1)
                    dve.scalar_tensor_tensor(out=t_lo[rows, o // 2, :], in0=B[6 + h % 2][rows, 0:N],
                                             scalar=gbias[rows, 1, o // 2:o // 2 + 1], in1=f32(t_hi[rows, o // 2, :]),
                                             op0=ALU.add, op1=ALU.subtract).then_inc(o_lo_done, 1)
                if h == 3:
                    split_lo(OUT_LAST - 1)
                if h < HEADS:
                    for j in range(NT):
                        if j == NT - 1 and h + 1 < HEADS:
                            inverse(h + 1)
                        dve.wait_ge(at_hi_done, NT * h + j + 1)
                        dve.tensor_tensor(at_lo[:, h % 2, j, :], B[3 + j][:, 0:N], f32(at_hi[:, h % 2, j, :]),
                                          ALU.subtract).then_inc(at_lo_done, 1)
                if h + 1 < HEADS:
                    normalise(h + 1)
            split_lo(OUT_LAST)
            split_lo(GNN_CHUNKS)
            dve.wait_ge(ffn_in, 16 * 9)
            link(dve.tensor_copy(brow[:, :], brow_f[:, :]))
            dve.tensor_tensor(brow[32:48, :], brow_f[32:48, :], f32(brow[32:48, :]), ALU.subtract).then_inc(rows_ready, 1)
            dve.wait_ge(rows_ready, 1)
            dve.wait_ge(resid_ready, NT)

            def both_stats(src, stat, to):
                for h in range(2):
                    ins = dve.bn_stats(stat[:, h, :], src[:, h * CW:(h + 1) * CW])
                link(ins)
                link(dve.bn_aggr(to, stat.rearrange("p a b -> p (a b)")))

            for t in range(NT):
                for h in range(2):
                    cut = slice(h * CW, (h + 1) * CW)
                    dve.wait_ge(proj_ready, 2 * t + h + 1)
                    link(dve.tensor_tensor(xres[:, t, cut], xres[:, t, cut], B[2 * t + h], ALU.add))
                    if h == 0:
                        dve.bn_stats(xstat[:, t, h, :], xres[:, t, cut])
                    else:
                        link(dve.bn_stats(xstat[:, t, h, :], xres[:, t, cut]))
                mean, v, a, b = fmv[:, t, 0:1], fmv[:, t, 1:2], fr[:, t, 2:3], fr[:, t, 0:1]
                link(dve.bn_aggr(fmv[:, t, 0:2], xstat[:, t, :, :].rearrange("p a b -> p (a b)")))
                link(dve.tensor_scalar(a, v, EPS, EPS, ALU.add, ALU.mult))
                dve.tensor_tensor(b, a, v, ALU.add).then_inc(var_ready, 1)
                link(dve.scalar_tensor_tensor(out=xf[:, t, :], in0=xres[:, t, :], scalar=mean, in1=lngb[:, :],
                                              op0=ALU.subtract, op1=ALU.mult))
                dve.wait_ge(fr_ready, 2 * t + 1)
                dve.scalar_tensor_tensor(out=xf[:, t, :], in0=xf[:, t, :], scalar=fr[:, t, 4:5], in1=lnbb[:, :],
                                         op0=ALU.mult, op1=ALU.add).then_inc(xf_ready, 1)
                dve.wait_ge(xf_ready, t + 1)
                both_stats(xf[:, t, :], xstat[:, t, :, :], fmv[:, t, 2:4])
                dve.tensor_scalar(fr[:, t, 1:2], fmv[:, t, 3:4], EPS, None, ALU.add).then_inc(var_ready, 1)
                if t > 0:
                    split_lo(GNN_CHUNKS + t)
                dve.wait_ge(fr_ready, 2 * t + 2)
                dve.wait_ge(xf_turned, 2 * t + 2)
                dve.tensor_scalar(xf[:, t, :], xf[:, t, :], fmv[:, t, 2:3], fr[:, t, 6:7], ALU.subtract, ALU.mult).then_inc(z_ready, 1)

            order, first_row = r8[:, 10, :, :], r8[:, 11, :, :]
            m1, m2, mx = r3[:, 0, :], r3[:, 1, :], r3[:, 2, :]

            def wide(v):
                return v.unsqueeze(2).to_broadcast([P, NT, NE])

            def largest(values, top, onehot):
                link(dve.tensor_reduce(top, values, AX, ALU.max))
                link(dve.tensor_tensor(eq, values, wide(top), ALU.is_equal))
                link(dve.tensor_tensor(ranked, eq, order, ALU.mult))
                link(dve.tensor_reduce(mx, ranked, AX, ALU.max))
                link(dve.tensor_tensor(onehot, ranked, wide(mx), ALU.is_equal))

            dve.wait_ge(ffn_consts, 6)
            dve.wait_ge(logits_ready, NT)
            link(dve.tensor_copy(lg, B[0][:, 0:NT * NE].rearrange("p (t e) -> p t e", t=NT)))
            largest(lg, m1, oh1)
            link(dve.scalar_tensor_tensor(out=gates, in0=oh1, scalar=NEG, in1=lg, op0=ALU.mult, op1=ALU.add))
            largest(gates, m2, oh2)
            dve.tensor_tensor(sel16[:, :, :], oh1, oh2, ALU.add).then_inc(sel_ready, 1)
            dve.tensor_tensor(r3[:, 7, :], m1, m2, ALU.subtract).then_inc(gap_ready, 1)
            dve.wait_ge(sel_ready, 1)
            link(dve.tensor_scalar(tmp, sel16[:, :, :], -1024.0, 1024.0, ALU.mult, ALU.add))
            dve.wait_ge(pos_ready, 1)
            link(dve.tensor_copy(pos, B[3][:, 0:NT * NE].rearrange("p (t e) -> p t e", t=NT)))
            link(dve.tensor_tensor(posm, pos, tmp, ALU.add))
            for e in range(NE):
                for t in range(NT):
                    ins = dve.tensor_scalar(slot_oh[:, e, t, :], slots16[:, :], posm[:, t, e:e + 1], None, ALU.is_equal)
                ins.then_inc(slot_oh_ready, 1)
                if e == 1:
                    dve.wait_ge(tok_summed, 2)
                    dve.tensor_copy(slot_tok[:, 0:2], B[2][:, 0:2]).then_inc(tok_ready, 1)
            early = (slice(None), slice(None), slice(0, LAST[0]))
            for j, oh in enumerate((oh1, oh2)):
                link(dve.tensor_tensor(tmp[early], oh[early], pos[early], ALU.mult))
                link(dve.tensor_reduce(r3[:, 5, :], tmp[early], AX, ALU.add))
                link(dve.tensor_tensor(tmp[early], oh[early], first_row[early], ALU.mult))
                link(dve.tensor_reduce(r3[:, 6, :], tmp[early], AX, ALU.add))
                link(dve.scalar_tensor_tensor(out=r3[:, 3 + j, :], in0=r3[:, 5, :], scalar=float(CAP - 1),
                                              in1=r3[:, 6, :], op0=ALU.min, op1=ALU.add))
            dve.tensor_copy(rows_u[:, :, :], r3[:, 3:5, :]).then_inc(rows_u_ready, 1)
            dve.wait_ge(gates_ready, 1)
            link(dve.tensor_tensor(over_gate, oh1, wide(r3[:, 8, :]), ALU.mult))
            link(dve.tensor_tensor(tmp, oh2, wide(r3[:, 9, :]), ALU.mult))
            link(dve.tensor_tensor(tmp, tmp, over_gate, ALU.add))
            link(dve.scalar_tensor_tensor(out=over_gate, in0=pos, scalar=float(CAP), in1=tmp, op0=ALU.is_ge, op1=ALU.mult))
            link(dve.scalar_tensor_tensor(out=gates, in0=pos, scalar=float(CAP), in1=tmp, op0=ALU.is_lt, op1=ALU.mult))
            for j, oh in enumerate((oh1, oh2)):
                link(dve.tensor_tensor(tmp[early], oh[early], gates[early], ALU.mult))
                link(dve.tensor_reduce(r3[:, 8 + j, :], tmp[early], AX, ALU.add))
            link(dve.tensor_reduce(r3[:, 2, 0:1], B[3][:, NT * NE:(NT + 1) * NE], AX, ALU.max))
            dve.tensor_copy(most[:, :], r3[:, 2, 0:1]).then_inc(most_ready, 1)
            dve.wait_ge(tok_summed, NE)
            dve.tensor_copy(slot_tok[:, 2:NE], B[7][:, 2:NE]).then_inc(tok_ready, 1)

            def tokens_lo(e, par):
                for a in range(2):
                    half = slice(4 * a, 4 * a + 4)
                    dve.wait_ge(xg_hi_done, 2 * e + a + 1)
                    dve.tensor_tensor(xg_lo[:, par, half, :].rearrange("p k n -> p (k n)"), xg[:, par, a * CW:(a + 1) * CW],
                                      f32(xg_hi[:, par, half, :]).rearrange("p k n -> p (k n)"), ALU.subtract).then_inc(xg_lo_done, 1)

            def hidden_lo(e, par):
                dve.wait_ge(ht_hi_done, e + 1)
                dve.tensor_tensor(ht_lo[:, par, :, :].rearrange("p k n -> p (k n)"), B[2],
                                  f32(ht_hi[:, par, :, :]).rearrange("p k n -> p (k n)"), ALU.subtract).then_inc(ht_lo_done, 1)

            def store_y(e, par):
                dve.wait_ge(chunk_used, f0(e + 1) + 6 if e < NE - 1 else CHUNKS)
                if e >= 2:
                    dve.wait_ge(y_stored[par], 16 * (e // 2))
                dve.tensor_scalar(y[:, par, :].rearrange("p (a n) -> p a n", a=2), ps[:, 3:5, :], 10000.0, -10000.0,
                                  ALU.min, ALU.max).then_inc(y_ready, 1)

            tokens_lo(0, 0)
            split_lo(FIRST - 2)
            split_lo(FIRST - 1)
            for e in range(NE):
                nxt = [k if FIRST <= k < CHUNKS and k not in POOL_LO else None for k in range(f0(e) + 3, f0(e) + 9)]
                if e:
                    hidden_lo(e - 1, (e - 1) % 2)
                if e >= 2:
                    store_y(e - 2, e % 2)
                if nxt[0]:
                    split_lo(nxt[0])
                if e == NE - 1:
                    wait_lo(dve, UP_LAST)
                    for j in range(2):
                        for t in range(NT):
                            ins = dve.tensor_scalar(last_rows[:, j, t, :], slots16[:, :], posm[:, t, LAST[j]:LAST[j] + 1], None, ALU.is_equal)
                    ins.then_inc(last_oh, 1)
                if nxt[1]:
                    split_lo(nxt[1])
                dve.wait_ge(chunk_used, up_chunks(e) + 2)
                if e:
                    dve.wait_ge(h_ready, e)
                dve.tensor_scalar(x2c[:, :], B[1], 20.0, -20.0, ALU.min, ALU.max).then_inc(x2_clipped, 1)
                if nxt[2]:
                    split_lo(nxt[2])
                dve.wait_ge(sig_done, e + 1)
                link(dve.tensor_tensor(sg[:, :], x2c[:, :], sg[:, :], ALU.mult))
                if e + 1 < NE:
                    tokens_lo(e + 1, (e + 1) % 2)
                dve.wait_ge(chunk_used, up_chunks(e) + 4)
                if e:
                    dve.wait_ge(h_turned, e)
                link(dve.tensor_tensor(hh[:, :], B[0], sg[:, :], ALU.mult))
                dve.tensor_scalar(hh[:, :], hh[:, :], 10000.0, -10000.0, ALU.min, ALU.max).then_inc(h_ready, 1)
                for k in nxt[3:6]:
                    if k:
                        split_lo(k)

            def add_rows(n):
                t, j = GATHERS[n]
                dve.wait_ge(y_rows_in[j][t], 16)
                link(dve.scalar_tensor_tensor(out=xres[:, t, :], in0=yg[:, YG_SLOT[n], :], scalar=r3[:, 8 + j, t:t + 1],
                                              in1=xres[:, t, :], op0=ALU.mult, op1=ALU.add))

            def y_rest(e, cut):
                dve.scalar_tensor_tensor(out=y_lo[e][:, cut], in0=y[:, e, cut], scalar=slot_gate[:, e:e + 1], in1=f32(y_hi[e][:, cut]),
                                         op0=ALU.mult, op1=ALU.subtract).then_inc(y_lo_done, 1)

            hidden_lo(NE - 1, (NE - 1) % 2)
            store_y(NE - 2, (NE - 2) % 2)
            dve.wait_ge(last_oh_turned, 1)
            dve.tensor_copy(slot_gate, B[7][:, 0:2]).then_inc(slot_gates, 1)
            for n in range(3):
                add_rows(n)
            dve.wait_ge(y_hi_done, 1)
            y_rest(0, slice(0, D))
            add_rows(3)
            dve.wait_ge(chunk_used, CHUNKS)
            halves = [slice(0, CW), slice(CW, D)]
            for half in range(2):
                dve.tensor_scalar(y[:, 1, halves[half]], B[3 + half], 10000.0, -10000.0, ALU.min, ALU.max).then_inc(y_half, 1)
            for half in range(2):
                dve.wait_ge(y_hi_done, 2 + half)
                y_rest(1, halves[half])
            for half in range(2):
                for t in range(NT):
                    dve.wait_ge(last_summed, NT * half + t + 1)
                    if t == NT - 1:
                        dve.wait_ge(tile_added, 1)
                    dve.tensor_tensor(xres[:, t, halves[half]], xres[:, t, halves[half]], B[SUM_BANKS[t][half]],
                                      ALU.add).then_inc(out_ready, 1)
            dve.wait_ge(out_ready, 2 * NT)
            with crowded(dve) as e:
                dve.tensor_copy(fr[:, :, 7:8], over_gate[:, :, bass.ds(e, 1)])
                dve.tensor_copy(selx[:, 0, :], sels[:, bass.ds(e, 1)].to_broadcast([48, P])).then_inc(over_sel, 1)
                dve.wait_ge(over_sel, e + 1)
                for j in range(EXP_CHUNKS):
                    dve.wait_ge(over_w_hi, e * EXP_CHUNKS + (j + 1))
                    dve.tensor_tensor(lo[j][:, :], raws[j % 3], f32(hi[j][:, :]), ALU.subtract).then_inc(over_w_lo, 1)
                for t in range(1, NT):
                    step = e * (NT - 1) + t
                    dve.wait_ge(over_hi, step)
                    dve.tensor_tensor(xg_lo[:, 0, :, :].rearrange("p k n -> p (k n)"), xg[:, 0, :],
                                      f32(xg_hi[:, 0, :, :]).rearrange("p k n -> p (k n)"), ALU.subtract).then_inc(over_lo, 1)
                    dve.wait_ge(over_up, step)
                    dve.tensor_scalar(x2c[:, :], B[1], 20.0, -20.0, ALU.min, ALU.max).then_inc(over_clipped, 1)
                    dve.wait_ge(over_sig, step)
                    dve.tensor_tensor(sg[:, :], x2c[:, :], sg[:, :], ALU.mult).then_inc(over_dve, 1)
                    dve.wait_ge(over_dve, e * (3 * (NT - 1)) + (3 * t - 2))
                    dve.tensor_tensor(hh[:, :], B[0], sg[:, :], ALU.mult).then_inc(over_dve, 1)
                    dve.wait_ge(over_dve, e * (3 * (NT - 1)) + (3 * t - 1))
                    dve.tensor_scalar(hh[:, :], hh[:, :], 10000.0, -10000.0, ALU.min, ALU.max).then_inc(over_h, 1)
                    dve.wait_ge(over_h_hi, step)
                    dve.tensor_tensor(ht_lo[:, 0, :, :].rearrange("p k n -> p (k n)"), B[2],
                                      f32(ht_hi[:, 0, :, :]).rearrange("p k n -> p (k n)"), ALU.subtract).then_inc(over_h_lo, 1)
                    dve.wait_ge(over_down, step)
                    dve.tensor_scalar(y[:, 0, :].rearrange("p (a n) -> p a n", a=2), ps[:, 3:5, :], 10000.0, -10000.0,
                                      ALU.min, ALU.max).then_inc(over_dve, 1)
                    dve.wait_ge(over_dve, e * (3 * (NT - 1)) + 3 * t)
                    dve.scalar_tensor_tensor(out=xres[:, t, :], in0=y[:, 0, :], scalar=fr[:, t, 7:8],
                                             in1=xres[:, t, :], op0=ALU.mult, op1=ALU.add).then_inc(over_added, 1)
                    dve.wait_ge(over_added, step)

        @block.tensor
        def _(pe):
            def three(o, a, b, first, last):
                for n, (s, m) in enumerate(((0, 0), (0, 1), (1, 0))):
                    ins = pe.matmul(o, a[s], b[m], start=first and n == 0, stop=last and n == 2)
                return ins

            def keep_warm(bank, times):
                for _ in range(times):
                    pe.transpose(bank[:, 0:P], ident[:, :], ident[:, :])

            pe.wait_ge(consts_ready, 2)
            for t in range(NT):
                pe.wait_ge(normed, t + 1)
                for k in range(KT):
                    ins = pe.transpose(x_bank(t, k // CK)[:, (k % CK) * P:(k % CK + 1) * P], xin[:, t, k * P:(k + 1) * P], ident[:, :])
                    if k % CK == CK - 1:
                        ins.then_inc(x_turned, 1)

            def weight(c, k, cut=slice(0, CW)):
                w = slice(k * CW + cut.start, k * CW + cut.stop)
                return hi[SLOT[c]][:, w], lo[SLOT[c]][:, w]

            def half(i):
                m, h = HALVES[i]
                group = i
                if group >= 2:
                    pe.wait_ge(group_evacuated, group - 1)
                for part in range(2):
                    c = 2 * i + part
                    wait_lo(pe, c)
                    if i == 0:
                        pe.wait_ge(x_lo, NT * (part + 1))
                    if NAMES[m][1] == "2":
                        pe.wait_ge(group_evacuated, 2 * (m - 1) + part + 1)
                    act_hi, act_lo = (t_hi, t_lo) if NAMES[m][1] == "2" else (xt_hi, xt_lo)
                    for kk in range(CK):
                        k = CK * part + kk
                        if NAMES[m] == "v2":
                            for t in range(NT):
                                tok = slice(t * P, (t + 1) * P)
                                ins = three(banks(group)[t][:, :], (act_hi[:, k, tok], act_lo[:, k, tok]), weight(c, kk),
                                            k == 0, k == KT - 1)
                        else:
                            for b in range(4):
                                ins = three(banks(group)[b][:, 0:N], weight(c, kk, slice(b * P, (b + 1) * P)),
                                            (act_hi[:, k, :], act_lo[:, k, :]), k == 0, k == KT - 1)
                    ins.then_inc(chunk_used, 1)

            def scores(h):
                rows = slice(HD * (h % 2), HD * (h % 2) + HD)
                for i in range(NT):
                    if h > 0:
                        pe.wait_ge(score_max, 3 * (h - 1) + i + 1)
                    tok = slice(i * P, (i + 1) * P)
                    three(B[i][:, 0:N], (q_hi[rows, h // 2, tok], q_lo[rows, h // 2, tok]),
                          (k_hi[rows, h // 2, :], k_lo[rows, h // 2, :]), True, True).then_inc(score_ready, 1)

            def turn(h):
                pe.wait_ge(first_normalised, h + 1)
                pe.wait_ge(normalised, (NT - 1) * (h + 1))
                for j in range(NT):
                    if h > 0:
                        pe.wait_ge(at_lo_done, 3 * (h - 1) + j + 1)
                    for i in range(NT):
                        ins = pe.transpose(B[3 + j][:, i * P:(i + 1) * P], pr[:, h % 2, i, j * P:(j + 1) * P], ident[:, :])
                    ins.then_inc(p_turned, 1)

            def attend(h):
                if h >= 2:
                    pe.wait_ge(o_lo_done, h - 1)
                pair = slice((h // 2) * P, (h // 2 + 1) * P)
                for j in range(NT):
                    pe.wait_ge(at_lo_done, 3 * h + j + 1)
                    ins = three(B[6 + h % 2][:, 0:N], (v_hi[:, j, pair], v_lo[:, j, pair]),
                                (at_hi[:, h % 2, j, :], at_lo[:, h % 2, j, :]), j == 0, j == NT - 1)
                ins.then_inc(o_ready, 1)

            for i in range(12):
                half(i)
            pe.wait_ge(group_evacuated, 11)
            keep_warm(B[0], WARM_UP)
            pe.wait_ge(group_evacuated, 12)
            scores(0)
            scores(1)
            for h in range(HEADS + 1):
                if h < HEADS:
                    turn(h)
                if h >= 1:
                    attend(h - 1)
                if h + 2 < HEADS:
                    scores(h + 2)
            def router(t):
                pe.wait_ge(xf_ready, t + 1)
                for k in range(KT):
                    if t and k % 4 == 0:
                        pe.wait_ge(xft_ready, 2 * (t - 1) + k // 4 + 1)
                    ins = pe.transpose(B[6 + k // 4][:, (k % 4) * P:(k % 4 + 1) * P], xf[:, t, k * P:(k + 1) * P], ident[:, :])
                    if k % 4 == 3:
                        ins.then_inc(xf_turned, 1)
                    if t == NT - 1 and k == 0:
                        ins.then_inc(chunk_used, 1)
                for k in range(KT):
                    pe.wait_ge(xft_ready, 2 * t + k // 4 + 1)
                    ins = pe.matmul(B[0][:, t * NE:(t + 1) * NE], xft[:, k, :], rws[:, k, :], start=k == 0, stop=k == KT - 1)
                ins.then_inc(logits_ready, 1)

            for t in range(NT):
                tok = slice(t * P, (t + 1) * P)
                for h in range(2):
                    for k in range(KT):
                        if t == 0:
                            wait_lo(pe, 24 + 2 * h + k // CK)
                            if h == 0:
                                pe.wait_ge(o_lo_done, 2 * k + 2)
                        elif k == 6 and h == 1:
                            router(t - 1)
                        ins = three(B[2 * t + h], (t_hi[:, k, tok], t_lo[:, k, tok]), weight(24 + 2 * h + k // CK, k % CK),
                                    k == 0, k == KT - 1)
                        if t == NT - 1 and (h, k) in ((0, CK), (1, 0), (1, CK - 1)):
                            ins.then_inc(chunk_used, 1)
                    ins.then_inc(proj_ready, 1)
            router(NT - 1)
            pe.wait_ge(sel_ready, 1)
            pe.wait_ge(ffn_consts, 6)
            for t in range(NT):
                for j in range(t + 1):
                    ins = pe.matmul(B[3][:, t * NE:(t + 1) * NE], ones16[:, :] if j < t else later16[:, :], sel16[:, j, :],
                                    start=j == 0, stop=j == t)
            for j in range(NT):
                ins = pe.matmul(B[3][:, NT * NE:(NT + 1) * NE], ones16[:, :], sel16[:, j, :], start=j == 0, stop=j == NT - 1)
            ins.then_inc(pos_ready, 1)
            for e in range(NE):
                pe.wait_ge(slot_oh_ready, e + 1)
                bank = B[2] if e < 2 else B[7]
                for t in range(NT):
                    ins = pe.matmul(bank[:, e:e + 1], slot_oh[:, e, t, :], tok16[:, t:t + 1], start=t == 0, stop=t == NT - 1)
                ins.then_inc(tok_summed, 1)

            def turn_tokens(e, par):
                pe.wait_ge(gathered[par], 16 * (e // 2 + 1))
                if e:
                    pe.wait_ge(xg_scaled, 2 * e)
                for k in range(KT):
                    ins = pe.transpose(B[5 + k // 4][:, (k % 4) * P:(k % 4 + 1) * P], xg[:, par, k * P:(k + 1) * P], ident[:, :])
                    if k % 4 == 3:
                        ins.then_inc(xg_turned, 1)

            def up(bank, e, par, c, cols):
                pe.matmul(bank, selx[0:40, e % 3, :], brow[0:40, cols], start=True, stop=False)
                for part in range(2):
                    wait_lo(pe, c + part)
                    pe.wait_ge(xg_lo_done, 2 * e + part + 1)
                    for kk in range(CK):
                        k = CK * part + kk
                        ins = three(bank, (xg_hi[:, par, k, :], xg_lo[:, par, k, :]), weight(c + part, kk), False, k == KT - 1)
                    ins.then_inc(chunk_used, 1)

            def down(e, par, c):
                pe.wait_ge(ht_lo_done, e + 1)
                if e:
                    pe.wait_ge(y_ready, e)
                for part in range(2):
                    cols = slice(D + part * CW, D + (part + 1) * CW)
                    pe.matmul(B[3 + part], selx[0:40, e % 3, :], brow[0:40, cols], start=True, stop=False)
                for part in range(2):
                    wait_lo(pe, c + part)
                    for k in range(HT):
                        ins = three(B[3 + part], (ht_hi[:, par, k, :], ht_lo[:, par, k, :]), weight(c + part, k), False, k == HT - 1)
                    ins.then_inc(chunk_used, 1)

            def turn_hidden(e):
                pe.wait_ge(h_ready, e + 1)
                if e:
                    pe.wait_ge(ht_lo_done, e)
                for k in range(HT):
                    ins = pe.transpose(B[2][:, k * P:(k + 1) * P], hh[:, k * P:(k + 1) * P], ident[:, :])
                ins.then_inc(h_turned, 1)

            turn_tokens(0, 0)
            pe.wait_ge(rows_ready, 1)
            for e in range(NE):
                par = e % 2
                c = up_chunks(e)
                pe.wait_ge(sel_set, e + 1)
                if e:
                    pe.wait_ge(x2_clipped, e)
                up(B[1], e, par, c, slice(CW, 2 * CW))
                if e + 1 < NE:
                    turn_tokens(e + 1, 1 - par)
                if e:
                    pe.wait_ge(h_ready, e)
                up(B[0], e, par, c + 2, slice(0, CW))
                if e:
                    down(e - 1, 1 - par, c + 4)
                turn_hidden(e)
            pe.wait_ge(last_oh, 1)
            pe.wait_ge(xg_scaled, 2 * NE)
            for j in range(2):
                for t in range(NT):
                    pe.transpose(B[5 + j][:, t * P:(t + 1) * P], last_rows[:, j, t, :], ident[:, :])
            for j in range(2):
                for t in range(NT):
                    ins = pe.matmul(B[7][:, j:j + 1], last_rows[:, j, t, :], gates[:, t, LAST[j]:LAST[j] + 1], start=t == 0, stop=t == NT - 1)
            ins.then_inc(last_oh_turned, 1)
            down(NE - 1, 1, CHUNKS - 2)

            def add_last(j, halves, first):
                for half in halves:
                    if j == 1:
                        pe.wait_ge(y_lo_done, 2 + half)
                    for t in range(NT):
                        for part in (y_hi, y_lo):
                            ins = pe.matmul(B[SUM_BANKS[t][half]], last_slots[:, j, t, :], part[j][:, half * CW:(half + 1) * CW],
                                            start=first and part is y_hi, stop=not first and part is y_lo)
                        if not first:
                            ins.then_inc(last_summed, 1)

            pe.wait_ge(last_oh_ready, 2)
            pe.wait_ge(slot_gates, 1)
            pe.wait_ge(y_lo_done, 1)
            add_last(0, (0, 1), True)
            add_last(1, (0, 1), False)

            def over_sum(bank, act_hi, act_lo, tiles, chunk0, bias_cols):
                pe.matmul(bank, selx[0:40, 0, :], brow[0:40, bias_cols], start=True, stop=False)
                for k in range(tiles):
                    s, w = chunk0 + k // CK, slice(k % CK * CW, (k % CK + 1) * CW)
                    ins = three(bank, (act_hi[:, 0, k, :], act_lo[:, 0, k, :]), (hi[s][:, w], lo[s][:, w]), False, k == tiles - 1)
                return ins

            pe.wait_ge(out_ready, 2 * NT)
            pe.sem_inc(over_expert, 1)
            with crowded(pe) as e:
                pe.wait_ge(over_sel, e + 1)
                pe.wait_ge(over_w_lo, e * EXP_CHUNKS + EXP_CHUNKS)
                for t in range(1, NT):
                    step = e * (NT - 1) + t
                    if t > 1:
                        pe.wait_ge(over_added, e * (NT - 1) + (t - 1))
                    pe.wait_ge(over_z_in, (e * (NT - 1) + t) * 16)
                    for k in range(KT):
                        ins = pe.transpose(B[5 + k // 4][:, (k % 4) * P:(k % 4 + 1) * P], xg[:, 1, k * P:(k + 1) * P], ident[:, :])
                    ins.then_inc(over_turned, 1)
                    pe.wait_ge(over_lo, step)
                    over_sum(B[1], xg_hi, xg_lo, KT, 0, slice(CW, 2 * CW))
                    over_sum(B[0], xg_hi, xg_lo, KT, 2, slice(0, CW)).then_inc(over_up, 1)
                    pe.wait_ge(over_h, step)
                    for k in range(HT):
                        ins = pe.transpose(B[2][:, k * P:(k + 1) * P], hh[:, k * P:(k + 1) * P], ident[:, :])
                    ins.then_inc(over_h_turned, 1)
                    pe.wait_ge(over_h_lo, step)
                    over_sum(B[3], ht_hi, ht_lo, HT, 4, slice(D, D + CW))
                    over_sum(B[4], ht_hi, ht_lo, HT, 5, slice(D + CW, 2 * D)).then_inc(over_down, 1)
                pe.wait_ge(over_added, e * (NT - 1) + (NT - 1))
                pe.sem_inc(over_expert, 1)


_INS = ["x", "src", "dst", "ety", "srcb", "dstb", "ew", "wg", "bcols", "bo", "lng", "lnb", "rw", "egc", "ebc", "wf", "b1", "b2", "be"]


def layouts(i):
    c = np.ascontiguousarray
    f = {k: np.asarray(v) for k, v in i.items()}
    g = "L0_gnn_"

    def chunks(w):
        n = w.shape[1] // CW
        return w.reshape(-1, CK, P, n, CW).transpose(3, 0, 2, 1, 4).reshape(n, -1, P, CE)

    wg = np.concatenate([chunks(f[g + n].T).reshape(4, P, CE) for n in ("wv", "wiv", "wk", "wik", "wq", "wiq", "wo")])
    u = "L0_ffn_"
    wf = np.stack([np.concatenate([chunks(f[u + "W2"][e]).reshape(2, P, CE), chunks(f[u + "W1"][e]).reshape(2, P, CE),
                                   chunks(f[u + "Wo"][e]).reshape(2, P, CE)]) for e in range(NE)])

    def edge(a):
        return c(a.reshape(EG, P).T)

    return {
        "x": c(f["x"]), "src": edge(f["src"]), "dst": edge(f["dst"]), "ety": edge(f["edge_type_5"]),
        "srcb": c(f["src"]), "dstb": c(f["dst"]), "ew": c(f[g + "edge_type_weights"]), "wg": c(wg),
        "bcols": c(np.stack([f[g + n].reshape(KT, P).T for n in ("bv", "biv", "bk", "bik", "bq", "biq")], 1)),
        "bo": c(f[g + "bo"]), "lng": c(f[u + "ln_g"]), "lnb": c(f[u + "ln_b"]),
        "rw": c(f[u + "router_w"].reshape(KT, P, NE).transpose(1, 0, 2)),
        "egc": c(f[u + "eg"].reshape(NE, KT, P).transpose(2, 0, 1)), "ebc": c(f[u + "eb"].reshape(NE, KT, P).transpose(2, 0, 1)),
        "wf": c(wf), "b1": c(f[u + "b1"]), "b2": c(f[u + "b2"]), "be": c(f[u + "bo"]),
    }


def kernel(**inputs):
    import concourse.bacc as bacc
    from concourse.bass_utils import run_bass_kernel_spmd

    nc = bacc.Bacc("TRN2", target_bir_lowering=False, num_devices=1)
    arrays = layouts(inputs)
    args = [nc.dram_tensor(f"in_{n}", arrays[n].shape, mybir.dt.from_np(arrays[n].dtype), kind="ExternalInput").ap() for n in _INS]
    out = nc.dram_tensor("out_0", (N, D), F32, kind="ExternalOutput").ap()
    gnn_ffn(nc, *args, out)
    r = run_bass_kernel_spmd(nc, [{f"in_{n}": arrays[n] for n in _INS}], core_ids=[0])
    return r.results[0]["out_0"]
```
